# Optimizing a Trainium2 kernel written in Bass

```python
import numpy as np
import jax
import jax.numpy as jnp

def _softmax(x, axis=-1):
    return jax.nn.softmax(x, axis=axis)

def _gelu(x):
    return jax.nn.gelu(x, approximate=True)

def _silu(x):
    return jax.nn.silu(x)

def _sigmoid(x):
    return jax.nn.sigmoid(x)

def _layernorm(x, axis=-1, eps=1e-05):
    m = jnp.mean(x, axis=axis, keepdims=True)
    v = jnp.var(x, axis=axis, keepdims=True)
    return (x - m) / jnp.sqrt(v + eps)

def _scatter_add(tgt, idx, src, axis=0):
    return tgt.at[idx].add(src)

def _segment_sum(src, seg, n):
    return jax.ops.segment_sum(src, seg, n)
kernel_name = 'mk_decoder_preln_d4_seqx_r8_3807d6'

def setup_inputs(seed: int=0):
    np.random.seed(seed)
    _w = jnp.asarray

    def _rec_inputs():
        import jax
        import jax.numpy as jnp
        _rk = jax.random.key(seed)
        x = -0.000125 + 0.9999 * jax.random.normal(jax.random.fold_in(_rk, 1), (16, 128, 128), jnp.float32)
        _lenS = 128 - jax.random.randint(jax.random.fold_in(_rk, 7), (16,), 0, max(1, 128 // 4) + 1, jnp.int32)
        _lenS2 = 128 - jax.random.randint(jax.random.fold_in(_rk, 8), (16,), 0, max(1, 128 // 4) + 1, jnp.int32)
        _ctx_1024P = jax.random.normal(jax.random.fold_in(_rk, 11), (16, 16, 128), jnp.float32)
        _ctx_1024c = jax.random.dirichlet(jax.random.fold_in(_rk, 511), 0.3 * jnp.ones((16,), jnp.float32), (16, 128))
        _ctx_1024t = jnp.einsum('bsk,bkd->bsd', _ctx_1024c, _ctx_1024P)
        _ctx_1024t = _ctx_1024t * jax.lax.rsqrt(jnp.mean(jnp.square(_ctx_1024t)) + 1e-12) * 0.953939
        ctx_1024 = -1.52775e-05 + 0.999936 * (_ctx_1024t + 0.3 * jax.random.normal(jax.random.fold_in(_rk, 611), (16, 128, 128), jnp.float32))
        _validS = jnp.arange(128)[None, :] < _lenS[:, None]
        _validS2 = jnp.arange(128)[None, :] < _lenS2[:, None]
        _causal = jnp.tril(jnp.ones((128, 128), dtype=bool))
        mask_1xSxS2_if1 = jnp.where(jnp.ones((1, 128, 128), dtype=bool), 1, 0).astype(jnp.int32)
        return (x, ctx_1024, mask_1xSxS2_if1)
    x, ctx_1024, mask_1xSxS2_if1 = _rec_inputs()

    def _L0_attn_setup():
        import jax, jax.numpy as jnp
        import numpy as np
        D_MODEL = 128
        NHEAD = 16
        D_HEAD = D_MODEL // NHEAD

        def rope_cos_sin(seq_len, dim, dtype=jnp.float32):
            inv_freq = 1.0 / 10000.0 ** (jnp.arange(0, dim, 2, dtype=jnp.float32) / dim)
            t = jnp.arange(seq_len, dtype=jnp.float32)
            freqs = jnp.outer(t, inv_freq)
            emb = jnp.concatenate([freqs, freqs], -1)
            return (jnp.cos(emb).astype(dtype), jnp.sin(emb).astype(dtype))

        def rotate_half(x):
            x1, x2 = jnp.split(x, 2, axis=-1)
            return jnp.concatenate([-x2, x1], axis=-1)

        def apply_rotary(x, cos, sin):
            return x * cos[None, None] + rotate_half(x) * sin[None, None]
        key = jax.random.key(seed)
        k1, k2, k3 = jax.random.split(key, 3)
        B, T, D = (1, 512, D_MODEL)
        x = jax.random.normal(k1, (B, T, D), dtype=jnp.float32)
        W_qkv = jax.random.normal(k2, (3 * D, D), dtype=jnp.float32) * 0.02
        W_out = jax.random.normal(k3, (D, D), dtype=jnp.float32) * 0.02
        return {'x': x, 'W_qkv': W_qkv, 'W_out': W_out}
    _L0_attn_all = _L0_attn_setup()
    _L0_attn_in = {k: v for k, v in _L0_attn_all.items() if k in ('W_qkv', 'W_out')}
    del _L0_attn_all

    def _L0_xattn_setup():
        import jax, jax.numpy as jnp
        import numpy as np
        DECAY = 0.9
        key = jax.random.key(seed)
        k1, k2, k3 = jax.random.split(key, 3)
        B, S, D = (8, 512, 128)
        q = jax.random.normal(k1, (B, S, D), dtype=jnp.float32)
        k = jax.random.normal(k2, (B, S, D), dtype=jnp.float32)
        v = jax.random.normal(k3, (B, S, D), dtype=jnp.float32)
        return {'q': q, 'k': k, 'v': v}
    _L0_xattn_all = _L0_xattn_setup()
    _L0_xattn_in = {k: v for k, v in _L0_xattn_all.items() if k in ()}
    del _L0_xattn_all

    def _L0_ffn_setup():
        import jax, jax.numpy as jnp
        import numpy as np
        D_MODEL = 128
        EXPANSION = 4
        D_HIDDEN = D_MODEL * EXPANSION
        NUM_STAGES = int(np.log2(D_HIDDEN))

        def butterfly(y, weights, dim):
            lead = y.shape[:-1]
            for stage in range(weights.shape[0]):
                s = 2 ** stage
                nb = dim // (2 * s)
                yr = y.reshape(*lead, nb, 2, s)
                a = yr[..., 0, :]
                b = yr[..., 1, :]
                w = weights[stage].reshape(nb, s, 2, 2)
                na = w[..., 0, 0] * a + w[..., 0, 1] * b
                nb2 = w[..., 1, 0] * a + w[..., 1, 1] * b
                y = jnp.stack([na, nb2], axis=-2).reshape(*lead, dim)
            return y
        key = jax.random.key(seed)
        ks = jax.random.split(key, 6)
        B, S = (4, 256)
        x = jax.random.normal(ks[0], (B, S, D_MODEL), jnp.float32)
        W_exp = jax.random.normal(ks[1], (D_MODEL, D_HIDDEN), jnp.float32) * 0.02
        b_exp = jnp.zeros((D_HIDDEN,), jnp.float32)
        up_weights = jax.random.normal(ks[2], (NUM_STAGES, D_HIDDEN // 2, 2, 2), jnp.float32) * 0.02
        up_bias = jnp.zeros((D_HIDDEN,), jnp.float32)
        down_weights = jax.random.normal(ks[3], (NUM_STAGES, D_HIDDEN // 2, 2, 2), jnp.float32) * 0.02
        W_con = jax.random.normal(ks[4], (D_HIDDEN, D_MODEL), jnp.float32) * 0.02
        b_con = jnp.zeros((D_MODEL,), jnp.float32)
        down_bias = jnp.zeros((D_MODEL,), jnp.float32)
        return dict(x=x, W_exp=W_exp, b_exp=b_exp, up_weights=up_weights, up_bias=up_bias, down_weights=down_weights, W_con=W_con, b_con=b_con, down_bias=down_bias)
    _L0_ffn_all = _L0_ffn_setup()
    _L0_ffn_in = {k: v for k, v in _L0_ffn_all.items() if k in ('W_exp', 'b_exp', 'up_weights', 'up_bias', 'down_weights', 'W_con', 'b_con', 'down_bias')}
    del _L0_ffn_all

    def _L1_attn_setup():
        import jax, jax.numpy as jnp
        import numpy as np
        _A = np.array([[1, 1, 1, 0, 1, 1, 1, 0, 0, 0, 1, 1], [1, 1, 0, 1, 1, 1, 0, 0, 0, 1, 1, 0], [1, 0, 1, 1, 1, 0, 0, 0, 1, 1, 0, 1], [0, 1, 1, 1, 0, 0, 0, 1, 1, 0, 1, 1], [0, 0, 0, 0, 1, 1, 1, 1, 1, 1, 1, 1], [1, 1, 1, 1, 0, 0, 0, 0, 0, 0, 0, 0], [0, 0, 0, 0, 1, 1, 1, 1, 0, 0, 0, 0], [1, 1, 0, 0, 1, 1, 0, 0, 1, 1, 0, 0], [1, 0, 1, 0, 1, 0, 1, 0, 1, 0, 1, 0], [0, 1, 0, 1, 0, 1, 0, 1, 0, 1, 0, 1], [1, 0, 0, 1, 1, 0, 0, 1, 1, 0, 0, 1], [0, 1, 1, 0, 0, 1, 1, 0, 0, 1, 1, 0]], dtype=np.float32)
        _H = jnp.asarray(np.concatenate([_A.T, np.eye(12, dtype=np.float32)], axis=1))

        def _fractal_dimension(x):
            s = x.reshape(-1)
            sn = (s - s.min()) / (s.max() - s.min() + 1e-10)
            counts = []
            for sc in (2, 4, 8, 16, 32):
                blk = sn[:sc * sc]
                counts.append(jnp.maximum(jnp.sum(blk > blk.mean()).astype(jnp.float32), 1.0))
            lx = jnp.log(jnp.array([2.0, 4.0, 8.0, 16.0, 32.0], dtype=jnp.float32))
            ly = jnp.log(jnp.stack(counts))
            n = jnp.float32(5.0)
            num = n * jnp.sum(lx * ly) - jnp.sum(lx) * jnp.sum(ly)
            den = n * jnp.sum(lx * lx) - jnp.sum(lx) ** 2
            return jnp.clip(-num / den, 1.0, 2.0)

        def _wave_filter(D, d):
            k = jnp.fft.fftfreq(d).astype(jnp.float32)
            ka = jnp.abs(k) + 1e-08
            omega = 1.0 + 0.2 * D
            a = 1.0 + 0.5 * D
            b = 0.1 * D
            real = jnp.sin(omega * D + a * ka)
            phase = omega * D - ka + b * ka ** 2
            return real * jnp.exp(1j * phase)

        def _golay_correct(bits):
            syn = (bits @ _H.T > 0.5).astype(jnp.float32)
            w = syn.sum(-1)
            _, idx = jax.lax.top_k(syn, 3)
            take = (jnp.arange(3)[None, :] < jnp.minimum(w, 3.0)[:, None]).astype(jnp.float32)
            pattern = (jax.nn.one_hot(idx, 24, dtype=jnp.float32) * take[..., None]).sum(axis=1)
            do_fix = ((w > 0) & (w <= 3))[:, None]
            return jnp.where(do_fix, jnp.mod(bits + pattern, 2.0), bits)
        key = jax.random.key(seed)
        k1, k2, k3 = jax.random.split(key, 3)
        B, S, E = (8, 256, 128)
        x = jax.random.normal(k1, (B, S, E), dtype=jnp.float32)
        W_el = jax.random.normal(k2, (E, 24), dtype=jnp.float32) * 0.02
        b_el = jnp.zeros((24,), dtype=jnp.float32)
        W_le = jax.random.normal(k3, (24, E), dtype=jnp.float32) * 0.02
        b_le = jnp.zeros((E,), dtype=jnp.float32)
        return {'x': x, 'W_el': W_el, 'b_el': b_el, 'W_le': W_le, 'b_le': b_le}
    _L1_attn_all = _L1_attn_setup()
    _L1_attn_in = {k: v for k, v in _L1_attn_all.items() if k in ('W_el', 'b_el', 'W_le', 'b_le')}
    del _L1_attn_all

    def _L1_xattn_setup():
        import jax, jax.numpy as jnp
        import numpy as np
        H = 16
        key = jax.random.key(seed)
        ks = jax.random.split(key, 11)
        B, L, D = (4, 256, 128)
        inp = {'query': jax.random.normal(ks[0], (B, L, D), jnp.float32), 'key': jax.random.normal(ks[1], (B, L, D), jnp.float32), 'value': jax.random.normal(ks[2], (B, L, D), jnp.float32), 'mask': jnp.ones((1, L, L), jnp.int32), 'Wq': jax.random.normal(ks[3], (D, D), jnp.float32) / np.sqrt(D).astype(np.float32), 'bq': jax.random.normal(ks[4], (D,), jnp.float32) * 0.02, 'Wk': jax.random.normal(ks[5], (D, D), jnp.float32) / np.sqrt(D).astype(np.float32), 'bk': jax.random.normal(ks[6], (D,), jnp.float32) * 0.02, 'Wv': jax.random.normal(ks[7], (D, D), jnp.float32) / np.sqrt(D).astype(np.float32), 'bv': jax.random.normal(ks[8], (D,), jnp.float32) * 0.02, 'Wo': jax.random.normal(ks[9], (D, D), jnp.float32) / np.sqrt(D).astype(np.float32), 'bo': jax.random.normal(ks[10], (D,), jnp.float32) * 0.02}
        return inp
    _L1_xattn_all = _L1_xattn_setup()
    _L1_xattn_in = {k: v for k, v in _L1_xattn_all.items() if k in ('Wq', 'bq', 'Wk', 'bk', 'Wv', 'bv', 'Wo', 'bo')}
    del _L1_xattn_all

    def _L1_ffn_setup():
        import jax, jax.numpy as jnp
        import numpy as np
        IN_DIM = 128
        OUT_DIM = 128
        NUM_EXPERTS = 8
        TOP_K = 2
        key = jax.random.key(seed)
        ks = jax.random.split(key, 5)
        s = 1.0 / np.sqrt(IN_DIM)
        x = jax.random.normal(ks[0], (4, 256, IN_DIM), dtype=jnp.float32)
        Wg = jax.random.uniform(ks[1], (IN_DIM, NUM_EXPERTS), jnp.float32, -s, s)
        bg = jnp.zeros((NUM_EXPERTS,), jnp.float32)
        We = jax.random.uniform(ks[2], (NUM_EXPERTS, OUT_DIM, IN_DIM), jnp.float32, -s, s)
        be = jax.random.uniform(ks[3], (NUM_EXPERTS, OUT_DIM), jnp.float32, -s, s)
        return {'x': x, 'Wg': Wg, 'bg': bg, 'We': We, 'be': be}
    _L1_ffn_all = _L1_ffn_setup()
    _L1_ffn_in = {k: v for k, v in _L1_ffn_all.items() if k in ('Wg', 'bg', 'We', 'be')}
    del _L1_ffn_all

    def _L2_attn_setup():
        import jax, jax.numpy as jnp
        import numpy as np

        def _sin_rpe(Lq, d_model, dtype):
            inv_freq = 1.0 / 10000.0 ** (jnp.arange(0, d_model, 2, dtype=jnp.float32) / d_model)
            pos = jnp.arange(-(Lq - 1), Lq, dtype=jnp.float32)
            ang = pos[:, None] * inv_freq[None, :]
            emb = jnp.zeros((2 * Lq - 1, d_model), dtype=jnp.float32)
            emb = emb.at[:, 0::2].set(jnp.sin(ang)).at[:, 1::2].set(jnp.cos(ang))
            return emb.astype(dtype)

        def _rel_shift(x):
            B, H, Lq, Lr = x.shape
            xp = jnp.concatenate([jnp.zeros((B, H, Lq, 1), x.dtype), x], axis=-1)
            xp = xp.reshape(B, H, Lr + 1, Lq)
            return xp[:, :, 1:].reshape(B, H, Lq, Lr)[..., Lr - Lq:]
        key = jax.random.key(seed)
        ks = jax.random.split(key, 7)
        B, Lq, D, H = (1, 256, 128, 16)
        d_head = D // H
        s = 0.02
        return {'w': jax.random.normal(ks[0], (B, Lq, D), jnp.float32), 'Wq': jax.random.normal(ks[1], (D, D), jnp.float32) * s, 'Wk': jax.random.normal(ks[2], (D, D), jnp.float32) * s, 'Wv': jax.random.normal(ks[3], (D, D), jnp.float32) * s, 'Wr': jax.random.normal(ks[4], (D, D), jnp.float32) * s, 'u_bias': jax.random.normal(ks[5], (H, d_head), jnp.float32) * 0.02, 'v_bias': jax.random.normal(ks[6], (H, d_head), jnp.float32) * 0.02}
    _L2_attn_all = _L2_attn_setup()
    _L2_attn_in = {k: v for k, v in _L2_attn_all.items() if k in ('Wq', 'Wk', 'Wv', 'Wr', 'u_bias', 'v_bias')}
    del _L2_attn_all

    def _L2_xattn_setup():
        import jax, jax.numpy as jnp
        import numpy as np
        BETA = 128
        NUM_HEADS = 16
        NORM = (BETA // NUM_HEADS) ** (-0.5)
        key = jax.random.key(seed)
        ks = jax.random.split(key, 6)
        B, N = (4, 256)
        D_in_q = D_in_k = D_in_v = 128
        D_out_k = D_out_v = 128
        q = jax.random.normal(ks[0], (B, N, D_in_q), dtype=jnp.float32)
        k = jax.random.normal(ks[1], (B, N, D_in_k), dtype=jnp.float32)
        v = jax.random.normal(ks[2], (B, N, D_in_v), dtype=jnp.float32)
        Wq = jax.random.normal(ks[3], (D_out_k, D_in_q), dtype=jnp.float32) * D_in_q ** (-0.5)
        Wk = jax.random.normal(ks[4], (D_out_k, D_in_k), dtype=jnp.float32) * D_in_k ** (-0.5)
        Wv = jax.random.normal(ks[5], (D_out_v, D_in_v), dtype=jnp.float32) * D_in_v ** (-0.5)
        return {'q': q, 'k': k, 'v': v, 'Wq': Wq, 'Wk': Wk, 'Wv': Wv}
    _L2_xattn_all = _L2_xattn_setup()
    _L2_xattn_in = {k: v for k, v in _L2_xattn_all.items() if k in ('Wq', 'Wk', 'Wv')}
    del _L2_xattn_all

    def _L2_ffn_setup():
        import jax, jax.numpy as jnp
        import numpy as np
        NUM_HEADS = 16
        TOP_K = 2
        key = jax.random.key(seed)
        ks = jax.random.split(key, 5)
        B, S, D, E = (4, 256, 128, 8)
        scale = 0.02
        return {'x': jax.random.normal(ks[0], (B, S, D), dtype=jnp.float32), 'W_qkv': jax.random.normal(ks[1], (D, 3 * D), dtype=jnp.float32) * scale, 'b_qkv': jnp.zeros((3 * D,), dtype=jnp.float32), 'W_gate': jax.random.normal(ks[2], (D, E), dtype=jnp.float32) * scale, 'b_gate': jnp.zeros((E,), dtype=jnp.float32), 'W_experts': jax.random.normal(ks[3], (E, D, D), dtype=jnp.float32) * scale, 'b_experts': jnp.zeros((E, D), dtype=jnp.float32)}
    _L2_ffn_all = _L2_ffn_setup()
    _L2_ffn_in = {k: v for k, v in _L2_ffn_all.items() if k in ('W_qkv', 'b_qkv', 'W_gate', 'b_gate', 'W_experts', 'b_experts')}
    del _L2_ffn_all

    def _L3_attn_setup():
        import jax, jax.numpy as jnp
        import numpy as np
        ALPHA = 1.2
        A = 1.0
        BANDWIDTH = 1.0
        D_INTRINSIC = 2
        SPHERE_RADIUS = 1.0
        NUM_HEADS = 16
        HIDDEN = 128
        HEAD_DIM = HIDDEN // NUM_HEADS
        EPS = 1e-07

        def _l2norm(t):
            n = jnp.sqrt(jnp.sum(t * t, axis=-1, keepdims=True))
            return t / jnp.maximum(n, 1e-12)
        key = jax.random.key(seed)
        k1, k2, k3, k4, k5 = jax.random.split(key, 5)
        B, S = (2, 256)
        scale = 0.02
        return {'x': jax.random.normal(k1, (B, S, HIDDEN), dtype=jnp.float32), 'w_qkv': jax.random.normal(k2, (3 * HIDDEN, HIDDEN), dtype=jnp.float32) * scale, 'b_qkv': jnp.zeros((3 * HIDDEN,), dtype=jnp.float32), 'w_out': jax.random.normal(k3, (HIDDEN, HIDDEN), dtype=jnp.float32) * scale, 'b_out': jnp.zeros((HIDDEN,), dtype=jnp.float32)}
    _L3_attn_all = _L3_attn_setup()
    _L3_attn_in = {k: v for k, v in _L3_attn_all.items() if k in ('w_qkv', 'b_qkv', 'w_out', 'b_out')}
    del _L3_attn_all

    def _L3_xattn_setup():
        import jax, jax.numpy as jnp
        import numpy as np
        key = jax.random.key(seed)
        ks = jax.random.split(key, 5)
        B, S, D, U = (4, 256, 128, 128)
        scale = 1.0 / np.sqrt(D)
        return {'query': jax.random.normal(ks[0], (B, S, D), dtype=jnp.float32), 'value': jax.random.normal(ks[1], (B, S, D), dtype=jnp.float32), 'Wq': jax.random.normal(ks[2], (D, U), dtype=jnp.float32) * scale, 'bq': jnp.zeros((U,), dtype=jnp.float32), 'Wk': jax.random.normal(ks[3], (D, U), dtype=jnp.float32) * scale, 'bk': jnp.zeros((U,), dtype=jnp.float32), 'Wv': jax.random.normal(ks[4], (D, U), dtype=jnp.float32) * scale, 'bv': jnp.zeros((U,), dtype=jnp.float32)}
    _L3_xattn_all = _L3_xattn_setup()
    _L3_xattn_in = {k: v for k, v in _L3_xattn_all.items() if k in ('Wq', 'bq', 'Wk', 'bk', 'Wv', 'bv')}
    del _L3_xattn_all

    def _L3_ffn_setup():
        import jax, jax.numpy as jnp
        import numpy as np
        N_EMBD = 128
        NUM_EXPERTS = 8
        TOP_K = 2
        D_FF = 4 * N_EMBD
        B, S = (4, 256)
        key = jax.random.key(seed)
        ks = jax.random.split(key, 7)
        scale = lambda fan_in: 1.0 / np.sqrt(fan_in)
        x = jax.random.normal(ks[0], (B, S, N_EMBD), dtype=jnp.float32)
        W_router = jax.random.normal(ks[1], (N_EMBD, NUM_EXPERTS), dtype=jnp.float32) * scale(N_EMBD)
        b_router = jnp.zeros((NUM_EXPERTS,), dtype=jnp.float32)
        W1 = jax.random.normal(ks[2], (NUM_EXPERTS, N_EMBD, D_FF), dtype=jnp.float32) * scale(N_EMBD)
        b1 = jnp.zeros((NUM_EXPERTS, D_FF), dtype=jnp.float32)
        W2 = jax.random.normal(ks[3], (NUM_EXPERTS, D_FF, N_EMBD), dtype=jnp.float32) * scale(D_FF)
        b2 = jnpp = jnp.zeros((NUM_EXPERTS, N_EMBD), dtype=jnp.float32)
        return {'x': x, 'W_router': W_router, 'b_router': b_router, 'W1': W1, 'b1': b1, 'W2': W2, 'b2': b2}
    _L3_ffn_all = _L3_ffn_setup()
    _L3_ffn_in = {k: v for k, v in _L3_ffn_all.items() if k in ('W_router', 'b_router', 'W1', 'b1', 'W2', 'b2')}
    del _L3_ffn_all
    return {'x': x, 'ctx_1024': ctx_1024, 'mask_1xSxS2_if1': mask_1xSxS2_if1, 'L0_attn_W_qkv': _L0_attn_in['W_qkv'], 'L0_attn_W_out': _L0_attn_in['W_out'], 'L0_ffn_W_exp': _L0_ffn_in['W_exp'], 'L0_ffn_b_exp': _L0_ffn_in['b_exp'], 'L0_ffn_up_weights': _L0_ffn_in['up_weights'], 'L0_ffn_up_bias': _L0_ffn_in['up_bias'], 'L0_ffn_down_weights': _L0_ffn_in['down_weights'], 'L0_ffn_W_con': _L0_ffn_in['W_con'], 'L0_ffn_b_con': _L0_ffn_in['b_con'], 'L0_ffn_down_bias': _L0_ffn_in['down_bias'], 'L1_attn_W_el': _L1_attn_in['W_el'], 'L1_attn_b_el': _L1_attn_in['b_el'], 'L1_attn_W_le': _L1_attn_in['W_le'], 'L1_attn_b_le': _L1_attn_in['b_le'], 'L1_xattn_Wq': _L1_xattn_in['Wq'], 'L1_xattn_bq': _L1_xattn_in['bq'], 'L1_xattn_Wk': _L1_xattn_in['Wk'], 'L1_xattn_bk': _L1_xattn_in['bk'], 'L1_xattn_Wv': _L1_xattn_in['Wv'], 'L1_xattn_bv': _L1_xattn_in['bv'], 'L1_xattn_Wo': _L1_xattn_in['Wo'], 'L1_xattn_bo': _L1_xattn_in['bo'], 'L1_ffn_Wg': _L1_ffn_in['Wg'], 'L1_ffn_bg': _L1_ffn_in['bg'], 'L1_ffn_We': _L1_ffn_in['We'], 'L1_ffn_be': _L1_ffn_in['be'], 'L2_attn_Wq': _L2_attn_in['Wq'], 'L2_attn_Wk': _L2_attn_in['Wk'], 'L2_attn_Wv': _L2_attn_in['Wv'], 'L2_attn_Wr': _L2_attn_in['Wr'], 'L2_attn_u_bias': _L2_attn_in['u_bias'], 'L2_attn_v_bias': _L2_attn_in['v_bias'], 'L2_xattn_Wq': _L2_xattn_in['Wq'], 'L2_xattn_Wk': _L2_xattn_in['Wk'], 'L2_xattn_Wv': _L2_xattn_in['Wv'], 'L2_ffn_W_qkv': _L2_ffn_in['W_qkv'], 'L2_ffn_b_qkv': _L2_ffn_in['b_qkv'], 'L2_ffn_W_gate': _L2_ffn_in['W_gate'], 'L2_ffn_b_gate': _L2_ffn_in['b_gate'], 'L2_ffn_W_experts': _L2_ffn_in['W_experts'], 'L2_ffn_b_experts': _L2_ffn_in['b_experts'], 'L3_attn_w_qkv': _L3_attn_in['w_qkv'], 'L3_attn_b_qkv': _L3_attn_in['b_qkv'], 'L3_attn_w_out': _L3_attn_in['w_out'], 'L3_attn_b_out': _L3_attn_in['b_out'], 'L3_xattn_Wq': _L3_xattn_in['Wq'], 'L3_xattn_bq': _L3_xattn_in['bq'], 'L3_xattn_Wk': _L3_xattn_in['Wk'], 'L3_xattn_bk': _L3_xattn_in['bk'], 'L3_xattn_Wv': _L3_xattn_in['Wv'], 'L3_xattn_bv': _L3_xattn_in['bv'], 'L3_ffn_W_router': _L3_ffn_in['W_router'], 'L3_ffn_b_router': _L3_ffn_in['b_router'], 'L3_ffn_W1': _L3_ffn_in['W1'], 'L3_ffn_b1': _L3_ffn_in['b1'], 'L3_ffn_W2': _L3_ffn_in['W2'], 'L3_ffn_b2': _L3_ffn_in['b2']}

def reference(x, ctx_1024, mask_1xSxS2_if1, L0_attn_W_qkv, L0_attn_W_out, L0_ffn_W_exp, L0_ffn_b_exp, L0_ffn_up_weights, L0_ffn_up_bias, L0_ffn_down_weights, L0_ffn_W_con, L0_ffn_b_con, L0_ffn_down_bias, L1_attn_W_el, L1_attn_b_el, L1_attn_W_le, L1_attn_b_le, L1_xattn_Wq, L1_xattn_bq, L1_xattn_Wk, L1_xattn_bk, L1_xattn_Wv, L1_xattn_bv, L1_xattn_Wo, L1_xattn_bo, L1_ffn_Wg, L1_ffn_bg, L1_ffn_We, L1_ffn_be, L2_attn_Wq, L2_attn_Wk, L2_attn_Wv, L2_attn_Wr, L2_attn_u_bias, L2_attn_v_bias, L2_xattn_Wq, L2_xattn_Wk, L2_xattn_Wv, L2_ffn_W_qkv, L2_ffn_b_qkv, L2_ffn_W_gate, L2_ffn_b_gate, L2_ffn_W_experts, L2_ffn_b_experts, L3_attn_w_qkv, L3_attn_b_qkv, L3_attn_w_out, L3_attn_b_out, L3_xattn_Wq, L3_xattn_bq, L3_xattn_Wk, L3_xattn_bk, L3_xattn_Wv, L3_xattn_bv, L3_ffn_W_router, L3_ffn_b_router, L3_ffn_W1, L3_ffn_b1, L3_ffn_W2, L3_ffn_b2):
    import jax
    import jax.numpy as jnp

    def _L0_attn_ref(x, W_qkv, W_out):
        import jax, jax.numpy as jnp
        import numpy as np
        D_MODEL = 128
        NHEAD = 16
        D_HEAD = D_MODEL // NHEAD

        def rope_cos_sin(seq_len, dim, dtype=jnp.float32):
            inv_freq = 1.0 / 10000.0 ** (jnp.arange(0, dim, 2, dtype=jnp.float32) / dim)
            t = jnp.arange(seq_len, dtype=jnp.float32)
            freqs = jnp.outer(t, inv_freq)
            emb = jnp.concatenate([freqs, freqs], -1)
            return (jnp.cos(emb).astype(dtype), jnp.sin(emb).astype(dtype))

        def rotate_half(x):
            x1, x2 = jnp.split(x, 2, axis=-1)
            return jnp.concatenate([-x2, x1], axis=-1)

        def apply_rotary(x, cos, sin):
            return x * cos[None, None] + rotate_half(x) * sin[None, None]
        B, T, D = x.shape
        H, dh = (NHEAD, D_HEAD)
        qkv = jnp.einsum('btd,ed->bte', x, W_qkv)
        q, k, v = jnp.split(qkv, 3, axis=-1)

        def split_heads(t):
            return t.reshape(B, T, H, dh).transpose(0, 2, 1, 3)
        q, k, v = (split_heads(q), split_heads(k), split_heads(v))
        cos, sin = rope_cos_sin(T, dh)
        q = apply_rotary(q, cos, sin)
        k = apply_rotary(k, cos, sin)
        scale = jnp.sqrt(jnp.float32(dh))
        scores = jnp.einsum('bhqd,bhkd->bhqk', q, k) / scale
        causal = jnp.tril(jnp.ones((T, T), dtype=bool))
        scores = jnp.where(causal[None, None], scores, -jnp.inf)
        attn = jax.nn.softmax(scores, axis=-1)
        out = jnp.einsum('bhqk,bhkd->bhqd', attn, v)
        out = out.transpose(0, 2, 1, 3).reshape(B, T, D)
        out = jnp.einsum('btd,ed->bte', out, W_out)
        return out

    def _L0_xattn_ref(q, k, v):
        import jax, jax.numpy as jnp
        import numpy as np
        DECAY = 0.9
        kv = jnp.swapaxes(k * v, 0, 1)

        def step(r, kv_t):
            r = DECAY * r + kv_t
            return (r, r)
        r0 = jnp.zeros(q.shape[:1] + q.shape[2:], dtype=q.dtype)
        _, rs = jax.lax.scan(step, r0, kv)
        return q * jnp.swapaxes(rs, 0, 1)

    def _L0_ffn_ref(x, W_exp, b_exp, up_weights, up_bias, down_weights, W_con, b_con, down_bias):
        import jax, jax.numpy as jnp
        import numpy as np
        D_MODEL = 128
        EXPANSION = 4
        D_HIDDEN = D_MODEL * EXPANSION
        NUM_STAGES = int(np.log2(D_HIDDEN))

        def butterfly(y, weights, dim):
            lead = y.shape[:-1]
            for stage in range(weights.shape[0]):
                s = 2 ** stage
                nb = dim // (2 * s)
                yr = y.reshape(*lead, nb, 2, s)
                a = yr[..., 0, :]
                b = yr[..., 1, :]
                w = weights[stage].reshape(nb, s, 2, 2)
                na = w[..., 0, 0] * a + w[..., 0, 1] * b
                nb2 = w[..., 1, 0] * a + w[..., 1, 1] * b
                y = jnp.stack([na, nb2], axis=-2).reshape(*lead, dim)
            return y
        h = jnp.einsum('bsd,dh->bsh', x, W_exp) + b_exp
        h = butterfly(h, up_weights, D_HIDDEN)
        h = jax.nn.gelu(h + up_bias, approximate=False)
        h = butterfly(h, down_weights, D_HIDDEN)
        y = jnp.einsum('bsh,hd->bsd', h, W_con) + b_con
        return y + down_bias

    def _L1_attn_ref(x, W_el, b_el, W_le, b_le):
        import jax, jax.numpy as jnp
        import numpy as np
        _A = np.array([[1, 1, 1, 0, 1, 1, 1, 0, 0, 0, 1, 1], [1, 1, 0, 1, 1, 1, 0, 0, 0, 1, 1, 0], [1, 0, 1, 1, 1, 0, 0, 0, 1, 1, 0, 1], [0, 1, 1, 1, 0, 0, 0, 1, 1, 0, 1, 1], [0, 0, 0, 0, 1, 1, 1, 1, 1, 1, 1, 1], [1, 1, 1, 1, 0, 0, 0, 0, 0, 0, 0, 0], [0, 0, 0, 0, 1, 1, 1, 1, 0, 0, 0, 0], [1, 1, 0, 0, 1, 1, 0, 0, 1, 1, 0, 0], [1, 0, 1, 0, 1, 0, 1, 0, 1, 0, 1, 0], [0, 1, 0, 1, 0, 1, 0, 1, 0, 1, 0, 1], [1, 0, 0, 1, 1, 0, 0, 1, 1, 0, 0, 1], [0, 1, 1, 0, 0, 1, 1, 0, 0, 1, 1, 0]], dtype=np.float32)
        _H = jnp.asarray(np.concatenate([_A.T, np.eye(12, dtype=np.float32)], axis=1))

        def _fractal_dimension(x):
            s = x.reshape(-1)
            sn = (s - s.min()) / (s.max() - s.min() + 1e-10)
            counts = []
            for sc in (2, 4, 8, 16, 32):
                blk = sn[:sc * sc]
                counts.append(jnp.maximum(jnp.sum(blk > blk.mean()).astype(jnp.float32), 1.0))
            lx = jnp.log(jnp.array([2.0, 4.0, 8.0, 16.0, 32.0], dtype=jnp.float32))
            ly = jnp.log(jnp.stack(counts))
            n = jnp.float32(5.0)
            num = n * jnp.sum(lx * ly) - jnp.sum(lx) * jnp.sum(ly)
            den = n * jnp.sum(lx * lx) - jnp.sum(lx) ** 2
            return jnp.clip(-num / den, 1.0, 2.0)

        def _wave_filter(D, d):
            k = jnp.fft.fftfreq(d).astype(jnp.float32)
            ka = jnp.abs(k) + 1e-08
            omega = 1.0 + 0.2 * D
            a = 1.0 + 0.5 * D
            b = 0.1 * D
            real = jnp.sin(omega * D + a * ka)
            phase = omega * D - ka + b * ka ** 2
            return real * jnp.exp(1j * phase)

        def _golay_correct(bits):
            syn = (bits @ _H.T > 0.5).astype(jnp.float32)
            w = syn.sum(-1)
            _, idx = jax.lax.top_k(syn, 3)
            take = (jnp.arange(3)[None, :] < jnp.minimum(w, 3.0)[:, None]).astype(jnp.float32)
            pattern = (jax.nn.one_hot(idx, 24, dtype=jnp.float32) * take[..., None]).sum(axis=1)
            do_fix = ((w > 0) & (w <= 3))[:, None]
            return jnp.where(do_fix, jnp.mod(bits + pattern, 2.0), bits)
        B, S, E = x.shape
        D = _fractal_dimension(x)
        filt = _wave_filter(D, E)
        x1 = jnp.fft.ifft(jnp.fft.fft(x, axis=-1) * filt, axis=-1).real.astype(x.dtype)
        lat = x1 @ W_el + b_el
        bits = (jax.nn.sigmoid(lat) > 0.5).astype(jnp.float32).reshape(B * S, 24)
        corrected = _golay_correct(bits).reshape(B, S, 24)
        return x1 + corrected @ W_le + b_le

    def _L1_xattn_ref(query, key, value, mask, Wq, bq, Wk, bk, Wv, bv, Wo, bo):
        import jax, jax.numpy as jnp
        import numpy as np
        H = 16
        B, L, D = query.shape
        dk = D // H
        scale = float(dk) ** (-0.5)

        def proj(x, W, b):
            return (x @ W.T + b).reshape(B, -1, H, dk).transpose(0, 2, 1, 3)
        q = proj(query, Wq, bq)
        k = proj(key, Wk, bk)
        v = proj(value, Wv, bv)
        scores = jnp.einsum('bhqd,bhkd->bhqk', q, k) * scale
        scores = jnp.where(mask[:, None, :, :] == 0, jnp.float32(-1000000000.0), scores)
        p_attn = jax.nn.softmax(scores, axis=-1)
        x = jnp.einsum('bhqk,bhkd->bhqd', p_attn, v)
        x = x.transpose(0, 2, 1, 3).reshape(B, -1, D)
        return x @ Wo.T + bo

    def _L1_ffn_ref(x, Wg, bg, We, be):
        import jax, jax.numpy as jnp
        import numpy as np
        IN_DIM = 128
        OUT_DIM = 128
        NUM_EXPERTS = 8
        TOP_K = 2
        gate = jax.nn.softmax(x @ Wg + bg, axis=-1)
        topk_vals, topk_idx = jax.lax.top_k(gate, TOP_K)
        onehot = jax.nn.one_hot(topk_idx, NUM_EXPERTS, dtype=gate.dtype)
        gate_sparse = jnp.einsum('bsk,bske->bse', topk_vals, onehot)
        gate_sparse = gate_sparse / jnp.sum(gate_sparse, axis=-1, keepdims=True)
        y = jnp.einsum('bsi,eoi->bseo', x, We) + be[None, None, :, :].transpose(0, 1, 2, 3)
        out = jnp.einsum('bseo,bse->bso', y, gate_sparse)
        return out

    def _L2_attn_ref(w, Wq, Wk, Wv, Wr, u_bias, v_bias):
        import jax, jax.numpy as jnp
        import numpy as np

        def _sin_rpe(Lq, d_model, dtype):
            inv_freq = 1.0 / 10000.0 ** (jnp.arange(0, d_model, 2, dtype=jnp.float32) / d_model)
            pos = jnp.arange(-(Lq - 1), Lq, dtype=jnp.float32)
            ang = pos[:, None] * inv_freq[None, :]
            emb = jnp.zeros((2 * Lq - 1, d_model), dtype=jnp.float32)
            emb = emb.at[:, 0::2].set(jnp.sin(ang)).at[:, 1::2].set(jnp.cos(ang))
            return emb.astype(dtype)

        def _rel_shift(x):
            B, H, Lq, Lr = x.shape
            xp = jnp.concatenate([jnp.zeros((B, H, Lq, 1), x.dtype), x], axis=-1)
            xp = xp.reshape(B, H, Lr + 1, Lq)
            return xp[:, :, 1:].reshape(B, H, Lq, Lr)[..., Lr - Lq:]
        B, Lq, D = w.shape
        H, d_head = u_bias.shape
        scale = 1.0 / np.sqrt(d_head).astype(np.float32)
        r = _sin_rpe(Lq, D, w.dtype)
        q = (w @ Wq.T).reshape(B, Lq, H, d_head).transpose(0, 2, 1, 3)
        k = (w @ Wk.T).reshape(B, Lq, H, d_head).transpose(0, 2, 1, 3)
        v = (w @ Wv.T).reshape(B, Lq, H, d_head).transpose(0, 2, 1, 3)
        rp = (r @ Wr.T).reshape(2 * Lq - 1, H, d_head).transpose(1, 0, 2)
        AC = jnp.einsum('bhid,bhjd->bhij', q + u_bias[None, :, None, :], k)
        BD = jnp.einsum('bhid,hjd->bhij', q + v_bias[None, :, None, :], rp)
        BD = _rel_shift(BD)
        attn = jax.nn.softmax((AC + BD) * scale, axis=-1)
        out = jnp.einsum('bhij,bhjd->bhid', attn, v)
        return out.transpose(0, 2, 1, 3).reshape(B, Lq, D)

    def _L2_xattn_ref(q, k, v, Wq, Wk, Wv):
        import jax, jax.numpy as jnp
        import numpy as np
        BETA = 128
        NUM_HEADS = 16
        NORM = (BETA // NUM_HEADS) ** (-0.5)
        qp = jax.nn.relu(jnp.einsum('bnd,od->bno', q, Wq))
        kp = jax.nn.relu(jnp.einsum('bnd,od->bno', k, Wk))
        vp = jax.nn.relu(jnp.einsum('bnd,od->bno', v, Wv))
        B, N, D = qp.shape
        dh = D // NUM_HEADS
        qh = qp.reshape(B, N, NUM_HEADS, dh)
        kh = kp.reshape(B, N, NUM_HEADS, dh)
        vh = vp.reshape(B, N, NUM_HEADS, vp.shape[-1] // NUM_HEADS)
        E = NORM * jnp.einsum('bqhd,bkhd->bhqk', qh, kh)
        A = jax.nn.softmax(E, axis=-1)
        out = jnp.einsum('bhqk,bkhd->bqhd', A, vh)
        return out.reshape(B, N, -1)

    def _L2_ffn_ref(x, W_qkv, b_qkv, W_gate, b_gate, W_experts, b_experts):
        import jax, jax.numpy as jnp
        import numpy as np
        NUM_HEADS = 16
        TOP_K = 2
        B, S, D = x.shape
        H = NUM_HEADS
        hd = D // H
        E = W_gate.shape[-1]
        qkv = (x @ W_qkv + b_qkv).reshape(B, S, 3, H, hd)
        q, k, v = (qkv[:, :, 0], qkv[:, :, 1], qkv[:, :, 2])
        attn = jnp.einsum('bqhd,bkhd->bhqk', q, k) / jnp.sqrt(jnp.asarray(hd, x.dtype))
        attn = jax.nn.softmax(attn, axis=-1)
        attn_out = jnp.einsum('bhqk,bkhd->bqhd', attn, v).reshape(B, S, D)
        gate = jax.nn.softmax(x @ W_gate + b_gate, axis=-1)
        top_g, top_i = jax.lax.top_k(gate, TOP_K)
        combine = jnp.sum(jax.nn.one_hot(top_i, E, dtype=x.dtype) * top_g[..., None], axis=2)
        expert_out = jnp.einsum('bsd,edf->bsef', x, W_experts) + b_experts
        moe_out = jnp.einsum('bsef,bse->bsf', expert_out, combine)
        return attn_out + moe_out

    def _L3_attn_ref(x, w_qkv, b_qkv, w_out, b_out):
        import jax, jax.numpy as jnp
        import numpy as np
        ALPHA = 1.2
        A = 1.0
        BANDWIDTH = 1.0
        D_INTRINSIC = 2
        SPHERE_RADIUS = 1.0
        NUM_HEADS = 16
        HIDDEN = 128
        HEAD_DIM = HIDDEN // NUM_HEADS
        EPS = 1e-07

        def _l2norm(t):
            n = jnp.sqrt(jnp.sum(t * t, axis=-1, keepdims=True))
            return t / jnp.maximum(n, 1e-12)
        B, S, H = x.shape
        qkv = x @ w_qkv.T + b_qkv
        q, k, v = jnp.split(qkv, 3, axis=-1)
        to_heads = lambda t: t.reshape(B, S, NUM_HEADS, HEAD_DIM).transpose(0, 2, 1, 3)
        q = _l2norm(to_heads(q))
        k = _l2norm(to_heads(k))
        v = to_heads(v)
        cos = jnp.einsum('bhsd,bhtd->bhst', q, k)
        g_dist = jnp.arccos(jnp.clip(cos, -1.0 + EPS, 1.0 - EPS)) * SPHERE_RADIUS
        attn_score = (1.0 + g_dist / BANDWIDTH ** 0.5) ** (-D_INTRINSIC - ALPHA)
        n_r = jnp.sum(attn_score, axis=-1)
        n_c = jnp.sum(attn_score, axis=-2)
        k_tilde = (n_r ** (-A))[..., :, None] * attn_score * (n_c ** (-A))[..., None, :]
        probs = k_tilde / jnp.maximum(jnp.sum(k_tilde, axis=-1, keepdims=True), 1e-12)
        out = jnp.einsum('bhst,bhtd->bhsd', probs, v)
        out = out.transpose(0, 2, 1, 3).reshape(B, S, H)
        return out @ w_out.T + b_out

    def _L3_xattn_ref(query, value, Wq, bq, Wk, bk, Wv, bv):
        import jax, jax.numpy as jnp
        import numpy as np
        Q = jnp.einsum('bsd,du->bsu', query, Wq) + bq
        K = jnp.einsum('btd,du->btu', value, Wk) + bk
        V = jnp.einsum('btd,du->btu', value, Wv) + bv
        d_k = jnp.asarray(K.shape[-1], dtype=jnp.float32)
        scores = jnp.einsum('bsu,btu->bst', Q, K) / jnp.sqrt(d_k)
        weights = jax.nn.softmax(scores, axis=-1)
        return jnp.einsum('bst,btu->bsu', weights, V)

    def _L3_ffn_ref(x, W_router, b_router, W1, b1, W2, b2):
        import jax, jax.numpy as jnp
        import numpy as np
        N_EMBD = 128
        NUM_EXPERTS = 8
        TOP_K = 2
        D_FF = 4 * N_EMBD
        B, S = (4, 256)
        Bv, Sv, D = x.shape
        flat_x = x.reshape(-1, D)
        T = flat_x.shape[0]
        logits = flat_x @ W_router + b_router
        top_vals, top_idx = jax.lax.top_k(logits, TOP_K)
        neg_inf = jnp.full_like(logits, -jnp.inf)
        sparse_logits = neg_inf.at[jnp.arange(T)[:, None], top_idx].set(top_vals)
        router_weights = jax.nn.softmax(sparse_logits, axis=-1)
        final_output = jnp.zeros_like(flat_x)
        for e in range(NUM_EXPERTS):
            expert_mask = jnp.any(top_idx == e, axis=-1)
            h = jax.nn.relu(flat_x @ W1[e] + b1[e])
            y = h @ W2[e] + b2[e]
            w = router_weights[:, e] * expert_mask.astype(x.dtype)
            final_output = final_output + y * w[:, None]
        return final_output.reshape(Bv, Sv, D)
    x = x + _L0_attn_ref(_layernorm(x, axis=-1), L0_attn_W_qkv, L0_attn_W_out)
    x = x + _L0_xattn_ref(_layernorm(x, axis=-1), ctx_1024, ctx_1024)
    x = x + _L0_ffn_ref(_layernorm(x, axis=-1), L0_ffn_W_exp, L0_ffn_b_exp, L0_ffn_up_weights, L0_ffn_up_bias, L0_ffn_down_weights, L0_ffn_W_con, L0_ffn_b_con, L0_ffn_down_bias)
    x = x + _L1_attn_ref(_layernorm(x, axis=-1), L1_attn_W_el, L1_attn_b_el, L1_attn_W_le, L1_attn_b_le)
    x = x + _L1_xattn_ref(_layernorm(x, axis=-1), ctx_1024, ctx_1024, mask_1xSxS2_if1, L1_xattn_Wq, L1_xattn_bq, L1_xattn_Wk, L1_xattn_bk, L1_xattn_Wv, L1_xattn_bv, L1_xattn_Wo, L1_xattn_bo)
    x = x + _L1_ffn_ref(_layernorm(x, axis=-1), L1_ffn_Wg, L1_ffn_bg, L1_ffn_We, L1_ffn_be)
    x = x + _L2_attn_ref(_layernorm(x, axis=-1), L2_attn_Wq, L2_attn_Wk, L2_attn_Wv, L2_attn_Wr, L2_attn_u_bias, L2_attn_v_bias)
    x = x + _L2_xattn_ref(_layernorm(x, axis=-1), ctx_1024, ctx_1024, L2_xattn_Wq, L2_xattn_Wk, L2_xattn_Wv)
    x = x + _L2_ffn_ref(_layernorm(x, axis=-1), L2_ffn_W_qkv, L2_ffn_b_qkv, L2_ffn_W_gate, L2_ffn_b_gate, L2_ffn_W_experts, L2_ffn_b_experts)
    x = x + _L3_attn_ref(_layernorm(x, axis=-1), L3_attn_w_qkv, L3_attn_b_qkv, L3_attn_w_out, L3_attn_b_out)
    x = x + _L3_xattn_ref(_layernorm(x, axis=-1), ctx_1024, L3_xattn_Wq, L3_xattn_bq, L3_xattn_Wk, L3_xattn_bk, L3_xattn_Wv, L3_xattn_bv)
    x = x + _L3_ffn_ref(_layernorm(x, axis=-1), L3_ffn_W_router, L3_ffn_b_router, L3_ffn_W1, L3_ffn_b1, L3_ffn_W2, L3_ffn_b2)
    return x

_drawn_inputs = setup_inputs


def setup_inputs(seed=0):
    import zlib

    import numpy as np

    out = dict(_drawn_inputs(seed))
    spreads = {'L0_ffn_b_exp': (0.0, 0.1),
     'L0_ffn_up_bias': (0.0, 0.1),
     'L0_ffn_b_con': (0.0, 0.8),
     'L0_ffn_down_bias': (0.0, 0.764),
     'L1_attn_b_el': (0.0, 0.8),
     'L1_attn_b_le': (0.0, 0.8),
     'L1_ffn_bg': (0.0, 0.598),
     'L2_ffn_b_qkv': (0.0, 0.8),
     'L2_ffn_b_gate': (0.0, 0.8),
     'L2_ffn_b_experts': (0.0, 0.8),
     'L3_attn_b_qkv': (0.0, 0.8),
     'L3_attn_b_out': (0.0, 0.8),
     'L3_xattn_bq': (0.0, 0.8),
     'L3_xattn_bk': (0.0, 2.0),
     'L3_xattn_bv': (0.0, 0.8),
     'L3_ffn_b_router': (0.0, 0.8),
     'L3_ffn_b1': (0.0, 0.8),
     'L3_ffn_b2': (0.0, 0.8)}
    factors = {'L0_attn_W_qkv': 6.693,
     'L0_attn_W_out': 6.506,
     'L1_attn_W_el': 8.0,
     'L1_attn_W_le': 8.0,
     'L1_xattn_Wq': 3.07,
     'L1_xattn_bq': 40.957,
     'L1_xattn_Wk': 3.042,
     'L1_xattn_bk': 64.0,
     'L1_xattn_bv': 26.139,
     'L1_xattn_bo': 25.808,
     'L1_ffn_be': 8.0,
     'L2_attn_Wq': 8.0,
     'L2_attn_Wk': 8.0,
     'L2_attn_Wv': 8.0,
     'L2_attn_Wr': 8.0,
     'L2_attn_u_bias': 30.272,
     'L2_attn_v_bias': 62.576,
     'L2_xattn_Wq': 8.0,
     'L2_xattn_Wk': 8.0,
     'L2_ffn_W_qkv': 8.0,
     'L2_ffn_W_gate': 8.0,
     'L2_ffn_W_experts': 8.0,
     'L3_attn_w_qkv': 8.0,
     'L3_attn_w_out': 8.0,
     'L3_xattn_Wq': 3.118,
     'L3_xattn_Wk': 3.114}
    for name, (base, spread) in spreads.items():
        noise = np.random.default_rng([zlib.crc32(name.encode()), seed]).standard_normal(out[name].shape)
        drawn = base * np.exp(spread * noise) if base else spread * noise
        out[name] = jnp.asarray(drawn.astype(out[name].dtype))
    for name, factor in factors.items():
        out[name] = (out[name] * factor).astype(out[name].dtype)
    return out
```

```python
from contextlib import ExitStack

import numpy as np

import concourse.bass as bass
from concourse import mybir

F32 = mybir.dt.float32
BF16 = mybir.dt.bfloat16
I32 = mybir.dt.int32
U32 = mybir.dt.uint32
ALU = mybir.AluOpType
ACT = mybir.ActivationFunctionType
AX = mybir.AxisListType.X

BATCH, SEQ, DIM = 16, 128, 128
HEADS = 16
HDIM = DIM // HEADS
LANES = 2
HALF = HEADS // 2 * SEQ
QUARTER = HALF // 2
VPAD = 32
HIDDEN0 = 512
STAGES0 = 9
EXPERTS = 8
FF3 = 512
CODE, DATA = 24, 12
EPS_LN = 1e-5
MASKED = -float(2 ** 100)
CLIP = 1.0 - 1e-7
SCALES = (2, 4, 8, 16, 32)
LN_SHIFT = 2.0 ** 30
LANE_RANGE = range(LANES)
EXP_LN, TANH_ARCTAN = "natural_log_exp_and_others", "sigmoid_and_others"


class Seen:

    def __init__(self):
        self.count = {}

    def next(self, sem, step=1):
        self.count[sem.num] = self.count.get(sem.num, 0) + step
        return self.count[sem.num]


def decoder_program(nc, dram, cols, out):
    with ExitStack() as whole:
        sems = []

        def sem(name):
            s = whole.enter_context(nc.semaphore(name))
            sems.append(s)
            return s

        def lane_sems(name):
            return [sem(f"{name}{u}") for u in LANE_RANGE]

        def sb(name, shape, dt=F32, scope=whole):
            return scope.enter_context(nc.sbuf_tensor(name, shape, dt))

        loaded = sem("loaded")
        stored = sem("stored")
        dve_step, act_step, pool_step = sem("dve_step"), sem("act_step"), sem("pool_step")
        prep = sem("prep")
        prep_taken = sem("prep_taken")
        prep_act = sem("prep_act")
        prep_row = sem("prep_row")
        x_in = lane_sems("x_in")
        x_done = lane_sems("x_done")
        var_ready = lane_sems("var_ready")
        rstd_ready = lane_sems("rstd_ready")
        xn_ready = lane_sems("xn_ready")
        xnT_psum = lane_sems("xnT_psum")
        xnT_ready = lane_sems("xnT_ready")
        ctxT_psum = lane_sems("ctxT_psum")
        ctxT_ready = lane_sems("ctxT_ready")
        proj_psum = lane_sems("proj_psum")
        qk_ready = lane_sems("qk_ready")
        qkT_psum = lane_sems("qkT_psum")
        kT_ready = lane_sems("kT_ready")
        v_ready = lane_sems("v_ready")
        expanded = lane_sems("expanded")
        bd_psum = lane_sems("bd_psum")
        bd_low = lane_sems("bd_low")
        bd_ready = lane_sems("bd_ready")
        bd_out = lane_sems("bd_out")
        bd_back = lane_sems("bd_back")
        scores_psum = lane_sems("scores_psum")
        scores_taken = lane_sems("scores_taken")
        probs_ready = lane_sems("probs_ready")
        pTB_psum = lane_sems("pTB_psum")
        pTC_psum = lane_sems("pTC_psum")
        pTB_ready = lane_sems("pTB_ready")
        pTC_ready = lane_sems("pTC_ready")
        oT_psum = lane_sems("oT_psum")
        oT_ready = lane_sems("oT_ready")
        o_psum = lane_sems("o_psum")
        att_ready = lane_sems("att_ready")
        attT_psum = lane_sems("attT_psum")
        attT_ready = lane_sems("attT_ready")
        y_psum = lane_sems("y_psum")
        gate_psum = lane_sems("gate_psum")
        gate_max = lane_sems("gate_max")
        gate_exp = lane_sems("gate_exp")
        small_ready = lane_sems("small_ready")
        smallT_psum = lane_sems("smallT_psum")
        smallT_ready = lane_sems("smallT_ready")
        h_psum = lane_sems("h_psum")
        h_ready = lane_sems("h_ready")
        h_odd_ready = lane_sems("h_odd_ready")
        y_taken = lane_sems("y_taken")
        logs_ready = lane_sems("logs_ready")
        kernel_ready = lane_sems("kernel_ready")
        logs_diff = lane_sems("logs_diff")

        pack = {n: sb(n, [128, dram[n].shape[1]]) for n in ("first", "later")}
        x_all = sb("x_all", [SEQ, BATCH * DIM])
        ctx_all = sb("ctx_all", [SEQ, BATCH * DIM])
        causal_bf = sb("causal_bf", [SEQ, 4, SEQ], BF16)
        maskadd_bf = sb("maskadd_bf", [SEQ, 4, SEQ], BF16)
        ident_bf = sb("ident_bf", [128, 128], BF16)
        w_up = sb("w_up", [DIM, HIDDEN0])
        w_down = sb("w_down", [128, HIDDEN0])
        up_bias = sb("up_bias", [128, 4])
        down_bias = sb("down_bias", [128, DIM])
        circ = sb("circ", [DIM, DIM])
        rel_low = sb("rel_low", [DIM, HEADS * SEQ])
        rel_high = sb("rel_high", [DIM, HEADS * SEQ])
        sel_int = sb("sel_int", [SEQ, SEQ], I32)

        bigA = [whole.enter_context(nc.psum_tensor(f"bigA{u}", [128, 1024], F32)) for u in LANE_RANGE]
        bankB = [whole.enter_context(nc.psum_tensor(f"bankB{u}", [128, 512], F32)) for u in LANE_RANGE]
        bankC = [whole.enter_context(nc.psum_tensor(f"bankC{u}", [128, 512], F32)) for u in LANE_RANGE]

        def field(name):
            for p in ("first", "later"):
                if name in cols[p]:
                    a, n, rows = cols[p][name]
                    return pack[p][0:rows, a:a + n]
            raise KeyError(name)

        ident = field("ident")
        head_mask = field("head_mask")

        def end_of_turn():
            nums = [s.num for s in sems]
            nc.gpsimd.sem_clear(range(min(nums), max(nums) + 1))
            nc.all_engine_barrier()

        def over_heads(t, n=HEADS):
            t = t[:, :]
            return t[:, None, :].to_broadcast([128, n, t.shape[1]])

        def per_head(t, inner=SEQ):
            return t[:, :, None].to_broadcast([128, t.shape[1], inner])

        with ExitStack() as scope, nc.Block() as block:
            rows = sb("rows", [1, dram["butterfly"].shape[1]], F32, scope)
            wide = [sb(f"wide{i}", [DIM, HIDDEN0], F32, scope) for i in range(2)]
            wide_t = sb("wide_t", [DIM, HIDDEN0], F32, scope)
            wide_s = sb("wide_s", [DIM, HIDDEN0], F32, scope)
            brow = [sb(f"brow{i}", [1, HIDDEN0], F32, scope) for i in range(2)]
            brow_t = sb("brow_t", [1, HIDDEN0], F32, scope)
            brow_s = sb("brow_s", [1, HIDDEN0], F32, scope)
            mask_raw = sb("mask_raw", [SEQ, SEQ], I32, scope)
            mask_f = sb("mask_f", [SEQ, SEQ], F32, scope)
            relT = sb("relT", [DIM, 2 * SEQ - 1], F32, scope)
            NS = 2 * STAGES0

            @block.sync
            def _(sp):
                sp.dma_start(pack["first"][:, :], dram["first"]).then_inc(loaded, 16)
                sp.dma_start(rows[:, :], dram["butterfly"]).then_inc(loaded, 16)
                sp.dma_start(mask_raw[:, :], dram["mask"]).then_inc(loaded, 16)
                sp.dma_start(x_all[:, :].rearrange("s (b d) -> s b d", b=BATCH),
                             dram["x"].rearrange("b s d -> s b d")).then_inc(loaded, 16)
                sp.dma_start(ctx_all[:, :].rearrange("s (b d) -> s b d", b=BATCH),
                             dram["ctx"].rearrange("b s d -> s b d")).then_inc(loaded, 16)
                sp.dma_start(pack["later"][:, :], dram["later"]).then_inc(loaded, 16)
                sp.wait_ge(loaded, 96)

            @block.tensor
            def _(pe):
                seen = Seen()
                pe.wait_ge(loaded, 96)
                for s in range(NS):
                    if s >= 2:
                        pe.wait_ge(prep_taken, s - 1)
                    for k in range(2):
                        a = s * 2 * HIDDEN0 + k * HIDDEN0
                        last = nc.tensor.matmul(bigA[s % 2][:, k * 512:k * 512 + 512], field("ones_row"),
                                                rows[0:1, a:a + HIDDEN0], start=True, stop=True)
                    last.then_inc(prep, 1)
                pe.wait_ge(prep_taken, NS)
                for c in range(4):
                    last = nc.tensor.transpose(bankB[0][:, c * 128:c * 128 + 128],
                                               wide[NS % 2][:, c * 128:c * 128 + 128], ident)
                last.then_inc(prep, 1)
                pe.wait_ge(prep_row, 1)
                for c in range(4):
                    last = nc.tensor.matmul(bankC[0][:, c:c + 1], brow[STAGES0 % 2][0:1, c * 128:c * 128 + 128],
                                            ident[0:1, 0:1], start=True, stop=True)
                last.then_inc(prep, 1)
                nc.tensor.matmul(bankC[1][:, 0:2 * SEQ - 1], field("L2_attn_WrT"), field("sin_rpe"),
                                 start=True, stop=True).then_inc(prep, 1)

            @block.vector
            def _(dve):
                seen = Seen()

                def link(ins):
                    ins.then_inc(dve_step, 1)
                    dve.wait_ge(dve_step, seen.next(dve_step))

                dve.wait_ge(loaded, 96)
                nc.vector.tensor_copy(ident_bf[:, :], ident)
                nc.vector.tensor_copy(causal_bf[:, :, :], over_heads(field("causal"), 4))
                nc.vector.tensor_copy(sel_int[:, :], field("rel_select"))
                link(nc.vector.tensor_scalar(mask_f[:, :], mask_raw[:, :], 0.0, MASKED, ALU.is_equal, ALU.mult))
                nc.vector.tensor_copy(maskadd_bf[:, :, :], over_heads(mask_f, 4))
                nc.vector.tensor_tensor(down_bias[:, :], field("L0_ffn_b_con"), field("L0_ffn_down_bias"), ALU.add)
                for s in range(NS):
                    first = s % STAGES0 == 0
                    stage = s if s < STAGES0 else NS - 1 - s
                    w = 2 ** stage
                    src = (field("L0_ffn_W_exp") if s < STAGES0 else field("L0_ffn_W_conT")) if first \
                        else wide[s % 2][:, :]
                    dst = w_up[:, :] if s == STAGES0 - 1 else wide[(s + 1) % 2][:, :]

                    def pairs(t):
                        return t.rearrange("p (n j s) -> p n j s", j=2, s=w)

                    dve.wait_ge(prep, s + 1)
                    diag, off = bigA[s % 2][:, 0:512], bigA[s % 2][:, 512:1024]
                    nc.vector.tensor_tensor(wide_t[:, :], src, diag, ALU.mult)
                    for j in range(2):
                        last = nc.vector.tensor_tensor(pairs(wide_s[:, :])[:, :, j, :], pairs(src)[:, :, 1 - j, :],
                                                       pairs(off)[:, :, j, :], ALU.mult)
                    link(last)
                    nc.vector.tensor_tensor(dst, wide_t[:, :], wide_s[:, :], ALU.add).then_inc(prep_taken, 1)
                    dve.wait_ge(prep_taken, s + 1)
                dve.wait_ge(prep, NS + 1)
                nc.vector.tensor_copy(w_down[:, :], bankB[0][:, :])
                dve.wait_ge(prep, NS + 2)
                nc.vector.tensor_tensor(up_bias[:, :], bankC[0][:, 0:4], field("L0_ffn_up_bias"), ALU.add)
                dve.wait_ge(prep, NS + 3)
                link(nc.vector.tensor_copy(relT[:, :], bankC[1][:, 0:2 * SEQ - 1]))
                for dst, a in ((rel_low, 0), (rel_high, SEQ - 1)):
                    nc.vector.tensor_tensor(dst[:, :].rearrange("p (h k) -> p h k", h=HEADS),
                                            over_heads(relT[:, a:a + SEQ]), per_head(head_mask), ALU.mult)

            @block.gpsimd
            def _(pool):
                seen = Seen()
                pool.wait_ge(loaded, 96)
                for s in range(STAGES0):
                    w = 2 ** s
                    src = field("L0_ffn_b_exp") if s == 0 else brow[s % 2][:, :]
                    diag = rows[0:1, s * 1024:s * 1024 + 512]
                    off = rows[0:1, s * 1024 + 512:s * 1024 + 1024]

                    def pairs(t):
                        return t.rearrange("p (n j s) -> p n j s", j=2, s=w)

                    nc.gpsimd.tensor_tensor(brow_t[:, :], src, diag, ALU.mult)
                    for j in range(2):
                        last = nc.gpsimd.tensor_tensor(pairs(brow_s[:, :])[:, :, j, :], pairs(src)[:, :, 1 - j, :],
                                                       pairs(off)[:, :, j, :], ALU.mult)
                    last.then_inc(pool_step, 1)
                    pool.wait_ge(pool_step, seen.next(pool_step))
                    last = nc.gpsimd.tensor_tensor(brow[(s + 1) % 2][:, :], brow_t[:, :], brow_s[:, :], ALU.add)
                    last.then_inc(pool_step, 1)
                    pool.wait_ge(pool_step, seen.next(pool_step))
                nc.gpsimd.tensor_copy(brow_t[:, :], brow[STAGES0 % 2][:, :]).then_inc(prep_row, 1)
        end_of_turn()

        def lane_sb(name, shape, dt=F32):
            return [sb(f"{name}{u}", shape, dt) for u in LANE_RANGE]

        x = lane_sb("x", [SEQ, DIM])
        xn = lane_sb("xn", [SEQ, DIM])
        xnT = lane_sb("xnT", [DIM, SEQ])
        ctx = lane_sb("ctx", [SEQ, DIM])
        ctxT = lane_sb("ctxT", [DIM, SEQ])
        qT = lane_sb("qT", [DIM, SEQ])
        qvT = lane_sb("qvT", [DIM, SEQ])
        kT = lane_sb("kT", [DIM, SEQ])
        tok = lane_sb("tok", [SEQ, 512])
        kX = lane_sb("kX", [DIM, HEADS * SEQ])
        sx = lane_sb("sx", [SEQ, HEADS * SEQ])
        pT = lane_sb("pT", [SEQ, HEADS * SEQ])
        zrel = lane_sb("zrel", [SEQ, HEADS * (SEQ + 1)])
        v32 = lane_sb("v32", [SEQ, HEADS, VPAD])
        oT = lane_sb("oT", [128, 512])
        att = lane_sb("att", [SEQ, DIM])
        attT = lane_sb("attT", [DIM, SEQ])
        stats = lane_sb("stats", [SEQ, 6])
        mv = lane_sb("mv", [SEQ, 2])
        rs = lane_sb("rs", [SEQ, 8])
        nmax = lane_sb("nmax", [SEQ, HEADS])
        hs = lane_sb("hs", [SEQ, 4 * HEADS])
        gate = lane_sb("gate", [SEQ, 64])
        gidx = lane_sb("gidx", [SEQ, 8], U32)
        gT = lane_sb("gT", [32, SEQ])
        golay = lane_sb("golay", [SEQ, DATA * CODE])
        dshift = pT

        def chained(engine, step_sem, seen):
            def link(ins):
                ins.then_inc(step_sem, 1)
                engine.wait_ge(step_sem, seen.next(step_sem))
            return link

        class TensorStages:
            def __init__(self, pe):
                self.pe, self.seen = pe, Seen()

            def wait(self, s):
                self.pe.wait_ge(s, self.seen.next(s))

            def context_transpose(self, u):
                self.wait(x_in[u])
                nc.tensor.transpose(bankC[u][:, 0:128], ctx[u][:, :], ident).then_inc(ctxT_psum[u], 1)
                self.wait(ctxT_ready[u])

            def norm_transpose(self):
                for u in LANE_RANGE:
                    self.wait(xn_ready[u])
                    nc.tensor.transpose(bankB[u][:, 0:128], xn[u][:, :], ident).then_inc(xnT_psum[u], 1)
                for u in LANE_RANGE:
                    self.wait(xnT_ready[u])

            def project_rope(self, u):
                nc.tensor.matmul(bigA[u][:, 0:512], xnT[u][:, :], field("L0_attn_WqksT"), start=True, stop=True)
                nc.tensor.matmul(bigA[u][:, 512:640], xnT[u][:, :], field("L0_attn_WvT"),
                                 start=True, stop=True).then_inc(proj_psum[u], 1)

            def rows_transpose(self, u):
                self.wait(qk_ready[u])
                nc.tensor.transpose(bankB[u][:, 0:128], tok[u][:, 0:128], ident)
                nc.tensor.transpose(bankB[u][:, 128:256], tok[u][:, 128:256], ident).then_inc(qkT_psum[u], 1)

            def project(self, u, name, source):
                nc.tensor.matmul(bankB[u][:, 0:128], field(name + "_WqT"), xnT[u][:, :], start=True, stop=True)
                nc.tensor.matmul(bankB[u][:, 128:256], field(name + "_WkT"), source[u][:, :], start=True, stop=True)
                nc.tensor.matmul(bigA[u][:, 512:640], source[u][:, :], field(name + "_WvT"),
                                 start=True, stop=True).then_inc(proj_psum[u], 1)

            def position_scores(self):
                for c in range(4):
                    for u in LANE_RANGE:
                        if c == 0:
                            self.wait(kT_ready[u])
                            self.wait(v_ready[u])
                        else:
                            self.wait(bd_ready[u])
                        nc.tensor.matmul(bigA[u][:, 0:512], qvT[u][:, :], rel_low[:, c * 512:c * 512 + 512],
                                         start=True, stop=True)
                        nc.tensor.matmul(bigA[u][:, 512:1024], qvT[u][:, :], rel_high[:, c * 512:c * 512 + 512],
                                         start=True, stop=True).then_inc(bd_psum[u], 1)
                for u in LANE_RANGE:
                    self.wait(bd_ready[u])

            def scores(self, u, half, mask, left=None, relative=False):
                self.wait(expanded[u])
                if half == 0 and not relative:
                    self.wait(kT_ready[u])
                    if left is None:
                        self.wait(v_ready[u])
                if half == 1:
                    self.wait(scores_taken[u])
                left = qT if left is None else left
                for b in range(2):
                    a = half * HALF + b * QUARTER
                    dst = bigA[u][:, b * 512:b * 512 + 512]
                    last = nc.tensor.matmul(dst, left[u][:, :], kX[u][:, a:a + QUARTER],
                                            start=True, stop=mask is None)
                    if mask is not None:
                        last = nc.tensor.matmul(dst, ident_bf[:, :], mask[:, :, :].rearrange("p h k -> p (h k)"),
                                                start=False, stop=True)
                last.then_inc(scores_psum[u], 1)

            def transpose_probs(self, u, half):
                self.wait(probs_ready[u])
                for bank, psum, ready in ((bankB, pTB_psum, pTB_ready), (bankC, pTC_psum, pTC_ready)):
                    if half == 1:
                        self.wait(ready[u])
                    for h in range(4):
                        a = half * HALF + (0 if bank is bankB else QUARTER) + h * SEQ
                        last = nc.tensor.transpose(bank[u][:, h * 128:h * 128 + 128], sx[u][:, a:a + SEQ], ident)
                    last.then_inc(psum[u], 1)

            def weighted_values(self, u, weights=None):
                direct = weights is not None
                self.wait(scores_taken[u])
                if direct:
                    self.wait(v_ready[u])
                for t in range(4):
                    if t >= 2 and not direct:
                        self.wait((pTB_ready, pTC_ready)[t - 2][u])
                    for g in range(4):
                        h = 4 * t + g
                        src = weights[u] if direct else pT[u]
                        last = nc.tensor.matmul(bigA[u][32 * g:32 * g + 32, t * 128:t * 128 + 128], v32[u][:, h, :],
                                                src[:, h * SEQ:h * SEQ + SEQ], start=True, stop=True)
                last.then_inc(oT_psum[u], 1)

            def values_transpose(self, u):
                self.wait(oT_ready[u])
                for t in range(4):
                    last = nc.tensor.transpose(bigA[u][:, 512 + t * 128:640 + t * 128],
                                               oT[u][:, t * 128:t * 128 + 128], ident)
                last.then_inc(o_psum[u], 1)

            def output_transpose(self, u):
                self.attention_taken(u)
                nc.tensor.transpose(bankB[u][:, 0:128], att[u][:, :], ident).then_inc(attT_psum[u], 1)

            def output_product(self, u, weight):
                self.wait(attT_ready[u])
                nc.tensor.matmul(bankC[u][:, 0:128], attT[u][:, :], field(weight),
                                 start=True, stop=True).then_inc(y_psum[u], 1)

            def attention(self, mask=None, relative=False):
                for half in range(2):
                    for u in LANE_RANGE:
                        self.scores(u, half, mask, None, relative)
                for half in range(2):
                    for u in LANE_RANGE:
                        self.transpose_probs(u, half)
                for u in LANE_RANGE:
                    self.weighted_values(u)
                for u in LANE_RANGE:
                    self.values_transpose(u)

            def attention_taken(self, u):
                self.wait(att_ready[u])

            def lanes(self, stage, *args):
                for u in LANE_RANGE:
                    stage(u, *args)

            def decay(self, u):
                self.seen.next(xn_ready[u])
                self.wait(small_ready[u])
                nc.tensor.matmul(bankC[u][:, 0:128], field("decay"), tok[u][:, 0:128],
                                 start=True, stop=True).then_inc(y_psum[u], 1)

            def butterfly_mlp(self, u):
                for c in range(4):
                    last = nc.tensor.matmul(bigA[u][:, c * 128:c * 128 + 128], w_up[:, c * 128:c * 128 + 128],
                                            xnT[u][:, :], start=True, stop=True)
                last.then_inc(h_psum[u], 1)

            def butterfly_mlp_out(self, u):
                self.wait(h_ready[u])
                for c in range(4):
                    last = nc.tensor.matmul(bankC[u][:, 0:128], kX[u][:, c * 128:c * 128 + 128],
                                            w_down[:, c * 128:c * 128 + 128], start=(c == 0), stop=(c == 3))
                last.then_inc(y_psum[u], 1)

            def filtered(self, u):
                nc.tensor.matmul(bankB[u][:, 0:128], circ[:, :], xnT[u][:, :], start=True, stop=True)\
                    .then_inc(attT_psum[u], 1)
                nc.tensor.matmul(bankC[u][:, 0:128], xnT[u][:, :], circ[:, :], start=True, stop=False)

            def latents(self, u):
                self.wait(attT_ready[u])
                nc.tensor.matmul(bankB[u][:, 128:128 + CODE], attT[u][:, :], field("L1_attn_W_el"),
                                 start=True, stop=True).then_inc(gate_psum[u], 1)

            def code_transpose(self, u):
                self.wait(small_ready[u])
                nc.tensor.transpose(bankB[u][0:CODE, 0:128], gate[u][:, 0:CODE], ident).then_inc(smallT_psum[u], 1)

            def code_product(self, u):
                self.wait(smallT_ready[u])
                nc.tensor.matmul(bankC[u][:, 0:128], gT[u][0:CODE, :], field("L1_attn_W_le"),
                                 start=False, stop=True).then_inc(y_psum[u], 1)

            def router(self, u, weight):
                nc.tensor.matmul(bankC[u][:, 0:EXPERTS], xnT[u][:, :], field(weight),
                                 start=True, stop=True).then_inc(gate_psum[u], 1)

            def gate_transpose(self, u):
                self.wait(small_ready[u])
                nc.tensor.transpose(bankB[u][0:EXPERTS, 0:128], gate[u][:, 0:EXPERTS], ident)\
                    .then_inc(smallT_psum[u], 1)

            def gate_bias(self, u, bias):
                self.wait(smallT_ready[u])
                nc.tensor.matmul(bankB[u][:, 128:256], gT[u][0:EXPERTS, :], field(bias),
                                 start=True, stop=True).then_inc(y_psum[u], 1)

            def linear_experts(self, u, weight):
                for b in range(2):
                    last = nc.tensor.matmul(bigA[u][:, b * 512:b * 512 + 512], xnT[u][:, :],
                                            field(weight)[:, b * 512:b * 512 + 512], start=True, stop=True)
                last.then_inc(h_psum[u], 1)

            def mlp_hidden(self, u, e):
                for c in range(4):
                    a = (e * 4 + c) * 128
                    last = nc.tensor.matmul(bigA[u][:, (e % 2) * 512 + c * 128:(e % 2) * 512 + c * 128 + 128],
                                            field("L3_ffn_W1")[:, a:a + 128], xnT[u][:, :], start=True, stop=True)
                last.then_inc(h_psum[u], 1)

            def mlp_out(self, u, e):
                self.wait(h_odd_ready[u] if e % 2 else h_ready[u])
                if e >= 1:
                    self.wait(y_taken[u])
                for c in range(4):
                    a = (e * 4 + c) * 128
                    last = nc.tensor.matmul(bankC[u][:, 128:256], kX[u][:, (e % 2) * 512 + c * 128:][:, 0:128],
                                            field("L3_ffn_W2")[:, a:a + 128], start=(c == 0), stop=(c == 3))
                last.then_inc(y_psum[u], 1)

            def single_scores(self, u):
                self.wait(kT_ready[u])
                nc.tensor.matmul(bigA[u][:, 0:128], qT[u][:, :], kT[u][:, :], start=True, stop=True)\
                    .then_inc(scores_psum[u], 1)

            def single_transpose(self, u):
                self.wait(probs_ready[u])
                nc.tensor.transpose(bankB[u][:, 0:128], sx[u][:, 0:128], ident).then_inc(attT_psum[u], 1)

            def single_values(self, u):
                self.wait(attT_ready[u])
                self.wait(v_ready[u])
                nc.tensor.matmul(bankC[u][:, 0:128], attT[u][:, :], tok[u][:, 0:128], start=True, stop=True)\
                    .then_inc(y_psum[u], 1)

            def project_rows(self, u):
                nc.tensor.matmul(bigA[u][:, 0:384], xnT[u][:, :], field("L3_attn_w_qkvT"), start=True, stop=True)\
                    .then_inc(proj_psum[u], 1)

        class VectorStages:
            def __init__(self, dve):
                self.dve, self.seen = dve, Seen()
                self.link = chained(dve, dve_step, self.seen)

            def wait(self, s):
                self.dve.wait_ge(s, self.seen.next(s))

            def lanes(self, stage, *args):
                for u in LANE_RANGE:
                    stage(u, *args)

            def first_wait(self, u):
                self.wait(x_in[u])

            def norm_stats(self, u):
                self.link(nc.vector.bn_stats(stats[u][:, :], x[u][:, :]))
                self.link(nc.vector.bn_aggr(mv[u][:, :], stats[u][:, :]))
                nc.vector.tensor_scalar(rs[u][:, 0:1], mv[u][:, 1:2], EPS_LN, None, ALU.add)\
                    .then_inc(var_ready[u], 1)

            def norm_apply(self, u):
                self.wait(rstd_ready[u])
                v, r, t, r2 = (rs[u][:, i:i + 1] for i in (0, 1, 2, 3))
                self.link(nc.vector.scalar_tensor_tensor(out=t, in0=r, scalar=v, in1=r, op0=ALU.mult, op1=ALU.mult))
                self.link(nc.vector.tensor_scalar(t, t, -0.5, 1.5, ALU.mult, ALU.add))
                self.link(nc.vector.tensor_tensor(r2, r, t, ALU.mult))
                nc.vector.tensor_scalar(xn[u][:, :], x[u][:, :], mv[u][:, 0:1], r2, ALU.subtract, ALU.mult)\
                    .then_inc(xn_ready[u], 1)

            def norm(self):
                self.lanes(self.norm_stats)
                self.lanes(self.norm_apply)

            def pad_values(self):
                for u in LANE_RANGE:
                    nc.vector.memset(v32[u][:, :, HDIM + 1:VPAD], 0.0)
                    self.link(nc.vector.memset(v32[u][:, :, HDIM:HDIM + 1], 1.0))

            def rope(self, u):
                self.wait(proj_psum[u])
                nc.vector.tensor_tensor(tok[u][:, 0:256], bigA[u][:, 0:256], field("rope_cos"), ALU.mult)
                self.link(nc.vector.tensor_tensor(tok[u][:, 256:512], bigA[u][:, 256:512], field("rope_sin"), ALU.mult))
                nc.vector.tensor_tensor(tok[u][:, 0:256], tok[u][:, 0:256], tok[u][:, 256:512], ALU.add)\
                    .then_inc(qk_ready[u], 1)

            def heads_of(self, t):
                return t.rearrange("p (h d) -> p h d", h=HEADS)

            def take_projection(self, u, kind, name=""):
                self.wait(proj_psum[u])
                q, k, v = bankB[u][:, 0:128], bankB[u][:, 128:256], bigA[u][:, 512:640]
                vh, vo = self.heads_of(v), v32[u][:, :, 0:HDIM]
                if kind == "bias":
                    nc.vector.tensor_scalar(kT[u][:, :], k, field(name + "_bk"), None, ALU.add)
                    nc.vector.tensor_scalar(qT[u][:, :], q, field(name + "_bq"), None, ALU.add).then_inc(kT_ready[u], 1)
                    nc.vector.tensor_tensor(vo, vh, self.heads_of(field(name + "_bv")), ALU.add).then_inc(v_ready[u], 1)
                elif kind == "relu":
                    nc.vector.tensor_scalar(kT[u][:, :], k, 0.0, None, ALU.max)
                    nc.vector.tensor_scalar(qT[u][:, :], q, 0.0, None, ALU.max).then_inc(kT_ready[u], 1)
                    nc.vector.tensor_scalar(vo, vh, 0.0, None, ALU.max).then_inc(v_ready[u], 1)
                else:
                    nc.vector.tensor_copy(kT[u][:, :], k)
                    nc.vector.tensor_scalar(qvT[u][:, :], q, field("L2_attn_v_bias"), None, ALU.add)
                    nc.vector.tensor_scalar(qT[u][:, :], q, field("L2_attn_u_bias"), None, ALU.add)\
                        .then_inc(kT_ready[u], 1)
                    nc.vector.tensor_copy(vo, vh).then_inc(v_ready[u], 1)

            def position_scores(self):
                for u in LANE_RANGE:
                    z = zrel[u][:, :].rearrange("p (h c) -> p h c", h=HEADS)
                    self.link(nc.vector.memset(z[:, :, 0:1], 0.0))
                for c in range(4):
                    for u in LANE_RANGE:
                        z = zrel[u][:, :].rearrange("p (h c) -> p h c", h=HEADS)
                        self.wait(bd_low[u])
                        nc.vector.copy_predicated(z[:, 4 * c:4 * c + 4, 1:SEQ + 1], over_heads(sel_int, 4),
                                                  bigA[u][:, 512:1024].rearrange("p (h k) -> p h k", h=4))\
                            .then_inc(bd_ready[u], 1)

            def take_scores(self, u, half, relative=False):
                self.wait(scores_psum[u])
                heads = slice(8 * half, 8 * half + 8)
                s = bigA[u][:, :].rearrange("p (h k) -> p h k", h=8)
                o = sx[u][:, :].rearrange("p (h k) -> p h k", h=HEADS)[:, heads, :]
                if relative:
                    if half == 0:
                        self.dve.wait_ge(bd_back[u], 16)
                    d = dshift[u][:, :].rearrange("p (h k) -> p h k", h=HEADS)[:, heads, :]
                    self.link(nc.vector.tensor_tensor(o, s, d, ALU.add))
                    s = o
                self.link(nc.vector.tensor_reduce(nmax[u][:, heads], s, AX, ALU.max, negate=True))
                nc.vector.tensor_tensor(o, s, per_head(nmax[u][:, heads]), ALU.add).then_inc(scores_taken[u], 1)

            def take_transposed(self, u, half):
                self.wait(pTC_psum[u])
                a = half * HALF + QUARTER
                nc.vector.tensor_copy(pT[u][:, a:a + QUARTER], bankC[u][:, :]).then_inc(pTC_ready[u], 1)

            def normalise(self, u):
                self.wait(o_psum[u])
                o = bigA[u][:, 512:1024].rearrange("p (h d) -> p h d", h=HEADS)
                r = hs[u][:, 0:HEADS]
                self.link(nc.vector.reciprocal(r[:, :, None], o[:, :, HDIM:HDIM + 1]))
                ins = nc.vector.tensor_tensor(self.heads_of(att[u][:, :]), o[:, :, 0:HDIM], per_head(r, HDIM), ALU.mult)
                ins.then_inc(att_ready[u], 1)
                self.wait(att_ready[u])

            def attention(self, relative=False):
                for half in range(2):
                    self.lanes(self.take_scores, half, relative)
                for half in range(2):
                    self.lanes(self.take_transposed, half)
                self.lanes(self.normalise)

            def add_attention(self, u):
                self.link(nc.vector.tensor_tensor(x[u][:, :], x[u][:, :], att[u][:, :], ALU.add))

            def add_result(self, u, bias=None, where=None):
                self.wait(y_psum[u])
                src = bankC[u][:, 0:128] if where is None else where[u][:, 128:256]
                self.link(nc.vector.tensor_tensor(x[u][:, :], x[u][:, :], src, ALU.add))
                if bias is not None:
                    self.link(nc.vector.tensor_tensor(x[u][:, :], x[u][:, :], bias, ALU.add))

            def retention(self, u):
                self.wait(y_psum[u])
                self.link(nc.vector.tensor_tensor(att[u][:, :], xn[u][:, :], bankC[u][:, 0:128], ALU.mult))
                self.link(nc.vector.tensor_tensor(x[u][:, :], x[u][:, :], att[u][:, :], ALU.add))

            def square_context(self, u):
                nc.vector.tensor_tensor(tok[u][:, 0:128], ctx[u][:, :], ctx[u][:, :], ALU.mult)\
                    .then_inc(small_ready[u], 1)

            def code_bits(self, u):
                self.wait(gate_psum[u])
                bits, data = gate[u][:, 0:CODE], gate[u][:, 0:DATA]
                syn, flip, weight = gate[u][:, 24:36], gate[u][:, 36:48], gate[u][:, 48:49]
                fix = gate[u][:, 49:50]
                lat = gate[u][:, 0:CODE]
                self.link(nc.vector.tensor_tensor(lat, bankB[u][:, 128:128 + CODE], field("L1_attn_b_el"), ALU.add))
                self.link(nc.vector.tensor_scalar(bits, lat, 0.0, None, ALU.is_gt))
                g = golay[u][:, :].rearrange("p (r c) -> p r c", r=DATA)
                parity = field("golay").rearrange("p (r c) -> p r c", r=DATA)
                self.link(nc.vector.tensor_tensor(g, bits[:, None, :].to_broadcast([SEQ, DATA, CODE]), parity, ALU.mult))
                self.link(nc.vector.tensor_reduce(syn, g, AX, ALU.add))
                self.link(nc.vector.tensor_scalar(syn, syn, 0.5, None, ALU.is_gt))
                nc.vector.tensor_reduce(weight, syn, AX, ALU.add)
                self.link(nc.vector.tensor_scalar(flip, data, -2.0, 1.0, ALU.mult, ALU.add))
                self.link(nc.vector.tensor_tensor(flip, flip, syn, ALU.mult))
                self.link(nc.vector.tensor_scalar(fix, weight, 3.0, None, ALU.is_le))
                nc.vector.scalar_tensor_tensor(out=data, in0=flip, scalar=fix, in1=data, op0=ALU.mult, op1=ALU.add)\
                    .then_inc(small_ready[u], 1)
                self.wait(small_ready[u])

            def gates_start(self, u, bias):
                self.wait(gate_psum[u])
                logits, top = gate[u][:, 8:16], gate[u][:, 16:24]
                self.link(nc.vector.tensor_tensor(logits, bankC[u][:, 0:EXPERTS], field(bias), ALU.add))
                self.link(nc.vector.max(top, logits))
                nc.vector.max_index(gidx[u][:, :], top, logits)
                nc.vector.tensor_scalar(gate[u][:, 24:25], top[:, 0:1], -1.0, None, ALU.mult).then_inc(gate_max[u], 1)

            def gates_finish(self, u, over_chosen):
                self.wait(gate_max[u])
                ix, one, two = gate[u][:, 26:28], gate[u][:, 32:40], gate[u][:, 40:48]
                e = gate[u][:, 48:56]
                total, inv = gate[u][:, 28:29], gate[u][:, 29:30]
                self.link(nc.vector.tensor_copy(ix, gidx[u][:, 0:2]))
                nc.vector.tensor_scalar(one, field("iota8"), ix[:, 0:1], None, ALU.is_equal)
                self.link(nc.vector.tensor_scalar(two, field("iota8"), ix[:, 1:2], None, ALU.is_equal))
                self.link(nc.vector.tensor_tensor(one, one, two, ALU.add))
                self.wait(gate_exp[u])
                self.link(nc.vector.tensor_tensor(two, one, e, ALU.mult))
                self.link(nc.vector.tensor_reduce(total, two if over_chosen else e, AX, ALU.add))
                self.link(nc.vector.reciprocal(inv, total))
                nc.vector.tensor_scalar(gate[u][:, 0:EXPERTS], two, inv, None, ALU.mult).then_inc(small_ready[u], 1)
                self.wait(small_ready[u])

            def add_linear_experts(self, u):
                self.wait(h_psum[u])
                for e in range(EXPERTS):
                    self.link(nc.vector.scalar_tensor_tensor(
                        out=x[u][:, :], in0=bigA[u][:, e * 128:e * 128 + 128], scalar=gate[u][:, e:e + 1],
                        in1=x[u][:, :], op0=ALU.mult, op1=ALU.add))

            def mlp_hidden(self, u, e):
                if e % 2 == 0:
                    self.seen.next(h_psum[u])
                    return
                self.wait(h_psum[u])
                for c in range(4):
                    i = e * 4 + c
                    last = nc.vector.tensor_scalar(kX[u][:, 512 + c * 128:640 + c * 128],
                                                   bigA[u][:, 512 + c * 128:640 + c * 128],
                                                   field("L3_ffn_b1")[:, i:i + 1], 0.0, ALU.add, ALU.max)
                last.then_inc(h_odd_ready[u], 1)

            def mlp_out(self, u, e):
                self.wait(y_psum[u])
                nc.vector.scalar_tensor_tensor(
                    out=x[u][:, :], in0=bankC[u][:, 128:256], scalar=gate[u][:, e:e + 1],
                    in1=x[u][:, :], op0=ALU.mult, op1=ALU.add).then_inc(y_taken[u], 1)
                self.wait(y_taken[u])

            def unit_rows(self, u):
                self.wait(proj_psum[u])
                b = field("L3_attn_b_qkv")
                nc.vector.tensor_tensor(v32[u][:, :, 0:HDIM], self.heads_of(bigA[u][:, 256:384]),
                                        self.heads_of(b[:, 256:384]), ALU.add)
                self.link(nc.vector.tensor_tensor(tok[u][:, 0:256], bigA[u][:, 0:256], b[:, 0:256], ALU.add))
                self.link(nc.vector.tensor_tensor(tok[u][:, 256:512], tok[u][:, 0:256], tok[u][:, 0:256], ALU.mult))
                n2 = hs[u][:, 0:2 * HEADS]
                self.link(nc.vector.tensor_reduce(n2, tok[u][:, 256:512].rearrange("p (h d) -> p h d", d=HDIM), AX, ALU.add))
                nc.vector.tensor_scalar(n2, n2, 1e-24, None, ALU.max).then_inc(var_ready[u], 1)

            def unit_apply(self, u):
                self.wait(rstd_ready[u])
                n2, r = hs[u][:, 0:2 * HEADS], hs[u][:, 2 * HEADS:4 * HEADS]
                t = golay[u][:, 0:2 * HEADS]
                self.link(nc.vector.tensor_scalar(r, r, LN_SHIFT ** 0.5, None, ALU.mult))
                self.link(nc.vector.tensor_tensor(t, n2, r, ALU.mult))
                self.link(nc.vector.tensor_tensor(t, t, r, ALU.mult))
                self.link(nc.vector.tensor_scalar(t, t, -0.5, 1.5, ALU.mult, ALU.add))
                self.link(nc.vector.tensor_tensor(r, r, t, ALU.mult))
                w = tok[u][:, 0:256].rearrange("p (h d) -> p h d", d=HDIM)
                nc.vector.tensor_tensor(w, w, per_head(r, HDIM), ALU.mult).then_inc(qk_ready[u], 1)

            def clip_cosines(self, u, half):
                self.wait(scores_psum[u])
                nc.vector.tensor_scalar(sx[u][:, half * HALF:half * HALF + HALF], bigA[u][:, :], -CLIP, CLIP,
                                        ALU.max, ALU.min).then_inc(scores_taken[u], 1)

            def column_sums(self, u):
                self.wait(kernel_ready[u])
                nc_sum, inv = hs[u][:, 0:HEADS], hs[u][:, HEADS:2 * HEADS]
                self.link(nc.vector.tensor_reduce(nc_sum, sx[u][:, :].rearrange("p (h k) -> p h k", h=HEADS), AX, ALU.add))
                self.link(nc.vector.reciprocal(inv, nc_sum))
                nc.vector.memset(v32[u][:, :, HDIM + 1:HDIM + 2], 1.0)
                nc.vector.tensor_copy(v32[u][:, :, HDIM:HDIM + 1], inv[:, :, None])
                nc.vector.tensor_tensor(v32[u][:, :, 0:HDIM], v32[u][:, :, 0:HDIM], per_head(inv, HDIM), ALU.mult)\
                    .then_inc(v_ready[u], 1)

            def manifold_normalise(self, u):
                self.wait(o_psum[u])
                o = bigA[u][:, 512:1024].rearrange("p (h d) -> p h d", h=HEADS)
                inv, t = hs[u][:, 0:HEADS], hs[u][:, HEADS:2 * HEADS]
                self.link(nc.vector.reciprocal(inv[:, :, None], o[:, :, HDIM + 1:HDIM + 2]))
                self.link(nc.vector.tensor_tensor(t[:, :, None], inv[:, :, None], o[:, :, HDIM:HDIM + 1], ALU.mult))
                self.link(nc.vector.tensor_scalar(t, t, 1e-12, None, ALU.max))
                self.link(nc.vector.reciprocal(t, t))
                self.link(nc.vector.tensor_tensor(t, t, inv, ALU.mult))
                nc.vector.tensor_tensor(self.heads_of(att[u][:, :]), o[:, :, 0:HDIM], per_head(t, HDIM), ALU.mult)\
                    .then_inc(att_ready[u], 1)

            def take_single(self, u):
                self.wait(proj_psum[u])
                nc.vector.tensor_scalar(kT[u][:, :], bankB[u][:, 128:256], field("L3_xattn_bk"), None, ALU.add)
                nc.vector.tensor_scalar(qT[u][:, :], bankB[u][:, 0:128], field("L3_xattn_bq"), None, ALU.add)\
                    .then_inc(kT_ready[u], 1)
                nc.vector.tensor_tensor(tok[u][:, 0:128], bigA[u][:, 512:640], field("L3_xattn_bv"), ALU.add)\
                    .then_inc(v_ready[u], 1)

            def single_max(self, u):
                self.wait(scores_psum[u])
                m = nmax[u][:, 0:1]
                self.link(nc.vector.tensor_reduce(m, bigA[u][:, 0:128], AX, ALU.max, negate=True))
                nc.vector.tensor_scalar(m, m, DIM ** -0.5, None, ALU.mult).then_inc(scores_taken[u], 1)

            def single_result(self, u):
                self.wait(y_psum[u])
                self.link(nc.vector.reciprocal(hs[u][:, 1:2], hs[u][:, 0:1]))
                self.link(nc.vector.scalar_tensor_tensor(out=x[u][:, :], in0=bankC[u][:, 0:128], scalar=hs[u][:, 1:2],
                                                         in1=x[u][:, :], op0=ALU.mult, op1=ALU.add))

            def finished(self, u):
                nc.vector.tensor_copy(att[u][:, :], x[u][:, :]).then_inc(x_done[u], 1)

        class ScalarStages:
            def __init__(self, act):
                self.act, self.seen = act, Seen()
                self.link = chained(act, act_step, self.seen)

            def wait(self, s):
                self.act.wait_ge(s, self.seen.next(s))

            def lanes(self, stage, *args):
                for u in LANE_RANGE:
                    stage(u, *args)

            def norm(self):
                for u in LANE_RANGE:
                    self.wait(var_ready[u])
                    self.link(nc.scalar.activation(rs[u][:, 2:3], rs[u][:, 0:1], ACT.Ln))
                    nc.scalar.activation(rs[u][:, 1:2], rs[u][:, 2:3], ACT.Exp, scale=-0.5).then_inc(rstd_ready[u], 1)
                for u in LANE_RANGE:
                    self.wait(xnT_psum[u])
                    nc.scalar.copy(xnT[u][:, :], bankB[u][:, 0:128]).then_inc(xnT_ready[u], 1)

            def context(self, u):
                self.wait(ctxT_psum[u])
                nc.scalar.copy(ctxT[u][:, :], bankC[u][:, 0:128]).then_inc(ctxT_ready[u], 1)

            def rope_values(self, u):
                self.wait(proj_psum[u])
                nc.scalar.copy(v32[u][:, :, 0:HDIM], bigA[u][:, 512:640].rearrange("p (h d) -> p h d", h=HEADS))\
                    .then_inc(v_ready[u], 1)

            def take_qkT(self, u):
                self.wait(qkT_psum[u])
                nc.scalar.copy(kT[u][:, :], bankB[u][:, 128:256])
                nc.scalar.copy(qT[u][:, :], bankB[u][:, 0:128]).then_inc(kT_ready[u], 1)

            def position_scores(self):
                for c in range(4):
                    for u in LANE_RANGE:
                        self.wait(bd_psum[u])
                        z = zrel[u][:, :].rearrange("p (h c) -> p h c", h=HEADS)
                        nc.scalar.copy(z[:, 4 * c:4 * c + 4, 1:SEQ + 1],
                                       bigA[u][:, 0:512].rearrange("p (h k) -> p h k", h=4)).then_inc(bd_low[u], 1)

            def exponentials(self, u, half, scale):
                self.wait(scores_taken[u])
                s = sx[u][:, half * HALF:half * HALF + HALF]
                nc.scalar.activation(s, s, ACT.Exp, scale=scale).then_inc(probs_ready[u], 1)

            def take_transposed(self, u, half):
                self.wait(pTB_psum[u])
                nc.scalar.copy(pT[u][:, half * HALF:half * HALF + QUARTER], bankB[u][:, :]).then_inc(pTB_ready[u], 1)

            def take_values(self, u):
                self.wait(oT_psum[u])
                nc.scalar.copy(oT[u][:, :], bigA[u][:, 0:512]).then_inc(oT_ready[u], 1)

            def attention(self, scale):
                for half in range(2):
                    self.lanes(self.exponentials, half, scale)
                for half in range(2):
                    self.lanes(self.take_transposed, half)
                self.lanes(self.take_values)

            def take_attT(self, u):
                self.wait(attT_psum[u])
                nc.scalar.copy(attT[u][:, :], bankB[u][:, 0:128]).then_inc(attT_ready[u], 1)

            def gelu(self, u):
                self.wait(h_psum[u])
                for c in range(4):
                    last = nc.scalar.activation(kX[u][:, c * 128:c * 128 + 128], bigA[u][:, c * 128:c * 128 + 128],
                                                ACT.Gelu, bias=up_bias[:, c:c + 1])
                last.then_inc(h_ready[u], 1)

            def skip_hidden(self, u):
                self.seen.next(h_psum[u])

            def take_small(self, u, n):
                self.wait(smallT_psum[u])
                nc.scalar.copy(gT[u][0:n, :], bankB[u][0:n, 0:128]).then_inc(smallT_ready[u], 1)

            def gates(self, u):
                self.wait(gate_max[u])
                nc.scalar.activation(gate[u][:, 48:56], gate[u][:, 8:16], ACT.Exp, bias=gate[u][:, 24:25])\
                    .then_inc(gate_exp[u], 1)

            def mlp_hidden(self, u, e):
                if e % 2 == 1:
                    self.seen.next(h_psum[u])
                    return
                self.wait(h_psum[u])
                for c in range(4):
                    i = e * 4 + c
                    last = nc.scalar.activation(kX[u][:, c * 128:c * 128 + 128], bigA[u][:, c * 128:c * 128 + 128],
                                                ACT.Relu, bias=field("L3_ffn_b1")[:, i:i + 1])
                last.then_inc(h_ready[u], 1)

            def unit_norms(self, u):
                self.wait(var_ready[u])
                n2, r = hs[u][:, 0:2 * HEADS], hs[u][:, 2 * HEADS:4 * HEADS]
                self.link(nc.scalar.activation(r, n2, ACT.Ln, scale=LN_SHIFT))
                nc.scalar.activation(r, r, ACT.Exp, scale=-0.5).then_inc(rstd_ready[u], 1)

            def cosine_logs(self, u):
                self.wait(scores_taken[u])
                self.wait(scores_taken[u])
                self.link(nc.scalar.activation(pT[u][:, :], sx[u][:, :], ACT.Ln, scale=-1.0, bias=field("ones")))
                nc.scalar.activation(sx[u][:, :], sx[u][:, :], ACT.Ln, scale=1.0, bias=field("ones"))\
                    .then_inc(logs_ready[u], 1)

            def angles(self, u):
                self.wait(logs_diff[u])
                self.link(nc.scalar.activation(sx[u][:, :], pT[u][:, :], ACT.Tanh, scale=0.25))
                self.link(nc.scalar.activation(sx[u][:, :], sx[u][:, :], ACT.Arctan))

            def kernel_values(self, u):
                self.link(nc.scalar.activation(sx[u][:, :], sx[u][:, :], ACT.Ln, scale=2.0, bias=field("one_half_pi")))
                nc.scalar.activation(sx[u][:, :], sx[u][:, :], ACT.Exp, scale=-3.2).then_inc(kernel_ready[u], 1)

            def single_exp(self, u):
                self.wait(scores_taken[u])
                nc.scalar.activation(sx[u][:, 0:128], bigA[u][:, 0:128], ACT.Exp, scale=DIM ** -0.5,
                                     bias=nmax[u][:, 0:1], accum_out=hs[u][:, 0:1]).then_inc(probs_ready[u], 1)

        def load_tables(name):
            nc.scalar.preload_act_table_set(name)

        class PoolStages:
            def __init__(self, pool):
                self.pool, self.seen = pool, Seen()

            def wait(self, s):
                self.pool.wait_ge(s, self.seen.next(s))

            def load(self, turn):
                for u in LANE_RANGE:
                    at = bass.ds(turn * (LANES * DIM) + u * DIM, DIM)
                    nc.gpsimd.tensor_copy(ctx[u][:, :], ctx_all[:, at])
                    nc.gpsimd.tensor_copy(x[u][:, :], x_all[:, at]).then_inc(x_in[u], 1)

            def expand(self, src=None):
                src = kT if src is None else src
                for half in range(2):
                    for u in LANE_RANGE:
                        if half == 0:
                            self.wait(kT_ready[u])
                        h = slice(8 * half, 8 * half + 8)
                        dst = kX[u][:, half * HALF:half * HALF + HALF].rearrange("p (h k) -> p h k", h=8)
                        nc.gpsimd.tensor_tensor(dst, over_heads(src[u], 8), per_head(head_mask[:, h]), ALU.mult)\
                            .then_inc(expanded[u], 1)

            def log_differences(self):
                for u in LANE_RANGE:
                    self.wait(logs_ready[u])
                    nc.gpsimd.tensor_tensor(pT[u][:, :], pT[u][:, :], sx[u][:, :], ALU.subtract)\
                        .then_inc(logs_diff[u], 1)

            def store(self, turn):
                for u in LANE_RANGE:
                    at = bass.ds(turn * (LANES * DIM) + u * DIM, DIM)
                    self.wait(x_done[u])
                    nc.gpsimd.tensor_copy(x_all[:, at], att[u][:, :])

        HSCALE = HDIM ** -0.5

        with nc.Fori(0, BATCH // LANES) as turn:
            with nc.Block() as block:
                @block.gpsimd
                def _(pool):
                    p = PoolStages(pool)
                    p.load(turn)
                    p.expand()
                    p.store(turn)

                @block.tensor
                def _(pe):
                    t = TensorStages(pe)
                    t.norm_transpose()
                    t.lanes(t.project_rope)
                    t.lanes(t.rows_transpose)
                    t.attention(causal_bf)
                    t.lanes(t.output_transpose)
                    t.lanes(t.output_product, "L0_attn_WoT")
                    t.lanes(t.decay)
                    t.norm_transpose()
                    t.lanes(t.butterfly_mlp)
                    t.lanes(t.butterfly_mlp_out)

                @block.vector
                def _(dve):
                    v = VectorStages(dve)
                    v.pad_values()
                    v.lanes(v.first_wait)
                    v.norm()
                    v.lanes(v.rope)
                    v.attention()
                    v.lanes(v.add_result)
                    v.lanes(v.square_context)
                    v.norm()
                    v.lanes(v.retention)
                    v.norm()
                    v.lanes(v.add_result, down_bias[:, :])
                    v.lanes(v.finished)

                @block.scalar
                def _(act):
                    load_tables(EXP_LN)
                    a = ScalarStages(act)
                    a.norm()
                    a.lanes(a.rope_values)
                    a.lanes(a.take_qkT)
                    a.attention(HSCALE)
                    a.lanes(a.take_attT)
                    for u in LANE_RANGE:
                        a.wait(var_ready[u])
                        a.link(nc.scalar.activation(rs[u][:, 2:3], rs[u][:, 0:1], ACT.Ln))
                        nc.scalar.activation(rs[u][:, 1:2], rs[u][:, 2:3], ACT.Exp, scale=-0.5)\
                            .then_inc(rstd_ready[u], 1)
                    a.norm()
                    a.lanes(a.gelu)
            end_of_turn()

        with ExitStack() as scope:
            all_stats = sb("all_stats", [SEQ, BATCH * 6], F32, scope)
            all_mv = sb("all_mv", [SEQ, BATCH * 2], F32, scope)
            all_r = sb("all_r", [SEQ, 4 * BATCH], F32, scope)
            xh = sx[0]
            head_row = sx[1]
            sn, above = kX[0], kX[1]
            ext = sb("ext", [SEQ, 2], F32, scope)
            sc = sb("sc", [1, 32], F32, scope)
            fr = sb("fr", [DIM, 16], F32, scope)
            scaled = sb("scaled", [DIM, DIM], F32, scope)
            block = scope.enter_context(nc.Block())
            mvv = all_mv[:, :].rearrange("p (b t) -> p b t", t=2)
            var, r0, rt, rr = (all_r[:, i * BATCH:(i + 1) * BATCH] for i in range(4))
            n_first = SCALES[-1] ** 2

            @block.sync
            def _(sp):
                sp.wait_ge(xn_ready[0], 1)
                sp.dma_start(head_row[0:1, 0:n_first], xh[0:n_first // DIM, 0:DIM]).then_inc(loaded, 16)
                sp.wait_ge(loaded, 16)

            @block.vector
            def _(dve):
                seen = Seen()
                link = chained(dve, dve_step, seen)
                for b in range(BATCH):
                    last = nc.vector.bn_stats(all_stats[:, b * 6:b * 6 + 6], x_all[:, b * DIM:b * DIM + DIM])
                link(last)
                for b in range(BATCH):
                    last = nc.vector.bn_aggr(all_mv[:, b * 2:b * 2 + 2], all_stats[:, b * 6:b * 6 + 6])
                link(last)
                nc.vector.tensor_scalar(var[:, :, None], mvv[:, :, 1:2], EPS_LN, None, ALU.add).then_inc(var_ready[0], 1)
                dve.wait_ge(rstd_ready[0], 1)
                link(nc.vector.tensor_tensor(rt, var, r0, ALU.mult))
                link(nc.vector.tensor_tensor(rt, rt, r0, ALU.mult))
                link(nc.vector.tensor_scalar(rt, rt, -0.5, 1.5, ALU.mult, ALU.add))
                link(nc.vector.tensor_tensor(rr, r0, rt, ALU.mult))
                xv, xo = (t[:, :].rearrange("p (b d) -> p b d", b=BATCH) for t in (x_all, xh))
                link(nc.vector.tensor_tensor(xo, xv, mvv[:, :, 0:1].to_broadcast([SEQ, BATCH, DIM]), ALU.subtract))
                nc.vector.tensor_tensor(xo, xo, per_head(rr, DIM), ALU.mult).then_inc(xn_ready[0], 1)
                dve.wait_ge(xn_ready[0], 1)
                nc.vector.tensor_reduce(ext[:, 0:1], xh[:, :], AX, ALU.min)
                nc.vector.tensor_reduce(ext[:, 1:2], xh[:, :], AX, ALU.max).then_inc(small_ready[0], 1)
                dve.wait_ge(smallT_psum[0], 1)
                low, span, inv = sc[0:1, 0:1], sc[0:1, 1:2], sc[0:1, 2:3]
                nc.vector.tensor_reduce(low, bankB[0][0:1, 0:128], AX, ALU.min)
                link(nc.vector.tensor_reduce(span, bankB[0][0:1, 128:256], AX, ALU.max))
                link(nc.vector.tensor_tensor(span, span, low, ALU.subtract))
                link(nc.vector.tensor_scalar(span, span, 1e-10, None, ALU.add))
                link(nc.vector.reciprocal(inv, span))
                dve.wait_ge(loaded, 16)
                link(nc.vector.tensor_scalar(sn[0:1, 0:n_first], head_row[0:1, 0:n_first], low, inv, ALU.subtract, ALU.mult))
                for i, s in enumerate(SCALES):
                    n = s * s
                    m, c = sc[0:1, 3:4], sc[0:1, 8 + i:9 + i]
                    link(nc.vector.tensor_reduce(m, sn[0:1, 0:n], AX, ALU.add))
                    link(nc.vector.tensor_scalar(m, m, 1.0 / n, None, ALU.mult))
                    link(nc.vector.tensor_scalar(above[0:1, 0:n], sn[0:1, 0:n], m, None, ALU.is_gt))
                    link(nc.vector.tensor_reduce(c, above[0:1, 0:n], AX, ALU.add))
                nc.vector.tensor_scalar(sc[0:1, 8:13], sc[0:1, 8:13], 1.0, None, ALU.max).then_inc(small_ready[1], 1)
                dve.wait_ge(smallT_ready[1], 1)
                ly, prod = sc[0:1, 13:18], sc[0:1, 18:23]
                nc.vector.tensor_reduce(sc[0:1, 23:24], ly, AX, ALU.add)
                link(nc.vector.tensor_tensor(prod, ly, field("log_scales"), ALU.mult))
                link(nc.vector.tensor_reduce(sc[0:1, 24:25], prod, AX, ALU.add))
                lx = np.log(np.asarray(SCALES, np.float32))
                n = len(SCALES)
                den = float(n * (lx * lx).sum() - lx.sum() ** 2)
                link(nc.vector.tensor_scalar(sc[0:1, 23:24], sc[0:1, 23:24], float(lx.sum()), None, ALU.mult))
                link(nc.vector.tensor_scalar(sc[0:1, 24:25], sc[0:1, 24:25], float(n), None, ALU.mult))
                link(nc.vector.tensor_tensor(sc[0:1, 24:25], sc[0:1, 23:24], sc[0:1, 24:25], ALU.subtract))
                link(nc.vector.tensor_scalar(sc[0:1, 24:25], sc[0:1, 24:25], 1.0 / den, 1.0, ALU.mult, ALU.max))
                nc.vector.tensor_scalar(sc[0:1, 25:26], sc[0:1, 24:25], 2.0, None, ALU.min).then_inc(att_ready[0], 1)
                dve.wait_ge(y_psum[0], 1)
                D, wD, a, b, t, u = (fr[:, i:i + 1] for i in range(6))
                ka, ka2 = field("freq"), field("freq_sq")
                link(nc.vector.tensor_copy(D, bankC[0][:, 0:1]))
                link(nc.vector.tensor_scalar(wD, D, 0.2, 1.0, ALU.mult, ALU.add))
                link(nc.vector.tensor_tensor(wD, wD, D, ALU.mult))
                link(nc.vector.tensor_scalar(a, D, 0.5, 1.0, ALU.mult, ALU.add))
                link(nc.vector.tensor_scalar(b, D, 0.1, None, ALU.mult))
                link(nc.vector.tensor_tensor(t, a, ka, ALU.mult))
                link(nc.vector.tensor_tensor(t, t, wD, ALU.add))
                link(nc.vector.tensor_scalar(fr[:, 6:7], t, -1.0, float(np.pi), ALU.mult, ALU.add))
                link(nc.vector.tensor_tensor(u, b, ka2, ALU.mult))
                link(nc.vector.tensor_tensor(u, u, ka, ALU.subtract))
                link(nc.vector.tensor_tensor(u, u, wD, ALU.add))
                nc.vector.tensor_scalar(fr[:, 7:8], u, -1.0, float(np.pi / 2), ALU.mult, ALU.add)\
                    .then_inc(small_ready[0], 1)
                dve.wait_ge(smallT_ready[0], 1)
                link(nc.vector.tensor_tensor(fr[:, 10:11], fr[:, 8:9], fr[:, 9:10], ALU.mult))
                nc.vector.tensor_scalar(scaled[:, :], field("dft"), fr[:, 10:11], None, ALU.mult).then_inc(qk_ready[0], 1)
                dve.wait_ge(y_psum[0], 2)
                nc.vector.tensor_copy(circ[:, :], bankC[0][:, 128:256])

            @block.scalar
            def _(act):
                link = chained(act, act_step, Seen())
                load_tables(EXP_LN)
                act.wait_ge(var_ready[0], 1)
                link(nc.scalar.activation(rt, var, ACT.Ln))
                nc.scalar.activation(r0, rt, ACT.Exp, scale=-0.5).then_inc(rstd_ready[0], 1)
                act.wait_ge(small_ready[1], 1)
                nc.scalar.activation(sc[0:1, 13:18], sc[0:1, 8:13], ACT.Ln).then_inc(smallT_ready[1], 1)
                act.wait_ge(small_ready[0], 2)
                nc.scalar.activation(fr[:, 8:9], fr[:, 6:7], ACT.Sin)
                nc.scalar.activation(fr[:, 9:10], fr[:, 7:8], ACT.Sin).then_inc(smallT_ready[0], 1)

            @block.tensor
            def _(pe):
                pe.wait_ge(small_ready[0], 1)
                nc.tensor.transpose(bankB[0][0:1, 0:128], ext[:, 0:1], ident)
                nc.tensor.transpose(bankB[0][0:1, 128:256], ext[:, 1:2], ident).then_inc(smallT_psum[0], 1)
                pe.wait_ge(att_ready[0], 1)
                nc.tensor.matmul(bankC[0][:, 0:1], field("ones_row"), sc[0:1, 25:26], start=True, stop=True)\
                    .then_inc(y_psum[0], 1)
                pe.wait_ge(qk_ready[0], 1)
                nc.tensor.matmul(bankC[0][:, 128:256], scaled[:, :], field("dft"), start=True, stop=True)\
                    .then_inc(y_psum[0], 1)
        end_of_turn()

        with nc.Fori(0, BATCH // LANES) as turn:
            with nc.Block() as block:
                @block.gpsimd
                def _(pool):
                    p = PoolStages(pool)
                    p.load(turn)
                    p.expand()
                    p.expand()
                    p.expand()
                    p.expand()
                    p.expand(qT)
                    p.log_differences()

                @block.sync
                def _(sp):
                    for u in LANE_RANGE:
                        sp.wait_ge(bd_ready[u], 4)
                        sp.dma_start(dram["shift"][u].rearrange("h (i c) -> i h c", c=SEQ + 1),
                                     zrel[u][:, :].rearrange("p (h c) -> p h c", h=HEADS)).then_inc(bd_out[u], 16)
                    for u in LANE_RANGE:
                        sp.wait_ge(bd_out[u], 16)
                        sp.dma_start(dshift[u][:, :].rearrange("p (h c) -> p h c", h=HEADS),
                                     dram["shift"][u][:, SEQ:SEQ + SEQ * SEQ].rearrange("h (i c) -> i h c", c=SEQ))\
                            .then_inc(bd_back[u], 16)
                    for u in LANE_RANGE:
                        sp.wait_ge(x_done[u], 1)
                        sp.dma_start(out[bass.ds(turn * LANES + u, 1), :, :].rearrange("b s d -> (b s) d"),
                                     att[u][:, :]).then_inc(stored, 16)
                    sp.wait_ge(stored, 32)

                @block.tensor
                def _(pe):
                    t = TensorStages(pe)
                    t.lanes(t.context_transpose)
                    t.norm_transpose()
                    t.lanes(t.filtered)
                    t.lanes(t.latents)
                    t.lanes(t.code_transpose)
                    t.lanes(t.code_product)
                    t.norm_transpose()
                    t.lanes(t.project, "L1_xattn", ctxT)
                    t.attention(maskadd_bf)
                    t.lanes(t.output_transpose)
                    t.lanes(t.output_product, "L1_xattn_WoT")
                    t.norm_transpose()
                    t.lanes(t.router, "L1_ffn_Wg")
                    t.lanes(t.linear_experts, "L1_ffn_WeT")
                    t.lanes(t.gate_transpose)
                    t.lanes(t.gate_bias, "L1_ffn_be")
                    t.norm_transpose()
                    t.lanes(t.project, "L2_attn", xnT)
                    t.position_scores()
                    t.attention(None, True)
                    t.lanes(t.attention_taken)
                    t.norm_transpose()
                    t.lanes(t.project, "L2_xattn", ctxT)
                    t.attention()
                    t.lanes(t.attention_taken)
                    t.norm_transpose()
                    t.lanes(t.router, "L2_ffn_W_gate")
                    t.lanes(t.project, "L2_ffn", xnT)
                    t.attention()
                    t.lanes(t.attention_taken)
                    t.lanes(t.linear_experts, "L2_ffn_W_experts")
                    t.lanes(t.gate_transpose)
                    t.lanes(t.gate_bias, "L2_ffn_b_experts")
                    t.norm_transpose()
                    t.lanes(t.project_rows)
                    t.lanes(t.rows_transpose)
                    for half in range(2):
                        for u in LANE_RANGE:
                            t.scores(u, half, None, kT)
                    t.lanes(t.weighted_values, sx)
                    t.lanes(t.values_transpose)
                    t.lanes(t.output_transpose)
                    t.lanes(t.output_product, "L3_attn_w_outT")
                    t.norm_transpose()
                    t.lanes(t.project, "L3_xattn", ctxT)
                    t.lanes(t.single_scores)
                    t.lanes(t.single_transpose)
                    t.lanes(t.single_values)
                    t.norm_transpose()
                    t.lanes(t.router, "L3_ffn_W_router")
                    t.lanes(t.mlp_hidden, 0)
                    t.lanes(t.gate_transpose)
                    t.lanes(t.gate_bias, "L3_ffn_b2")
                    for e in range(EXPERTS):
                        if e + 1 < EXPERTS:
                            t.lanes(t.mlp_hidden, e + 1)
                        t.lanes(t.mlp_out, e)

                @block.vector
                def _(dve):
                    v = VectorStages(dve)
                    v.pad_values()
                    v.lanes(v.first_wait)
                    v.norm()
                    v.lanes(v.code_bits)
                    v.lanes(v.add_result, field("L1_attn_b_le"))
                    v.norm()
                    v.lanes(v.take_projection, "bias", "L1_xattn")
                    v.attention()
                    v.lanes(v.add_result, field("L1_xattn_bo"))
                    v.norm()
                    v.lanes(v.gates_start, "L1_ffn_bg")
                    v.lanes(v.gates_finish, True)
                    v.lanes(v.add_linear_experts)
                    v.lanes(v.add_result, None, bankB)
                    v.norm()
                    v.lanes(v.take_projection, "relative")
                    v.position_scores()
                    v.attention(True)
                    v.lanes(v.add_attention)
                    v.norm()
                    v.lanes(v.take_projection, "relu")
                    v.attention()
                    v.lanes(v.add_attention)
                    v.norm()
                    v.lanes(v.gates_start, "L2_ffn_b_gate")
                    v.lanes(v.take_projection, "bias", "L2_ffn")
                    v.attention()
                    v.lanes(v.add_attention)
                    v.lanes(v.gates_finish, False)
                    v.lanes(v.add_linear_experts)
                    v.lanes(v.add_result, None, bankB)
                    v.norm()
                    v.lanes(v.unit_rows)
                    v.lanes(v.unit_apply)
                    for half in range(2):
                        v.lanes(v.clip_cosines, half)
                    v.lanes(v.column_sums)
                    v.lanes(v.manifold_normalise)
                    v.lanes(v.add_result, field("L3_attn_b_out"))
                    v.norm()
                    v.lanes(v.take_single)
                    v.lanes(v.single_max)
                    v.lanes(v.single_result)
                    v.norm()
                    v.lanes(v.gates_start, "L3_ffn_b_router")
                    v.lanes(v.gates_finish, True)
                    v.lanes(v.add_result, None, bankB)
                    v.lanes(v.mlp_hidden, 0)
                    for e in range(EXPERTS):
                        if e + 1 < EXPERTS:
                            v.lanes(v.mlp_hidden, e + 1)
                        v.lanes(v.mlp_out, e)
                    v.lanes(v.finished)

                @block.scalar
                def _(act):
                    load_tables(EXP_LN)
                    a = ScalarStages(act)
                    a.lanes(a.context)
                    a.norm()
                    a.lanes(a.take_attT)
                    a.lanes(a.take_small, CODE)
                    a.norm()
                    a.attention(HSCALE)
                    a.lanes(a.take_attT)
                    a.norm()
                    a.lanes(a.gates)
                    a.lanes(a.skip_hidden)
                    a.lanes(a.take_small, EXPERTS)
                    a.norm()
                    a.position_scores()
                    a.attention(HSCALE)
                    a.norm()
                    a.attention(HSCALE)
                    a.norm()
                    a.lanes(a.gates)
                    a.attention(HSCALE)
                    a.lanes(a.skip_hidden)
                    a.lanes(a.take_small, EXPERTS)
                    a.norm()
                    a.lanes(a.unit_norms)
                    a.lanes(a.take_qkT)
                    a.lanes(a.cosine_logs)
                    load_tables(TANH_ARCTAN)
                    a.lanes(a.angles)
                    load_tables(EXP_LN)
                    a.lanes(a.kernel_values)
                    a.lanes(a.take_values)
                    a.lanes(a.take_attT)
                    a.norm()
                    a.lanes(a.single_exp)
                    a.lanes(a.take_attT)
                    a.norm()
                    a.lanes(a.gates)
                    a.lanes(a.take_small, EXPERTS)
                    a.lanes(a.mlp_hidden, 0)
                    for e in range(EXPERTS):
                        if e + 1 < EXPERTS:
                            a.lanes(a.mlp_hidden, e + 1)
            end_of_turn()


def rope_tables():
    freq = 1.0 / 10000.0 ** (np.arange(0, HDIM, 2, dtype=np.float32) / HDIM)
    angle = np.outer(np.arange(SEQ, dtype=np.float32), freq.astype(np.float32))
    emb = np.concatenate([angle, angle], -1).astype(np.float32)
    sign = np.where(np.arange(HDIM) < HDIM // 2, -1.0, 1.0)
    cos, sin = np.cos(emb), np.sin(emb) * sign
    return np.tile(cos, (1, 2 * HEADS)), np.tile(sin, (1, 2 * HEADS))


def position_table():
    freq = (1.0 / 10000.0 ** (np.arange(0, DIM, 2, dtype=np.float32) / DIM)).astype(np.float32)
    pos = np.arange(-(SEQ - 1), SEQ, dtype=np.float32)
    angle = (pos[:, None] * freq[None, :]).astype(np.float32)
    emb = np.zeros((2 * SEQ - 1, DIM), np.float32)
    emb[:, 0::2], emb[:, 1::2] = np.sin(angle), np.cos(angle)
    return emb


def fourier_basis():
    n, rows, freq = np.arange(DIM), [np.full(DIM, DIM ** -0.5)], [0]
    for k in range(1, DIM // 2):
        rows += [np.cos(2 * np.pi * k * n / DIM) * (2 / DIM) ** 0.5, np.sin(2 * np.pi * k * n / DIM) * (2 / DIM) ** 0.5]
        freq += [k, k]
    rows.append((1 - 2 * (n % 2)) * DIM ** -0.5)
    freq.append(DIM // 2)
    ka = (np.asarray(freq, np.float32) / np.float32(DIM)) + np.float32(1e-8)
    return np.asarray(rows), ka.astype(np.float32)


GOLAY_A = ["111011100011", "110111000110", "101110001101", "011100011011", "000011111111", "111100000000",
           "000011110000", "110011001100", "101010101010", "010101010101", "100110011001", "011001100110"]


def constants():
    cos, sin = rope_tables()
    basis, ka = fourier_basis()
    i, j = np.arange(SEQ)[:, None], np.arange(SEQ)[None, :]
    t = np.arange(SEQ)
    a = np.array([[int(c) for c in row] for row in GOLAY_A], np.float32)
    parity = np.concatenate([a.T, np.eye(DATA)], axis=1)
    return {
        "ident": np.eye(128),
        "head_mask": (np.arange(DIM)[:, None] // HDIM == np.arange(HEADS)[None, :]),
        "ones_row": np.ones((1, 128)),
        "ones": np.ones((128, 1)),
        "one_half_pi": np.full((128, 1), 1 + np.pi / 2),
        "rope_cos": cos, "rope_sin": sin,
        "causal": np.where(j <= i, 0.0, MASKED),
        "decay": np.where(t[None, :] >= t[:, None], 0.9 ** np.maximum(t[None, :] - t[:, None], 0), 0.0),
        "sin_rpe": position_table().T,
        "rel_select": (j >= SEQ - 1 - i),
        "dft": basis,
        "freq": ka[:, None], "freq_sq": (ka * ka)[:, None],
        "log_scales": np.log(np.asarray(SCALES, np.float32))[None, :],
        "golay": np.broadcast_to(parity.reshape(1, -1), (SEQ, DATA * CODE)),
        "iota8": np.broadcast_to(np.arange(EXPERTS)[None, :], (SEQ, EXPERTS)),
    }


def lay_out(w):
    def rows(v):
        return np.broadcast_to(np.asarray(v).reshape(1, -1), (128, np.asarray(v).size))

    def column(v):
        return np.asarray(v).reshape(-1, 1)

    qkv0 = np.asarray(w["L0_attn_W_qkv"])
    swap = np.arange(DIM).reshape(HEADS, 2, HDIM // 2)[:, ::-1].reshape(-1)
    q0, k0, v0 = qkv0[0:128], qkv0[128:256], qkv0[256:384]
    first = {
        "L0_attn_WqksT": np.concatenate([q0, k0, q0[swap], k0[swap]], 0).T,
        "L0_attn_WvT": v0.T, "L0_attn_WoT": w["L0_attn_W_out"].T,
        "L0_ffn_W_exp": w["L0_ffn_W_exp"], "L0_ffn_W_conT": w["L0_ffn_W_con"].T,
        "L0_ffn_b_exp": w["L0_ffn_b_exp"].reshape(1, -1),
        "L0_ffn_up_bias": w["L0_ffn_up_bias"].reshape(4, 128).T,
        "L0_ffn_b_con": rows(w["L0_ffn_b_con"]), "L0_ffn_down_bias": rows(w["L0_ffn_down_bias"]),
    }
    qkv2, b2 = w["L2_ffn_W_qkv"], w["L2_ffn_b_qkv"]
    later = {
        "L1_attn_W_el": w["L1_attn_W_el"], "L1_attn_b_el": rows(w["L1_attn_b_el"]),
        "L1_attn_W_le": w["L1_attn_W_le"], "L1_attn_b_le": rows(w["L1_attn_b_le"]),
        "L1_xattn_WqT": w["L1_xattn_Wq"].T, "L1_xattn_WkT": w["L1_xattn_Wk"].T, "L1_xattn_WvT": w["L1_xattn_Wv"].T,
        "L1_xattn_WoT": w["L1_xattn_Wo"].T, "L1_xattn_bq": column(w["L1_xattn_bq"]),
        "L1_xattn_bk": column(w["L1_xattn_bk"]), "L1_xattn_bv": rows(w["L1_xattn_bv"]),
        "L1_xattn_bo": rows(w["L1_xattn_bo"]),
        "L1_ffn_Wg": w["L1_ffn_Wg"], "L1_ffn_bg": rows(w["L1_ffn_bg"]), "L1_ffn_be": w["L1_ffn_be"],
        "L1_ffn_WeT": w["L1_ffn_We"].transpose(2, 0, 1).reshape(DIM, -1),
        "L2_attn_WqT": w["L2_attn_Wq"].T, "L2_attn_WkT": w["L2_attn_Wk"].T, "L2_attn_WvT": w["L2_attn_Wv"].T,
        "L2_attn_WrT": w["L2_attn_Wr"].T,
        "L2_attn_u_bias": column(w["L2_attn_u_bias"]), "L2_attn_v_bias": column(w["L2_attn_v_bias"]),
        "L2_xattn_WqT": w["L2_xattn_Wq"].T, "L2_xattn_WkT": w["L2_xattn_Wk"].T, "L2_xattn_WvT": w["L2_xattn_Wv"].T,
        "L2_ffn_WqT": qkv2[:, 0:128], "L2_ffn_WkT": qkv2[:, 128:256], "L2_ffn_WvT": qkv2[:, 256:384],
        "L2_ffn_bq": column(b2[0:128]), "L2_ffn_bk": column(b2[128:256]), "L2_ffn_bv": rows(b2[256:384]),
        "L2_ffn_W_gate": w["L2_ffn_W_gate"], "L2_ffn_b_gate": rows(w["L2_ffn_b_gate"]),
        "L2_ffn_W_experts": w["L2_ffn_W_experts"].transpose(1, 0, 2).reshape(DIM, -1),
        "L2_ffn_b_experts": w["L2_ffn_b_experts"],
        "L3_attn_w_qkvT": w["L3_attn_w_qkv"].T, "L3_attn_b_qkv": rows(w["L3_attn_b_qkv"]),
        "L3_attn_w_outT": w["L3_attn_w_out"].T, "L3_attn_b_out": rows(w["L3_attn_b_out"]),
        "L3_xattn_WqT": w["L3_xattn_Wq"], "L3_xattn_WkT": w["L3_xattn_Wk"], "L3_xattn_WvT": w["L3_xattn_Wv"],
        "L3_xattn_bq": column(w["L3_xattn_bq"]), "L3_xattn_bk": column(w["L3_xattn_bk"]),
        "L3_xattn_bv": rows(w["L3_xattn_bv"]),
        "L3_ffn_W_router": w["L3_ffn_W_router"], "L3_ffn_b_router": rows(w["L3_ffn_b_router"]),
        "L3_ffn_W1": w["L3_ffn_W1"].transpose(1, 0, 2).reshape(DIM, -1),
        "L3_ffn_b1": w["L3_ffn_b1"].reshape(EXPERTS * 4, 128).T,
        "L3_ffn_W2": w["L3_ffn_W2"].reshape(EXPERTS, 4, 128, DIM).transpose(2, 0, 1, 3).reshape(128, -1),
        "L3_ffn_b2": w["L3_ffn_b2"],
    }
    return first, later


def side_by_side(fields):
    where, at = {}, 0
    for name, a in fields.items():
        where[name] = (at, a.shape[1], a.shape[0])
        at += a.shape[1]
    packed = np.zeros((128, at), np.float32)
    for name, a in fields.items():
        c, n, r = where[name]
        packed[0:r, c:c + n] = a
    return packed, where


def butterfly_rows(up, down):
    parts = []
    for weights, backwards in ((up, False), (down, True)):
        for s in (range(STAGES0 - 1, -1, -1) if backwards else range(STAGES0)):
            w = weights[s].reshape(HIDDEN0 // (2 * 2 ** s), 2 ** s, 2, 2)
            off = (w[..., 1, 0], w[..., 0, 1]) if backwards else (w[..., 0, 1], w[..., 1, 0])
            parts += [np.stack([w[..., 0, 0], w[..., 1, 1]], 1).reshape(-1), np.stack(off, 1).reshape(-1)]
    return np.concatenate(parts).reshape(1, -1)


def kernel(**inputs):
    import concourse.bacc as bacc
    from concourse.bass_utils import run_bass_kernel_spmd

    w = {k: np.asarray(v) for k, v in inputs.items()}
    first, later = lay_out(w)
    packs = {"first": side_by_side({**constants(), **first}), "later": side_by_side(later)}
    arrays = {
        "first": packs["first"][0], "later": packs["later"][0],
        "butterfly": np.ascontiguousarray(butterfly_rows(w["L0_ffn_up_weights"], w["L0_ffn_down_weights"])),
        "mask": np.ascontiguousarray(w["mask_1xSxS2_if1"][0]),
        "x": np.ascontiguousarray(w["x"]), "ctx": np.ascontiguousarray(w["ctx_1024"]),
    }
    nc = bacc.Bacc("TRN2", target_bir_lowering=False, num_devices=1)
    dram = {n: nc.dram_tensor(f"in_{n}", a.shape, mybir.dt.from_np(a.dtype), kind="ExternalInput").ap()
            for n, a in arrays.items()}
    dram["shift"] = [nc.dram_tensor(f"shift_{u}", (HEADS, SEQ * (SEQ + 1)), F32, kind="Internal").ap()
                     for u in LANE_RANGE]
    out = nc.dram_tensor("out_0", (BATCH, SEQ, DIM), F32, kind="ExternalOutput").ap()
    decoder_program(nc, dram, {n: p[1] for n, p in packs.items()}, out)
    r = run_bass_kernel_spmd(nc, [{f"in_{n}": a for n, a in arrays.items()}], core_ids=[0])
    return r.results[0]["out_0"]
```

```python
from contextlib import ExitStack

import numpy as np

import concourse.bass as bass
from concourse import mybir

F32 = mybir.dt.float32
BF16 = mybir.dt.bfloat16
I32 = mybir.dt.int32
U32 = mybir.dt.uint32
ALU = mybir.AluOpType
ACT = mybir.ActivationFunctionType
AX = mybir.AxisListType.X

BATCH, SEQ, DIM = 16, 128, 128
HEADS = 16
HDIM = DIM // HEADS
LANES = 2
ROUNDS = 2
TURNS = BATCH // (LANES * ROUNDS)
HALF = HEADS // 2 * SEQ
QUARTER = HALF // 2
VPAD = 32
HIDDEN0 = 512
STAGES0 = 9
EXPERTS = 8
FF3 = 512
CODE, DATA = 24, 12
EPS_LN = 1e-5
MASKED = -float(2 ** 100)
CLIP = 1.0 - 1e-7
SCALES = (2, 4, 8, 16, 32)
LN_SHIFT = 2.0 ** 30
LANE_RANGE = range(LANES)
EXP_LN, TANH_ARCTAN = "natural_log_exp_and_others", "sigmoid_and_others"


ORDER_FIRST = {
    "gpsimd":
        "01000111001100101101",
    "tensor":
        "010101010000101010000100110110110111011100101110001010100100001100001110100110111101110100110101",
    "vector":
        "000011010101110011010001101100000000011000001011010011111110111110000000101011111110100110010011"
        "11000011000010101101001010100011111111000111",
    "scalar":
        "01010100110000100100101110111010101001110100110000101000110101011110110100110110",
}
ORDER_OTHERS = {
    "gpsimd":
        "010010110110010011100001110000111100001101111001100001110001110000111101",
    "sync":
        "00000100011111110000000011111111",
    "tensor":
        "100101010101010100010100100001000110110110101111001010001111001010111001001011001000010101001101"
        "101111011000100100110000001011111011010011001010100100000101011010011011111010111101010001111100"
        "000000000110110101001101010100110000110000000001011010101011111011101101111000101001010000010011"
        "001011010110111101101101110001111101010110001000010010000110101111110111010100100010100010010111"
        "111010110011001011010000100001011001110011111010111101010001111100000000000110110101001100111001"
        "010001010010000101001111111111111111",
    "vector":
        "010001010011111000010110110101010100001000101011111100010111000000000100100000001010010101010100"
        "001011011110110101111111011111101110100100001010001011111110100000000011111110111000110000010010"
        "000000001010010111011101101011111111110001000000100000000011010101010101010110110110111001111101"
        "111101001011111000000010000000000000111111000000010010101110001111111100000000011011111011110011"
        "001000000010101011100011101000000110001110001011000101101110111100111011111111111110011100000001"
        "000100010000010000000110000001011111101011111111111111111111111100011000000001011101001001010011"
        "011001111110110110110000010010000000000010110111011101110101111111110001000000100000000011100101"
        "011010101001110101111001111101101111000111101000001001000000000000111111000000010011001110001111"
        "111100000000110011111011110001110000011011111011111111111111",
    "scalar":
        "010011010101010010100000010110111011010011010101011100010101010000010101111101100101010000001011"
        "011101100110100000011001110111101100110110010001101010100001001001110011110001100010101011001011"
        "010100000010101100101111111100101110110100100001000011001101111101101010000101000111011110100110"
        "101100000001111101101101010110100001101010100001000110111001110100111111",
}


class Seen:

    def __init__(self):
        self.count = {}

    def next(self, sem, step=1):
        self.count[sem.num] = self.count.get(sem.num, 0) + step
        return self.count[sem.num]


def interleave(order, programs):
    for lane in order:
        next(programs[int(lane)])
    for program in programs:
        for _ in program:
            pass


def decoder_program(nc, dram, cols, out):
    with ExitStack() as whole:
        stored = whole.enter_context(nc.semaphore("stored"))
        sems = []

        def sem(name):
            s = whole.enter_context(nc.semaphore(name))
            sems.append(s)
            return s

        def lane_sems(name):
            return [sem(f"{name}{u}") for u in LANE_RANGE]

        def sb(name, shape, dt=F32, scope=whole):
            return scope.enter_context(nc.sbuf_tensor(name, shape, dt))

        loaded = sem("loaded")
        weights_in = sem("weights_in")
        parts_ready = sem("parts_ready")
        part_rows_in = sem("part_rows_in")
        loaded_later = sem("loaded_later")
        x_kept = lane_sems("x_kept")
        dve_step, act_step, pool_step = sem("dve_step"), sem("act_step"), sem("pool_step")
        prep = sem("prep")
        prep_taken = sem("prep_taken")
        prep_act = sem("prep_act")
        prep_row = sem("prep_row")
        x_in = lane_sems("x_in")
        x_done = lane_sems("x_done")
        var_ready = lane_sems("var_ready")
        rstd_ready = lane_sems("rstd_ready")
        xn_ready = lane_sems("xn_ready")
        xnT_psum = lane_sems("xnT_psum")
        xnT_ready = lane_sems("xnT_ready")
        ctxT_psum = lane_sems("ctxT_psum")
        ctxT_ready = lane_sems("ctxT_ready")
        proj_psum = lane_sems("proj_psum")
        qk_ready = lane_sems("qk_ready")
        qkT_psum = lane_sems("qkT_psum")
        q_psum = lane_sems("q_psum")
        k_psum = lane_sems("k_psum")
        v_psum = lane_sems("v_psum")
        left_ready = lane_sems("left_ready")
        right_ready = lane_sems("right_ready")
        v_ready = lane_sems("v_ready")
        expanded_first = lane_sems("expanded_first")
        expanded = lane_sems("expanded")
        bd_psum = lane_sems("bd_psum")
        bd_low = lane_sems("bd_low")
        bd_ready = lane_sems("bd_ready")
        bd_out = [[sem(f"bd_out{u}_{c}") for c in range(4)] for u in LANE_RANGE]
        bd_back = [[sem(f"bd_back{u}_{c}") for c in range(4)] for u in LANE_RANGE]
        scores_psum = lane_sems("scores_psum")
        max_ready = lane_sems("max_ready")
        scores_taken = lane_sems("scores_taken")
        probs_ready = lane_sems("probs_ready")
        pT_psum = lane_sems("pT_psum")
        pT_ready = lane_sems("pT_ready")
        oT_psum = lane_sems("oT_psum")
        oT_ready = lane_sems("oT_ready")
        o_psum = lane_sems("o_psum")
        att_ready = lane_sems("att_ready")
        attT_psum = lane_sems("attT_psum")
        attT_ready = lane_sems("attT_ready")
        y_psum = lane_sems("y_psum")
        gate_psum = lane_sems("gate_psum")
        gate_max = lane_sems("gate_max")
        gate_exp = lane_sems("gate_exp")
        small_ready = lane_sems("small_ready")
        smallT_psum = lane_sems("smallT_psum")
        smallT_ready = lane_sems("smallT_ready")
        h_psum = lane_sems("h_psum")
        h_ready = lane_sems("h_ready")
        h_odd_ready = lane_sems("h_odd_ready")
        y_taken = lane_sems("y_taken")
        logs_ready = lane_sems("logs_ready")
        kernel_ready = lane_sems("kernel_ready")
        logs_diff = lane_sems("logs_diff")
        logs_diff_high = lane_sems("logs_diff_high")

        pack = {n: sb(n, [128, dram[n].shape[1]]) for n in ("first", "later")}
        x_all = sb("x_all", [SEQ, BATCH * DIM])
        ctx_all = sb("ctx_all", [SEQ, BATCH * DIM])
        causal_bf = sb("causal_bf", [SEQ, 4, SEQ], BF16)
        maskadd_bf = sb("maskadd_bf", [SEQ, 4, SEQ], BF16)
        ident_bf = sb("ident_bf", [128, 128], BF16)
        w_up = sb("w_up", [DIM, HIDDEN0])
        w_down = sb("w_down", [128, HIDDEN0])
        up_bias = sb("up_bias", [128, 4])
        down_bias = sb("down_bias", [128, DIM])
        circ = sb("circ", [DIM, DIM])
        rel_low = sb("rel_low", [DIM, HEADS * SEQ])
        rel_high = sb("rel_high", [DIM, HEADS * SEQ])
        sel_int = sb("sel_int", [SEQ, SEQ], I32)

        bigA = [whole.enter_context(nc.psum_tensor(f"bigA{u}", [128, 1024], F32)) for u in LANE_RANGE]
        bankB = [whole.enter_context(nc.psum_tensor(f"bankB{u}", [128, 512], F32)) for u in LANE_RANGE]
        bankC = [whole.enter_context(nc.psum_tensor(f"bankC{u}", [128, 512], F32)) for u in LANE_RANGE]

        def field(name):
            for p in ("first", "later"):
                if name in cols[p]:
                    a, n, rows = cols[p][name]
                    return pack[p][0:rows, a:a + n]
            raise KeyError(name)

        ident = field("ident")
        head_mask = field("head_mask")

        HSCALE = HDIM ** -0.5
        Q_BIASES = ("L1_xattn_bq", "L2_attn_u_bias", "L2_attn_v_bias", "L2_ffn_bq")
        q_biases = sb("q_biases", [DIM, len(Q_BIASES)])

        def q_bias(name):
            i = Q_BIASES.index(name)
            return q_biases[:, i:i + 1]

        def end_of_turn():
            nums = [s.num for s in sems]
            nc.gpsimd.sem_clear(range(min(nums), max(nums) + 1))
            nc.all_engine_barrier()

        def over_heads(t, n=HEADS):
            t = t[:, :]
            return t[:, None, :].to_broadcast([128, n, t.shape[1]])

        def per_head(t, inner=SEQ):
            return t[:, :, None].to_broadcast([128, t.shape[1], inner])

        with ExitStack() as scope, nc.Block() as block:
            n_weights = 2 * STAGES0 * 2 * HIDDEN0
            rows = sb("rows", [1, n_weights // 2], F32, scope)
            spread = sb("spread", [128, n_weights // 128], F32, scope)
            rest = sb("rest", [128, n_weights // 128], F32, scope)
            parts = [sb(f"part{i}", [128, n_weights // 128], BF16, scope) for i in range(3)]
            part_rows = sb("part_rows", [3, n_weights], BF16, scope)
            ones3 = sb("ones3", [3, 128], BF16, scope)
            wide = [sb(f"wide{i}", [DIM, HIDDEN0], F32, scope) for i in range(2)]
            wide_t = sb("wide_t", [DIM, HIDDEN0], F32, scope)
            wide_s = sb("wide_s", [DIM, HIDDEN0], F32, scope)
            brow = [sb(f"brow{i}", [1, HIDDEN0], F32, scope) for i in range(2)]
            brow_t = sb("brow_t", [1, HIDDEN0], F32, scope)
            brow_s = sb("brow_s", [1, HIDDEN0], F32, scope)
            mask_raw = sb("mask_raw", [SEQ, SEQ], I32, scope)
            mask_f = sb("mask_f", [SEQ, SEQ], F32, scope)
            relT = sb("relT", [DIM, 2 * SEQ - 1], F32, scope)
            NS = 2 * STAGES0

            @block.sync
            def _(sp):
                sp.dma_start(spread[:, :], dram["butterfly"][0, :].rearrange("(p n) -> p n", p=128))\
                    .then_inc(weights_in, 16)
                sp.dma_start(pack["first"][:, :], dram["first"]).then_inc(loaded, 16)
                sp.dma_start(rows[:, :], dram["butterfly"][:, 0:n_weights // 2]).then_inc(loaded, 16)
                sp.dma_start(mask_raw[:, :], dram["mask"]).then_inc(loaded_later, 16)
                sp.wait_ge(part_rows_in, 48)
                sp.dma_start(x_all[:, :].rearrange("s (b d) -> s b d", b=BATCH),
                             dram["x"].rearrange("b s d -> s b d")).then_inc(loaded_later, 16)
                sp.dma_start(ctx_all[:, :].rearrange("s (b d) -> s b d", b=BATCH),
                             dram["ctx"].rearrange("b s d -> s b d")).then_inc(loaded_later, 16)
                sp.dma_start(pack["later"][:, :], dram["later"]).then_inc(loaded_later, 16)
                sp.wait_ge(loaded_later, 64)

            @block.scalar
            def _(act):
                act.wait_ge(parts_ready, 1)
                for i in range(3):
                    act.dma_start(part_rows[i:i + 1, :].rearrange("o (p n) -> o p n", p=128),
                                  parts[i][:, :]).then_inc(part_rows_in, 16)
                act.wait_ge(part_rows_in, 48)

            @block.tensor
            def _(pe):
                seen = Seen()
                pe.wait_ge(loaded, 32)
                pe.wait_ge(part_rows_in, 48)
                for s in range(NS):
                    if s >= 2:
                        pe.wait_ge(prep_taken, s - 1)
                    for k in range(2):
                        a = s * 2 * HIDDEN0 + k * HIDDEN0
                        last = nc.tensor.matmul(bigA[s % 2][:, k * 512:k * 512 + 512], ones3[:, :],
                                                part_rows[:, a:a + HIDDEN0], start=True, stop=True)
                    last.then_inc(prep, 1)
                pe.wait_ge(prep_taken, NS)
                for c in range(4):
                    last = nc.tensor.transpose(bankB[0][:, c * 128:c * 128 + 128],
                                               wide[NS % 2][:, c * 128:c * 128 + 128], ident)
                last.then_inc(prep, 1)
                pe.wait_ge(prep_row, 1)
                for c in range(4):
                    last = nc.tensor.matmul(bankC[0][:, c:c + 1], brow[STAGES0 % 2][0:1, c * 128:c * 128 + 128],
                                            ident[0:1, 0:1], start=True, stop=True)
                last.then_inc(prep, 1)
                pe.wait_ge(loaded_later, 64)
                nc.tensor.matmul(bankC[1][:, 0:2 * SEQ - 1], field("L2_attn_WrT"), field("sin_rpe"),
                                 start=True, stop=True).then_inc(prep, 1)

            @block.vector
            def _(dve):
                seen = Seen()

                def link(ins):
                    ins.then_inc(dve_step, 1)
                    dve.wait_ge(dve_step, seen.next(dve_step))

                nc.vector.memset(ones3[:, :], 1.0)
                dve.wait_ge(weights_in, 16)
                link(nc.vector.tensor_copy(parts[0][:, :], spread[:, :]))
                link(nc.vector.tensor_tensor(rest[:, :], spread[:, :], parts[0][:, :], ALU.subtract))
                link(nc.vector.tensor_copy(parts[1][:, :], rest[:, :]))
                link(nc.vector.tensor_tensor(rest[:, :], rest[:, :], parts[1][:, :], ALU.subtract))
                nc.vector.tensor_copy(parts[2][:, :], rest[:, :]).then_inc(parts_ready, 1)
                dve.wait_ge(loaded, 32)
                nc.vector.tensor_copy(ident_bf[:, :], ident)
                nc.vector.tensor_copy(causal_bf[:, :, :], over_heads(field("causal"), 4))
                nc.vector.tensor_copy(sel_int[:, :], field("rel_select"))
                nc.vector.tensor_tensor(down_bias[:, :], field("L0_ffn_b_con"), field("L0_ffn_down_bias"), ALU.add)
                for s in range(NS):
                    first = s % STAGES0 == 0
                    stage = s if s < STAGES0 else NS - 1 - s
                    w = 2 ** stage
                    src = (field("L0_ffn_W_exp") if s < STAGES0 else field("L0_ffn_W_conT")) if first \
                        else wide[s % 2][:, :]
                    dst = w_up[:, :] if s == STAGES0 - 1 else wide[(s + 1) % 2][:, :]

                    def pairs(t):
                        return t.rearrange("p (n j s) -> p n j s", j=2, s=w)

                    dve.wait_ge(prep, s + 1)
                    diag, off = bigA[s % 2][:, 0:512], bigA[s % 2][:, 512:1024]
                    nc.vector.tensor_tensor(wide_t[:, :], src, diag, ALU.mult)
                    for j in range(2):
                        last = nc.vector.tensor_tensor(pairs(wide_s[:, :])[:, :, j, :], pairs(src)[:, :, 1 - j, :],
                                                       pairs(off)[:, :, j, :], ALU.mult)
                    link(last)
                    nc.vector.tensor_tensor(dst, wide_t[:, :], wide_s[:, :], ALU.add).then_inc(prep_taken, 1)
                    dve.wait_ge(prep_taken, s + 1)
                dve.wait_ge(prep, NS + 1)
                nc.vector.tensor_copy(w_down[:, :], bankB[0][:, :])
                dve.wait_ge(prep, NS + 2)
                nc.vector.tensor_tensor(up_bias[:, :], bankC[0][:, 0:4], field("L0_ffn_up_bias"), ALU.add)
                dve.wait_ge(loaded_later, 64)
                for name in Q_BIASES:
                    nc.vector.tensor_scalar(q_bias(name), field(name), HSCALE, None, ALU.mult)
                link(nc.vector.tensor_scalar(mask_f[:, :], mask_raw[:, :], 0.0, MASKED, ALU.is_equal, ALU.mult))
                nc.vector.tensor_copy(maskadd_bf[:, :, :], over_heads(mask_f, 4))
                dve.wait_ge(prep, NS + 3)
                link(nc.vector.tensor_copy(relT[:, :], bankC[1][:, 0:2 * SEQ - 1]))
                for dst, a in ((rel_low, 0), (rel_high, SEQ - 1)):
                    nc.vector.tensor_tensor(dst[:, :].rearrange("p (h k) -> p h k", h=HEADS),
                                            over_heads(relT[:, a:a + SEQ]), per_head(head_mask), ALU.mult)

            @block.gpsimd
            def _(pool):
                seen = Seen()
                pool.wait_ge(loaded, 32)
                for s in range(STAGES0):
                    w = 2 ** s
                    src = field("L0_ffn_b_exp") if s == 0 else brow[s % 2][:, :]
                    diag = rows[0:1, s * 1024:s * 1024 + 512]
                    off = rows[0:1, s * 1024 + 512:s * 1024 + 1024]

                    def pairs(t):
                        return t.rearrange("p (n j s) -> p n j s", j=2, s=w)

                    nc.gpsimd.tensor_tensor(brow_t[:, :], src, diag, ALU.mult)
                    for j in range(2):
                        last = nc.gpsimd.tensor_tensor(pairs(brow_s[:, :])[:, :, j, :], pairs(src)[:, :, 1 - j, :],
                                                       pairs(off)[:, :, j, :], ALU.mult)
                    last.then_inc(pool_step, 1)
                    pool.wait_ge(pool_step, seen.next(pool_step))
                    last = nc.gpsimd.tensor_tensor(brow[(s + 1) % 2][:, :], brow_t[:, :], brow_s[:, :], ALU.add)
                    last.then_inc(pool_step, 1)
                    pool.wait_ge(pool_step, seen.next(pool_step))
                nc.gpsimd.tensor_copy(brow_t[:, :], brow[STAGES0 % 2][:, :]).then_inc(prep_row, 1)
        end_of_turn()

        def lane_sb(name, shape, dt=F32):
            return [sb(f"{name}{u}", shape, dt) for u in LANE_RANGE]

        x = lane_sb("x", [SEQ, DIM])
        xn = lane_sb("xn", [SEQ, DIM])
        xnT = lane_sb("xnT", [DIM, SEQ])
        ctx = lane_sb("ctx", [SEQ, DIM])
        ctxT = lane_sb("ctxT", [DIM, SEQ])
        left = lane_sb("left", [DIM, SEQ])
        right = lane_sb("right", [DIM, SEQ])
        qvT = lane_sb("qvT", [DIM, SEQ])
        tok = lane_sb("tok", [SEQ, 512])
        kX = lane_sb("kX", [DIM, HEADS * SEQ])
        sx = lane_sb("sx", [SEQ, HEADS * SEQ])
        pT = lane_sb("pT", [SEQ, HEADS * SEQ])
        zrel = lane_sb("zrel", [SEQ, HEADS * (SEQ + 1)])
        v32 = lane_sb("v32", [SEQ, HEADS, VPAD])
        oT = lane_sb("oT", [128, 512])
        att = lane_sb("att", [SEQ, DIM])
        attT = lane_sb("attT", [DIM, SEQ])
        stats = lane_sb("stats", [SEQ, 6])
        mv = lane_sb("mv", [SEQ, 2])
        rs = lane_sb("rs", [SEQ, 8])
        nmax = lane_sb("nmax", [SEQ, HEADS])
        hs = lane_sb("hs", [SEQ, 4 * HEADS])
        gate = lane_sb("gate", [SEQ, 64])
        gidx = lane_sb("gidx", [SEQ, 8], U32)
        gT = lane_sb("gT", [32, SEQ])
        golay = lane_sb("golay", [SEQ, DATA * CODE])
        dshift = pT

        def chained(engine, step_sem, seen):
            def link(ins):
                ins.then_inc(step_sem, 1)
                engine.wait_ge(step_sem, seen.next(step_sem))
            return link

        def batch_columns(turn, u, i):
            return bass.ds(turn * (LANES * ROUNDS * DIM) + (i * LANES + u) * DIM, DIM)

        def quarter(t, q):
            return t[:, q * QUARTER:(q + 1) * QUARTER]

        def by_head(t, n):
            return t.rearrange("p (h k) -> p h k", h=n)

        def result_bank(u):
            return bigA[u][:, 0:DIM]

        class TensorStages:

            def __init__(self, pe):
                self.pe, self.seen = pe, Seen()

            def wait(self, s):
                self.pe.wait_ge(s, self.seen.next(s))

            def context_transpose(self, u):
                self.wait(x_in[u])
                nc.tensor.transpose(bankC[u][:, 0:128], ctx[u][:, :], ident).then_inc(ctxT_psum[u], 1)

            def norm_transpose(self, u):
                self.wait(xn_ready[u])
                nc.tensor.transpose(bankB[u][:, 0:128], xn[u][:, :], ident).then_inc(xnT_psum[u], 1)

            def normed(self, u):
                self.wait(xnT_ready[u])

            def project_rope(self, u):
                self.normed(u)
                nc.tensor.matmul(bigA[u][:, 0:512], xnT[u][:, :], field("L0_attn_WqksT"), start=True, stop=True)
                nc.tensor.matmul(bigA[u][:, 512:640], xnT[u][:, :], field("L0_attn_WvT"),
                                 start=True, stop=True).then_inc(proj_psum[u], 1)

            def rows_transpose(self, u):
                self.wait(qk_ready[u])
                nc.tensor.transpose(bankB[u][:, 0:128], tok[u][:, 0:128], ident)
                nc.tensor.transpose(bankC[u][:, 0:128], tok[u][:, 128:256], ident).then_inc(qkT_psum[u], 1)

            def project_q(self, u, name):
                nc.tensor.matmul(bankB[u][:, 0:128], field(name + "_WqT"), xnT[u][:, :], start=True, stop=True)\
                    .then_inc(q_psum[u], 1)

            def project_kv(self, u, name, source):
                nc.tensor.matmul(bankC[u][:, 0:128], field(name + "_WkT"), source[u][:, :], start=True, stop=True)\
                    .then_inc(k_psum[u], 1)
                nc.tensor.matmul(bigA[u][:, 512:640], source[u][:, :], field(name + "_WvT"),
                                 start=True, stop=True).then_inc(v_psum[u], 1)

            def position_scores(self, u, c):
                if c == 0:
                    self.wait(left_ready[u])
                    self.wait(v_ready[u])
                elif c == 1:
                    self.wait(expanded_first[u])
                else:
                    self.wait(bd_ready[u])
                low, high = (bankB[u], bankC[u]) if c % 2 else (bigA[u][:, 0:512], bigA[u][:, 512:1024])
                nc.tensor.matmul(low[:, 0:512], qvT[u][:, :], quarter(rel_low, c), start=True, stop=True)
                nc.tensor.matmul(high[:, 0:512], qvT[u][:, :], quarter(rel_high, c), start=True, stop=True)\
                    .then_inc(bd_psum[u], 1)

            def scores(self, u, q, mask=None, kind=""):
                if kind == "relative":
                    if q < 2:
                        self.wait(bd_ready[u])
                    if q >= 1:
                        self.wait(expanded[u])
                else:
                    if q == 0:
                        self.wait(left_ready[u])
                    if q == 1 and kind != "geodesic":
                        self.wait(v_ready[u])
                    self.wait(expanded_first[u] if q == 0 else expanded[u])
                if q == 0:
                    self.seen.next(right_ready[u])
                if q >= 2 and kind == "geodesic":
                    self.wait(scores_taken[u])
                dst = bigA[u][:, (q % 2) * 512:(q % 2) * 512 + 512]
                last = nc.tensor.matmul(dst, left[u][:, :], quarter(kX[u], q), start=True, stop=mask is None)
                if mask is not None:
                    last = nc.tensor.matmul(dst, ident_bf[:, :], mask[:, :, :].rearrange("p h k -> p (h k)"),
                                            start=False, stop=True)
                last.then_inc(scores_psum[u], 1)

            def transpose_probs(self, u, q):
                self.wait(probs_ready[u])
                if q >= 2:
                    self.wait(pT_ready[u])
                bank = bankC[u] if q % 2 else bankB[u]
                for h in range(4):
                    last = nc.tensor.transpose(bank[:, h * 128:h * 128 + 128],
                                               sx[u][:, q * QUARTER + h * SEQ:q * QUARTER + h * SEQ + SEQ], ident)
                last.then_inc(pT_psum[u], 1)

            def weighted_values(self, u, t, direct=False):
                if t == 0 and direct:
                    self.wait(v_ready[u])
                    self.seen.next(scores_taken[u], 2)
                if t >= 2 and not direct:
                    self.wait(pT_ready[u])
                for g in range(4):
                    h = 4 * t + g
                    src = sx[u] if direct else pT[u]
                    last = nc.tensor.matmul(bigA[u][32 * g:32 * g + 32, t * 128:t * 128 + 128], v32[u][:, h, :],
                                            src[:, h * SEQ:h * SEQ + SEQ], start=True, stop=True)
                if t == 3:
                    last.then_inc(oT_psum[u], 1)

            def values_transpose(self, u):
                self.wait(oT_ready[u])
                for t in range(4):
                    last = nc.tensor.transpose(bigA[u][:, 512 + t * 128:640 + t * 128],
                                               oT[u][:, t * 128:t * 128 + 128], ident)
                last.then_inc(o_psum[u], 1)

            def attention(self, u, mask=None, kind=""):
                yield self.scores(u, 0, mask, kind)
                yield self.scores(u, 1, mask, kind)
                yield self.transpose_probs(u, 0)
                yield self.scores(u, 2, mask, kind)
                yield self.transpose_probs(u, 1)
                yield self.scores(u, 3, mask, kind)
                yield self.transpose_probs(u, 2)
                yield self.weighted_values(u, 0)
                yield self.transpose_probs(u, 3)
                yield self.weighted_values(u, 1)
                yield self.weighted_values(u, 2)
                yield self.weighted_values(u, 3)
                yield self.values_transpose(u)
                self.wait(att_ready[u])

            def output_transpose(self, u):
                nc.tensor.transpose(bankB[u][:, 0:128], att[u][:, :], ident).then_inc(attT_psum[u], 1)

            def output_product(self, u, weight):
                self.wait(attT_ready[u])
                nc.tensor.matmul(result_bank(u), attT[u][:, :], field(weight),
                                 start=True, stop=True).then_inc(y_psum[u], 1)

            def decay(self, u):
                self.wait(small_ready[u])
                nc.tensor.matmul(result_bank(u), field("decay"), tok[u][:, 0:128],
                                 start=True, stop=True).then_inc(y_psum[u], 1)

            def butterfly_hidden(self, u):
                self.normed(u)
                for c in range(4):
                    last = nc.tensor.matmul(bigA[u][:, 512 + c * 128:640 + c * 128], w_up[:, c * 128:c * 128 + 128],
                                            xnT[u][:, :], start=True, stop=True)
                last.then_inc(h_psum[u], 1)

            def butterfly_out(self, u):
                self.wait(h_ready[u])
                for c in range(4):
                    last = nc.tensor.matmul(result_bank(u), kX[u][:, c * 128:c * 128 + 128],
                                            w_down[:, c * 128:c * 128 + 128], start=(c == 0), stop=(c == 3))
                last.then_inc(y_psum[u], 1)

            def filtered(self, u):
                self.normed(u)
                nc.tensor.matmul(bankB[u][:, 0:128], circ[:, :], xnT[u][:, :], start=True, stop=True)\
                    .then_inc(attT_psum[u], 1)
                nc.tensor.matmul(result_bank(u), xnT[u][:, :], circ[:, :], start=True, stop=False)

            def latents(self, u):
                self.wait(attT_ready[u])
                nc.tensor.matmul(bankB[u][:, 128:128 + CODE], attT[u][:, :], field("L1_attn_W_el"),
                                 start=True, stop=True).then_inc(gate_psum[u], 1)

            def code_transpose(self, u):
                self.wait(small_ready[u])
                nc.tensor.transpose(bankB[u][0:CODE, 0:128], gate[u][:, 0:CODE], ident).then_inc(smallT_psum[u], 1)

            def code_product(self, u):
                self.wait(smallT_ready[u])
                nc.tensor.matmul(result_bank(u), gT[u][0:CODE, :], field("L1_attn_W_le"),
                                 start=False, stop=True).then_inc(y_psum[u], 1)

            def router(self, u, weight, bank):
                nc.tensor.matmul(bank[u][:, 0:EXPERTS], xnT[u][:, :], field(weight),
                                 start=True, stop=True).then_inc(gate_psum[u], 1)

            def gate_transpose(self, u):
                self.wait(small_ready[u])
                nc.tensor.transpose(bankB[u][0:EXPERTS, 0:128], gate[u][:, 0:EXPERTS], ident)\
                    .then_inc(smallT_psum[u], 1)

            def gate_bias(self, u, bias):
                self.wait(smallT_ready[u])
                nc.tensor.matmul(bankB[u][:, 128:256], gT[u][0:EXPERTS, :], field(bias),
                                 start=True, stop=True).then_inc(y_psum[u], 1)

            def linear_experts(self, u, weight, b):
                nc.tensor.matmul(bigA[u][:, b * 512:b * 512 + 512], xnT[u][:, :], quarter(field(weight), b),
                                 start=True, stop=True).then_inc(h_psum[u], 1)

            def mlp_hidden(self, u, e):
                for c in range(4):
                    a = (e * 4 + c) * 128
                    last = nc.tensor.matmul(bigA[u][:, (e % 2) * 512 + c * 128:(e % 2) * 512 + c * 128 + 128],
                                            field("L3_ffn_W1")[:, a:a + 128], xnT[u][:, :], start=True, stop=True)
                last.then_inc(h_psum[u], 1)

            def mlp_out(self, u, e):
                self.wait(h_odd_ready[u] if e % 2 else h_ready[u])
                if e == 1:
                    self.wait(y_taken[u])
                    self.wait(y_taken[u])
                elif e >= 3:
                    self.wait(y_taken[u])
                bank = bankB[u] if e % 2 else bankC[u]
                for c in range(4):
                    a = (e * 4 + c) * 128
                    last = nc.tensor.matmul(bank[:, 128:256], kX[u][:, (e % 2) * 512 + c * 128:][:, 0:128],
                                            field("L3_ffn_W2")[:, a:a + 128], start=(c == 0), stop=(c == 3))
                last.then_inc(y_psum[u], 1)

            def single_scores(self, u):
                self.wait(left_ready[u])
                self.wait(right_ready[u])
                nc.tensor.matmul(result_bank(u), left[u][:, :], right[u][:, :], start=True, stop=True)\
                    .then_inc(scores_psum[u], 1)

            def single_transpose(self, u):
                self.seen.next(scores_taken[u])
                self.wait(probs_ready[u])
                nc.tensor.transpose(bankB[u][:, 0:128], sx[u][:, 0:128], ident).then_inc(attT_psum[u], 1)

            def single_values(self, u):
                self.wait(attT_ready[u])
                self.wait(v_ready[u])
                nc.tensor.matmul(bankC[u][:, 0:128], attT[u][:, :], tok[u][:, 0:128], start=True, stop=True)\
                    .then_inc(y_psum[u], 1)

            def project_rows(self, u):
                self.normed(u)
                nc.tensor.matmul(bigA[u][:, 0:384], xnT[u][:, :], field("L3_attn_w_qkvT"), start=True, stop=True)\
                    .then_inc(proj_psum[u], 1)

            def rope_attention(self, u):
                yield self.norm_transpose(u)
                yield self.project_rope(u)
                yield self.rows_transpose(u)
                yield from self.attention(u, causal_bf)
                yield self.output_transpose(u)
                yield self.output_product(u, "L0_attn_WoT")

            def retention(self, u):
                yield self.decay(u)
                self.seen.next(xn_ready[u])

            def butterfly_mlp(self, u):
                yield self.norm_transpose(u)
                yield self.butterfly_hidden(u)
                yield self.butterfly_out(u)

            def filter_and_code(self, u):
                yield self.context_transpose(u)
                yield self.norm_transpose(u)
                yield self.filtered(u)
                yield self.latents(u)
                yield self.code_transpose(u)
                yield self.code_product(u)

            def masked_attention(self, u):
                self.wait(ctxT_ready[u])
                yield self.project_kv(u, "L1_xattn", ctxT)
                yield self.norm_transpose(u)
                self.normed(u)
                yield self.project_q(u, "L1_xattn")
                yield from self.attention(u, maskadd_bf)
                yield self.output_transpose(u)
                yield self.output_product(u, "L1_xattn_WoT")

            def linear_mixture(self, u):
                yield self.norm_transpose(u)
                self.normed(u)
                yield self.router(u, "L1_ffn_Wg", bankC)
                yield self.linear_experts(u, "L1_ffn_WeT", 0)
                yield self.linear_experts(u, "L1_ffn_WeT", 1)
                yield self.gate_transpose(u)
                yield self.gate_bias(u, "L1_ffn_be")
                self.seen.next(y_taken[u])

            def relative_attention(self, u):
                yield self.norm_transpose(u)
                self.normed(u)
                yield self.project_q(u, "L2_attn")
                yield self.project_kv(u, "L2_attn", xnT)
                for c in range(4):
                    yield self.position_scores(u, c)
                yield from self.attention(u, None, "relative")

            def relu_attention(self, u):
                yield self.project_kv(u, "L2_xattn", ctxT)
                yield self.norm_transpose(u)
                self.normed(u)
                yield self.project_q(u, "L2_xattn")
                yield from self.attention(u)

            def mixture_and_attention(self, u):
                yield self.norm_transpose(u)
                self.normed(u)
                yield self.router(u, "L2_ffn_W_gate", bigA)
                yield self.project_q(u, "L2_ffn")
                yield self.project_kv(u, "L2_ffn", xnT)
                yield from self.attention(u)
                yield self.linear_experts(u, "L2_ffn_W_experts", 0)
                yield self.linear_experts(u, "L2_ffn_W_experts", 1)
                yield self.gate_transpose(u)
                yield self.gate_bias(u, "L2_ffn_b_experts")
                self.seen.next(y_taken[u])

            def geodesic_attention(self, u):
                yield self.norm_transpose(u)
                yield self.project_rows(u)
                yield self.rows_transpose(u)
                for q in range(4):
                    yield self.scores(u, q, None, "geodesic")
                for t in range(4):
                    yield self.weighted_values(u, t, True)
                yield self.values_transpose(u)
                self.wait(att_ready[u])
                yield self.output_transpose(u)
                yield self.output_product(u, "L3_attn_w_outT")

            def single_attention(self, u):
                yield self.project_kv(u, "L3_xattn", ctxT)
                yield self.norm_transpose(u)
                self.normed(u)
                yield self.project_q(u, "L3_xattn")
                yield self.single_scores(u)
                yield self.single_transpose(u)
                yield self.single_values(u)

            def mlp_mixture(self, u):
                yield self.norm_transpose(u)
                self.normed(u)
                yield self.router(u, "L3_ffn_W_router", bankC)
                yield self.mlp_hidden(u, 0)
                yield self.mlp_hidden(u, 1)
                for e in range(EXPERTS):
                    if e == 1:
                        yield self.gate_transpose(u)
                        yield self.gate_bias(u, "L3_ffn_b2")
                    yield self.mlp_out(u, e)
                    if e + 2 < EXPERTS:
                        yield self.mlp_hidden(u, e + 2)
                self.seen.next(y_taken[u], 2)

            def start(self, u):
                yield

            def finished(self, u):
                pass

        class VectorStages:
            def __init__(self, dve):
                self.dve, self.seen = dve, Seen()

            def after(self, ins):
                ins.then_inc(dve_step, 1)
                count = self.seen.next(dve_step)
                yield
                self.dve.wait_ge(dve_step, count)

            def wait(self, s):
                self.dve.wait_ge(s, self.seen.next(s))

            def norm_stats(self, u):
                yield from self.after(nc.vector.bn_stats(stats[u][:, :], x[u][:, :]))
                nc.vector.bn_aggr(mv[u][:, :], stats[u][:, :]).then_inc(var_ready[u], 1)
                yield
                self.wait(var_ready[u])
                yield from self.after(nc.vector.tensor_scalar(rs[u][:, 0:1], mv[u][:, 1:2], EPS_LN, None, ALU.add))

            def norm_apply(self, u):
                self.wait(rstd_ready[u])
                v, r, t = (rs[u][:, i:i + 1] for i in (0, 1, 2))
                yield from self.after(nc.vector.scalar_tensor_tensor(out=t, in0=r, scalar=v, in1=r, op0=ALU.mult, op1=ALU.mult))
                nc.vector.tensor_scalar(xn[u][:, :], x[u][:, :], mv[u][:, 0:1], r, ALU.subtract, ALU.mult)
                yield from self.after(nc.vector.tensor_scalar(t, t, -0.5, 1.5, ALU.mult, ALU.add))
                nc.vector.tensor_scalar(xn[u][:, :], xn[u][:, :], t, None, ALU.mult).then_inc(xn_ready[u], 1)
                yield

            def start(self, u):
                nc.vector.memset(v32[u][:, :, HDIM + 1:VPAD], 0.0)
                nc.vector.memset(v32[u][:, :, HDIM:HDIM + 1], 1.0)
                yield
                self.wait(x_in[u])

            def rope(self, u):
                self.wait(proj_psum[u])
                nc.vector.tensor_tensor(tok[u][:, 0:256], bigA[u][:, 0:256], field("rope_cos"), ALU.mult)
                yield from self.after(nc.vector.tensor_tensor(tok[u][:, 256:512], bigA[u][:, 256:512], field("rope_sin"), ALU.mult))
                nc.vector.tensor_tensor(tok[u][:, 0:256], tok[u][:, 0:256], tok[u][:, 256:512], ALU.add)\
                    .then_inc(qk_ready[u], 1)
                yield

            def heads_of(self, t):
                return t.rearrange("p (h d) -> p h d", h=HEADS)

            def take_right(self, u, source, name, kind):
                src = source[:, 0:128]
                spread, own = over_heads(src, 4), per_head(head_mask[:, 0:4])
                first = by_head(quarter(kX[u], 0), 4)
                if kind == "bias":
                    bias = field(name + "_bk")
                    nc.vector.tensor_scalar(right[u][:, :], src, bias, None, ALU.add).then_inc(right_ready[u], 1)
                    if name == "L3_xattn":
                        return
                    last = nc.vector.scalar_tensor_tensor(out=first, in0=spread, scalar=bias, in1=own,
                                                          op0=ALU.add, op1=ALU.mult)
                elif kind == "relu":
                    nc.vector.tensor_scalar(right[u][:, :], src, 0.0, None, ALU.max).then_inc(right_ready[u], 1)
                    last = nc.vector.scalar_tensor_tensor(out=first, in0=spread, scalar=0.0, in1=own,
                                                          op0=ALU.max, op1=ALU.mult)
                else:
                    nc.vector.tensor_copy(right[u][:, :], src).then_inc(right_ready[u], 1)
                    last = nc.vector.tensor_tensor(first, spread, own, ALU.mult)
                last.then_inc(expanded_first[u], 1)

            def take_kv(self, u, kind, name=""):
                self.wait(k_psum[u])
                self.take_right(u, bankC[u], name, kind)
                self.wait(v_psum[u])
                v = bigA[u][:, 512:640]
                vh, vo = self.heads_of(v), v32[u][:, :, 0:HDIM]
                if name == "L3_xattn":
                    last = nc.vector.tensor_tensor(tok[u][:, 0:128], v, field(name + "_bv"), ALU.add)
                elif kind == "bias":
                    last = nc.vector.tensor_tensor(vo, vh, self.heads_of(field(name + "_bv")), ALU.add)
                elif kind == "relu":
                    last = nc.vector.tensor_scalar(vo, vh, 0.0, None, ALU.max)
                else:
                    last = nc.vector.tensor_copy(vo, vh)
                last.then_inc(v_ready[u], 1)

            def take_transposed(self, u, source):
                self.wait(qkT_psum[u])
                self.take_right(u, source[u], "", "")

            def position_scores(self, u, c):
                z = by_head(zrel[u][:, :], HEADS)
                if c == 0:
                    yield from self.after(nc.vector.memset(z[:, :, 0:1], 0.0))
                self.wait(bd_low[u])
                high = bankC[u][:, :] if c % 2 else bigA[u][:, 512:1024]
                nc.vector.copy_predicated(z[:, 4 * c:4 * c + 4, 1:SEQ + 1], over_heads(sel_int, 4), by_head(high, 4))\
                    .then_inc(bd_ready[u], 1)
                yield

            def scores_max(self, u, q, relative=False):
                self.wait(scores_psum[u])
                heads = slice(4 * q, 4 * q + 4)
                s = by_head(bigA[u][:, (q % 2) * 512:(q % 2) * 512 + 512], 4)
                if relative:
                    o = by_head(quarter(sx[u], q), 4)
                    self.dve.wait_ge(bd_back[u][q], self.seen.next(bd_back[u][q], 16))
                    yield from self.after(nc.vector.tensor_tensor(o, s, by_head(quarter(dshift[u], q), 4), ALU.add))
                    s = o
                nc.vector.tensor_reduce(nmax[u][:, heads], s, AX, ALU.max, negate=True).then_inc(max_ready[u], 1)
                yield

            def normalise(self, u):
                self.wait(o_psum[u])
                o = bigA[u][:, 512:1024].rearrange("p (h d) -> p h d", h=HEADS)
                r = hs[u][:, 0:HEADS]
                yield from self.after(nc.vector.reciprocal(r[:, :, None], o[:, :, HDIM:HDIM + 1]))
                ins = nc.vector.tensor_tensor(self.heads_of(att[u][:, :]), o[:, :, 0:HDIM], per_head(r, HDIM), ALU.mult)
                ins.then_inc(att_ready[u], 1)
                yield
                self.wait(att_ready[u])

            def attention(self, u, relative=False):
                for q in range(4):
                    yield from self.scores_max(u, q, relative)

            def add_attention(self, u):
                yield from self.after(nc.vector.tensor_tensor(x[u][:, :], x[u][:, :], att[u][:, :], ALU.add))

            def add_bias(self, u, bias):
                yield from self.after(nc.vector.tensor_tensor(x[u][:, :], x[u][:, :], bias, ALU.add))

            def add_result(self, u):
                self.wait(y_psum[u])
                yield from self.after(nc.vector.tensor_tensor(x[u][:, :], x[u][:, :], result_bank(u), ALU.add))

            def add_gated_bias(self, u):
                self.wait(y_psum[u])
                nc.vector.tensor_tensor(x[u][:, :], x[u][:, :], bankB[u][:, 128:256], ALU.add).then_inc(y_taken[u], 1)
                self.wait(y_taken[u])

            def retain(self, u):
                self.wait(y_psum[u])
                yield from self.after(nc.vector.tensor_tensor(att[u][:, :], xn[u][:, :], result_bank(u), ALU.mult))
                yield from self.after(nc.vector.tensor_tensor(x[u][:, :], x[u][:, :], att[u][:, :], ALU.add))

            def square_context(self, u):
                nc.vector.tensor_tensor(tok[u][:, 0:128], ctx[u][:, :], ctx[u][:, :], ALU.mult)\
                    .then_inc(small_ready[u], 1)

            def code_bits(self, u):
                self.wait(gate_psum[u])
                bits, data = gate[u][:, 0:CODE], gate[u][:, 0:DATA]
                syn, flip, weight = gate[u][:, 24:36], gate[u][:, 36:48], gate[u][:, 48:49]
                fix = gate[u][:, 49:50]
                lat = gate[u][:, 0:CODE]
                yield from self.after(nc.vector.tensor_tensor(lat, bankB[u][:, 128:128 + CODE], field("L1_attn_b_el"), ALU.add))
                yield from self.after(nc.vector.tensor_scalar(bits, lat, 0.0, None, ALU.is_gt))
                g = golay[u][:, :].rearrange("p (r c) -> p r c", r=DATA)
                parity = field("golay").rearrange("p (r c) -> p r c", r=DATA)
                yield from self.after(nc.vector.tensor_tensor(g, bits[:, None, :].to_broadcast([SEQ, DATA, CODE]), parity, ALU.mult))
                yield from self.after(nc.vector.tensor_reduce(syn, g, AX, ALU.add))
                yield from self.after(nc.vector.tensor_scalar(syn, syn, 0.5, None, ALU.is_gt))
                nc.vector.tensor_reduce(weight, syn, AX, ALU.add)
                yield from self.after(nc.vector.tensor_scalar(flip, data, -2.0, 1.0, ALU.mult, ALU.add))
                yield from self.after(nc.vector.tensor_tensor(flip, flip, syn, ALU.mult))
                yield from self.after(nc.vector.tensor_scalar(fix, weight, 3.0, None, ALU.is_le))
                nc.vector.scalar_tensor_tensor(out=data, in0=flip, scalar=fix, in1=data, op0=ALU.mult, op1=ALU.add)\
                    .then_inc(small_ready[u], 1)
                yield
                self.wait(small_ready[u])

            def gates_start(self, u, bias, bank):
                self.wait(gate_psum[u])
                logits, top = gate[u][:, 8:16], gate[u][:, 16:24]
                yield from self.after(nc.vector.tensor_tensor(logits, bank[u][:, 0:EXPERTS], field(bias), ALU.add))
                yield from self.after(nc.vector.max(top, logits))
                nc.vector.max_index(gidx[u][:, :], top, logits)
                nc.vector.tensor_scalar(gate[u][:, 24:25], top[:, 0:1], -1.0, None, ALU.mult).then_inc(gate_max[u], 1)
                yield

            def gates_finish(self, u, over_chosen):
                self.wait(gate_max[u])
                ix, one, two = gate[u][:, 26:28], gate[u][:, 32:40], gate[u][:, 40:48]
                e = gate[u][:, 48:56]
                total, inv = gate[u][:, 28:29], gate[u][:, 29:30]
                yield from self.after(nc.vector.tensor_copy(ix, gidx[u][:, 0:2]))
                nc.vector.tensor_scalar(one, field("iota8"), ix[:, 0:1], None, ALU.is_equal)
                yield from self.after(nc.vector.tensor_scalar(two, field("iota8"), ix[:, 1:2], None, ALU.is_equal))
                yield from self.after(nc.vector.tensor_tensor(one, one, two, ALU.add))
                self.wait(gate_exp[u])
                yield from self.after(nc.vector.tensor_tensor(two, one, e, ALU.mult))
                yield from self.after(nc.vector.tensor_reduce(total, two if over_chosen else e, AX, ALU.add))
                yield from self.after(nc.vector.reciprocal(inv, total))
                nc.vector.tensor_scalar(gate[u][:, 0:EXPERTS], two, inv, None, ALU.mult).then_inc(small_ready[u], 1)
                yield
                self.wait(small_ready[u])

            def add_linear_experts(self, u, b):
                self.wait(h_psum[u])
                for e in range(4 * b, 4 * b + 4):
                    yield from self.after(nc.vector.scalar_tensor_tensor(
                        out=x[u][:, :], in0=bigA[u][:, e * 128:e * 128 + 128], scalar=gate[u][:, e:e + 1],
                        in1=x[u][:, :], op0=ALU.mult, op1=ALU.add))

            def mlp_hidden(self, u, e):
                self.wait(h_psum[u])
                for c in range(4):
                    i = e * 4 + c
                    last = nc.vector.tensor_scalar(kX[u][:, 512 + c * 128:640 + c * 128],
                                                   bigA[u][:, 512 + c * 128:640 + c * 128],
                                                   field("L3_ffn_b1")[:, i:i + 1], 0.0, ALU.add, ALU.max)
                last.then_inc(h_odd_ready[u], 1)

            def mlp_out(self, u, e):
                self.wait(y_psum[u])
                bank = bankB[u] if e % 2 else bankC[u]
                nc.vector.scalar_tensor_tensor(
                    out=x[u][:, :], in0=bank[:, 128:256], scalar=gate[u][:, e:e + 1],
                    in1=x[u][:, :], op0=ALU.mult, op1=ALU.add).then_inc(y_taken[u], 1)
                self.wait(y_taken[u])

            def unit_rows(self, u):
                self.wait(proj_psum[u])
                b = field("L3_attn_b_qkv")
                yield from self.after(nc.vector.tensor_tensor(tok[u][:, 0:256], bigA[u][:, 0:256], b[:, 0:256], ALU.add))
                yield from self.after(nc.vector.tensor_tensor(tok[u][:, 256:512], tok[u][:, 0:256], tok[u][:, 0:256], ALU.mult))
                n2 = hs[u][:, 0:2 * HEADS]
                yield from self.after(nc.vector.tensor_reduce(n2, tok[u][:, 256:512].rearrange("p (h d) -> p h d", d=HDIM), AX, ALU.add))
                nc.vector.tensor_scalar(n2, n2, 1e-24, None, ALU.max).then_inc(var_ready[u], 1)
                yield
                self.wait(var_ready[u])
                nc.vector.tensor_tensor(v32[u][:, :, 0:HDIM], self.heads_of(bigA[u][:, 256:384]),
                                        self.heads_of(b[:, 256:384]), ALU.add)
                yield

            def unit_apply(self, u):
                self.wait(rstd_ready[u])
                n2, r = hs[u][:, 0:2 * HEADS], hs[u][:, 2 * HEADS:4 * HEADS]
                t = golay[u][:, 0:2 * HEADS]
                yield from self.after(nc.vector.tensor_scalar(r, r, LN_SHIFT ** 0.5, None, ALU.mult))
                yield from self.after(nc.vector.tensor_tensor(t, n2, r, ALU.mult))
                yield from self.after(nc.vector.tensor_tensor(t, t, r, ALU.mult))
                yield from self.after(nc.vector.tensor_scalar(t, t, -0.5, 1.5, ALU.mult, ALU.add))
                yield from self.after(nc.vector.tensor_tensor(r, r, t, ALU.mult))
                w = tok[u][:, 0:256].rearrange("p (h d) -> p h d", d=HDIM)
                nc.vector.tensor_tensor(w, w, per_head(r, HDIM), ALU.mult).then_inc(qk_ready[u], 1)
                yield

            def clip_cosines(self, u, q):
                self.wait(scores_psum[u])
                nc.vector.tensor_scalar(quarter(sx[u], q), bigA[u][:, (q % 2) * 512:(q % 2) * 512 + 512], -CLIP, CLIP,
                                        ALU.max, ALU.min).then_inc(scores_taken[u], 1)

            def log_difference(self, u):
                self.dve.wait_ge(logs_ready[u], self.seen.next(logs_ready[u], 2))
                nc.vector.tensor_tensor(pT[u][:, HALF:], pT[u][:, HALF:], sx[u][:, HALF:], ALU.subtract)\
                    .then_inc(logs_diff_high[u], 1)

            def column_sums(self, u, half):
                self.wait(kernel_ready[u])
                heads = slice(8 * half, 8 * half + 8)
                nc_sum, inv = hs[u][:, 0:HEADS][:, heads], hs[u][:, HEADS:2 * HEADS][:, heads]
                v = v32[u][:, heads, :]
                yield from self.after(nc.vector.tensor_reduce(nc_sum, by_head(sx[u][:, half * HALF:half * HALF + HALF], 8), AX, ALU.add))
                yield from self.after(nc.vector.reciprocal(inv, nc_sum))
                nc.vector.memset(v[:, :, HDIM + 1:HDIM + 2], 1.0)
                nc.vector.tensor_copy(v[:, :, HDIM:HDIM + 1], inv[:, :, None])
                last = nc.vector.tensor_tensor(v[:, :, 0:HDIM], v[:, :, 0:HDIM], per_head(inv, HDIM), ALU.mult)
                if half == 1:
                    last.then_inc(v_ready[u], 1)
                yield

            def manifold_normalise(self, u):
                self.wait(o_psum[u])
                o = bigA[u][:, 512:1024].rearrange("p (h d) -> p h d", h=HEADS)
                inv, t = hs[u][:, 0:HEADS], hs[u][:, HEADS:2 * HEADS]
                yield from self.after(nc.vector.reciprocal(inv[:, :, None], o[:, :, HDIM + 1:HDIM + 2]))
                yield from self.after(nc.vector.tensor_tensor(t[:, :, None], inv[:, :, None], o[:, :, HDIM:HDIM + 1], ALU.mult))
                yield from self.after(nc.vector.tensor_scalar(t, t, 1e-12, None, ALU.max))
                yield from self.after(nc.vector.reciprocal(t, t))
                yield from self.after(nc.vector.tensor_tensor(t, t, inv, ALU.mult))
                nc.vector.tensor_tensor(self.heads_of(att[u][:, :]), o[:, :, 0:HDIM], per_head(t, HDIM), ALU.mult)\
                    .then_inc(att_ready[u], 1)
                self.seen.next(att_ready[u])
                yield

            def single_max(self, u):
                self.wait(scores_psum[u])
                m = nmax[u][:, 0:1]
                yield from self.after(nc.vector.tensor_reduce(m, result_bank(u), AX, ALU.max, negate=True))
                nc.vector.tensor_scalar(m, m, DIM ** -0.5, None, ALU.mult).then_inc(scores_taken[u], 1)
                yield

            def single_result(self, u):
                self.wait(y_psum[u])
                yield from self.after(nc.vector.reciprocal(hs[u][:, 1:2], hs[u][:, 0:1]))
                yield from self.after(nc.vector.scalar_tensor_tensor(out=x[u][:, :], in0=bankC[u][:, 0:128], scalar=hs[u][:, 1:2],
                                                         in1=x[u][:, :], op0=ALU.mult, op1=ALU.add))
                yield

            def finished(self, u):
                nc.vector.tensor_copy(att[u][:, :], x[u][:, :]).then_inc(x_done[u], 1)

            def rope_attention(self, u):
                yield from self.norm_stats(u)
                yield from self.norm_apply(u)
                self.seen.next(xn_ready[u])
                yield from self.rope(u)
                yield self.take_transposed(u, bankC)
                yield from self.attention(u)
                yield from self.normalise(u)
                yield from self.add_result(u)

            def retention(self, u):
                yield self.square_context(u)
                self.seen.next(small_ready[u])
                yield from self.norm_stats(u)
                yield from self.norm_apply(u)
                self.wait(xn_ready[u])
                yield from self.retain(u)

            def butterfly_mlp(self, u):
                yield from self.norm_stats(u)
                yield from self.norm_apply(u)
                self.seen.next(xn_ready[u])
                yield from self.add_bias(u, down_bias[:, :])
                yield from self.add_result(u)

            def filter_and_code(self, u):
                yield from self.norm_stats(u)
                yield from self.norm_apply(u)
                yield from self.add_bias(u, field("L1_attn_b_le"))
                yield from self.code_bits(u)
                yield from self.add_result(u)

            def masked_attention(self, u):
                yield from self.norm_stats(u)
                yield self.take_kv(u, "bias", "L1_xattn")
                yield from self.norm_apply(u)
                yield from self.add_bias(u, field("L1_xattn_bo"))
                yield from self.attention(u)
                yield from self.normalise(u)
                yield from self.add_result(u)

            def linear_mixture(self, u):
                yield from self.norm_stats(u)
                yield from self.norm_apply(u)
                yield from self.gates_start(u, "L1_ffn_bg", bankC)
                yield from self.gates_finish(u, True)
                yield from self.add_linear_experts(u, 0)
                yield from self.add_linear_experts(u, 1)
                yield self.add_gated_bias(u)

            def relative_attention(self, u):
                yield from self.norm_stats(u)
                yield from self.norm_apply(u)
                yield self.take_kv(u, "")
                for c in range(4):
                    yield from self.position_scores(u, c)
                yield from self.attention(u, True)
                yield from self.normalise(u)
                yield from self.add_attention(u)

            def relu_attention(self, u):
                yield from self.norm_stats(u)
                yield self.take_kv(u, "relu")
                yield from self.norm_apply(u)
                yield from self.attention(u)
                yield from self.normalise(u)
                yield from self.add_attention(u)

            def mixture_and_attention(self, u):
                yield from self.norm_stats(u)
                yield from self.norm_apply(u)
                yield from self.gates_start(u, "L2_ffn_b_gate", bigA)
                yield self.take_kv(u, "bias", "L2_ffn")
                yield from self.gates_finish(u, False)
                yield from self.attention(u)
                yield from self.normalise(u)
                yield from self.add_attention(u)
                yield from self.add_linear_experts(u, 0)
                yield from self.add_linear_experts(u, 1)
                yield self.add_gated_bias(u)

            def geodesic_attention(self, u):
                yield from self.norm_stats(u)
                yield from self.norm_apply(u)
                yield from self.unit_rows(u)
                yield from self.unit_apply(u)
                yield self.take_transposed(u, bankB)
                for q in range(4):
                    yield self.clip_cosines(u, q)
                yield from self.add_bias(u, field("L3_attn_b_out"))
                yield self.log_difference(u)
                yield from self.column_sums(u, 0)
                yield from self.column_sums(u, 1)
                yield from self.manifold_normalise(u)
                yield from self.add_result(u)

            def single_attention(self, u):
                yield from self.norm_stats(u)
                yield self.take_kv(u, "bias", "L3_xattn")
                yield from self.norm_apply(u)
                yield from self.single_max(u)
                yield from self.single_result(u)

            def mlp_mixture(self, u):
                yield from self.norm_stats(u)
                yield from self.norm_apply(u)
                yield from self.gates_start(u, "L3_ffn_b_router", bankC)
                for e in range(EXPERTS):
                    if e % 2 == 0:
                        self.seen.next(h_psum[u])
                        yield self.mlp_hidden(u, e + 1)
                    if e == 0:
                        yield from self.gates_finish(u, True)
                    yield self.mlp_out(u, e)
                    if e == 0:
                        yield self.add_gated_bias(u)

        class ScalarStages:
            def __init__(self, act):
                self.act, self.seen = act, Seen()
                self.link = chained(act, act_step, self.seen)

            def wait(self, s):
                self.act.wait_ge(s, self.seen.next(s))

            def rstd(self, u):
                self.wait(var_ready[u])
                self.link(nc.scalar.activation(rs[u][:, 3:4], mv[u][:, 1:2], ACT.Ln, bias=field("eps_ln")))
                nc.scalar.activation(rs[u][:, 1:2], rs[u][:, 3:4], ACT.Exp, scale=-0.5).then_inc(rstd_ready[u], 1)

            def take_xnT(self, u):
                self.wait(xnT_psum[u])
                nc.scalar.copy(xnT[u][:, :], bankB[u][:, 0:128]).then_inc(xnT_ready[u], 1)

            def norm(self, u):
                yield self.rstd(u)
                yield self.take_xnT(u)

            def context(self, u):
                self.wait(ctxT_psum[u])
                nc.scalar.copy(ctxT[u][:, :], bankC[u][:, 0:128]).then_inc(ctxT_ready[u], 1)

            def rope_values(self, u):
                self.wait(proj_psum[u])
                nc.scalar.copy(v32[u][:, :, 0:HDIM], bigA[u][:, 512:640].rearrange("p (h d) -> p h d", h=HEADS))\
                    .then_inc(v_ready[u], 1)

            def take_transposed(self, u, source, scale):
                self.wait(qkT_psum[u])
                nc.scalar.activation(left[u][:, :], source[u][:, 0:128], ACT.Copy, scale=scale)\
                    .then_inc(left_ready[u], 1)

            def take_q(self, u, name):
                self.wait(q_psum[u])
                q = bankB[u][:, 0:128]
                if name == "L2_xattn":
                    last = nc.scalar.activation(left[u][:, :], q, ACT.Relu, scale=HSCALE)
                elif name == "L3_xattn":
                    last = nc.scalar.activation(left[u][:, :], q, ACT.Identity, bias=field("L3_xattn_bq"))
                else:
                    if name == "L2_attn":
                        nc.scalar.activation(qvT[u][:, :], q, ACT.Identity, scale=HSCALE, bias=q_bias("L2_attn_v_bias"))
                        name = "L2_attn_u_bias"
                    else:
                        name += "_bq"
                    last = nc.scalar.activation(left[u][:, :], q, ACT.Identity, scale=HSCALE, bias=q_bias(name))
                last.then_inc(left_ready[u], 1)

            def position_scores(self, u, c):
                self.wait(bd_psum[u])
                low = bankB[u][:, :] if c % 2 else bigA[u][:, 0:512]
                nc.scalar.copy(by_head(zrel[u][:, :], HEADS)[:, 4 * c:4 * c + 4, 1:SEQ + 1], by_head(low, 4))\
                    .then_inc(bd_low[u], 1)

            def exponentials(self, u, q, relative=False):
                self.wait(max_ready[u])
                src = quarter(sx[u], q) if relative else bigA[u][:, (q % 2) * 512:(q % 2) * 512 + 512]
                for h in range(4):
                    last = nc.scalar.activation(quarter(sx[u], q)[:, h * SEQ:h * SEQ + SEQ], src[:, h * SEQ:h * SEQ + SEQ],
                                                ACT.Exp, bias=nmax[u][:, 4 * q + h:4 * q + h + 1])
                last.then_inc(probs_ready[u], 1)

            def take_probs(self, u, q):
                self.wait(pT_psum[u])
                bank = bankC[u] if q % 2 else bankB[u]
                nc.scalar.copy(quarter(pT[u], q), bank[:, :]).then_inc(pT_ready[u], 1)

            def take_values(self, u):
                self.wait(oT_psum[u])
                nc.scalar.copy(oT[u][:, :], bigA[u][:, 0:512]).then_inc(oT_ready[u], 1)

            def attention(self, u, relative=False):
                yield self.exponentials(u, 0, relative)
                yield self.exponentials(u, 1, relative)
                yield self.take_probs(u, 0)
                yield self.exponentials(u, 2, relative)
                yield self.take_probs(u, 1)
                yield self.exponentials(u, 3, relative)
                yield self.take_probs(u, 2)
                yield self.take_probs(u, 3)
                yield self.take_values(u)

            def take_attT(self, u):
                self.wait(attT_psum[u])
                nc.scalar.copy(attT[u][:, :], bankB[u][:, 0:128]).then_inc(attT_ready[u], 1)

            def gelu(self, u):
                self.wait(h_psum[u])
                for c in range(4):
                    last = nc.scalar.activation(kX[u][:, c * 128:c * 128 + 128], bigA[u][:, 512 + c * 128:640 + c * 128],
                                                ACT.Gelu, bias=up_bias[:, c:c + 1])
                last.then_inc(h_ready[u], 1)
                load_tables(EXP_LN)

            def skip_linear_experts(self, u):
                self.seen.next(h_psum[u], 2)

            def take_small(self, u, n):
                self.wait(smallT_psum[u])
                nc.scalar.copy(gT[u][0:n, :], bankB[u][0:n, 0:128]).then_inc(smallT_ready[u], 1)

            def gates(self, u):
                self.wait(gate_max[u])
                nc.scalar.activation(gate[u][:, 48:56], gate[u][:, 8:16], ACT.Exp, bias=gate[u][:, 24:25])\
                    .then_inc(gate_exp[u], 1)

            def mlp_hidden(self, u, e):
                self.wait(h_psum[u])
                for c in range(4):
                    i = e * 4 + c
                    last = nc.scalar.activation(kX[u][:, c * 128:c * 128 + 128], bigA[u][:, c * 128:c * 128 + 128],
                                                ACT.Relu, bias=field("L3_ffn_b1")[:, i:i + 1])
                last.then_inc(h_ready[u], 1)

            def unit_norms(self, u):
                self.wait(var_ready[u])
                n2, r = hs[u][:, 0:2 * HEADS], hs[u][:, 2 * HEADS:4 * HEADS]
                self.link(nc.scalar.activation(r, n2, ACT.Ln, scale=LN_SHIFT))
                nc.scalar.activation(r, r, ACT.Exp, scale=-0.5).then_inc(rstd_ready[u], 1)

            def cosine_logs(self, u, half):
                self.wait(scores_taken[u])
                self.wait(scores_taken[u])
                c = sx[u][:, half * HALF:half * HALF + HALF]
                self.link(nc.scalar.activation(pT[u][:, half * HALF:half * HALF + HALF], c, ACT.Ln, scale=-1.0,
                                               bias=field("ones")))
                nc.scalar.activation(c, c, ACT.Ln, scale=1.0, bias=field("ones")).then_inc(logs_ready[u], 1)

            def angles(self, u):
                load_tables(TANH_ARCTAN)
                for half, ready in ((0, logs_diff), (1, logs_diff_high)):
                    self.wait(ready[u])
                    a = sx[u][:, half * HALF:half * HALF + HALF]
                    self.link(nc.scalar.activation(a, pT[u][:, half * HALF:half * HALF + HALF], ACT.Tanh, scale=0.25))
                    self.link(nc.scalar.activation(a, a, ACT.Arctan))
                load_tables(EXP_LN)

            def kernel_values(self, u, half):
                a = sx[u][:, half * HALF:half * HALF + HALF]
                self.link(nc.scalar.activation(a, a, ACT.Ln, scale=2.0, bias=field("one_half_pi")))
                nc.scalar.activation(a, a, ACT.Exp, scale=-3.2).then_inc(kernel_ready[u], 1)

            def single_exp(self, u):
                self.wait(scores_taken[u])
                nc.scalar.activation(sx[u][:, 0:128], result_bank(u), ACT.Exp, scale=DIM ** -0.5,
                                     bias=nmax[u][:, 0:1], accum_out=hs[u][:, 0:1]).then_inc(probs_ready[u], 1)

            def rope_attention(self, u):
                yield from self.norm(u)
                yield self.rope_values(u)
                yield self.take_transposed(u, bankB, HSCALE)
                yield from self.attention(u)
                yield self.take_attT(u)

            def retention(self, u):
                yield self.rstd(u)

            def butterfly_mlp(self, u):
                yield from self.norm(u)
                yield self.gelu(u)

            def filter_and_code(self, u):
                yield self.context(u)
                yield from self.norm(u)
                yield self.take_attT(u)
                yield self.take_small(u, CODE)

            def masked_attention(self, u):
                yield from self.norm(u)
                yield self.take_q(u, "L1_xattn")
                yield from self.attention(u)
                yield self.take_attT(u)

            def linear_mixture(self, u):
                yield from self.norm(u)
                yield self.gates(u)
                self.skip_linear_experts(u)
                yield self.take_small(u, EXPERTS)

            def relative_attention(self, u):
                yield from self.norm(u)
                yield self.take_q(u, "L2_attn")
                for c in range(4):
                    yield self.position_scores(u, c)
                yield from self.attention(u, True)

            def relu_attention(self, u):
                yield from self.norm(u)
                yield self.take_q(u, "L2_xattn")
                yield from self.attention(u)

            def mixture_and_attention(self, u):
                yield from self.norm(u)
                yield self.gates(u)
                yield self.take_q(u, "L2_ffn")
                yield from self.attention(u)
                self.skip_linear_experts(u)
                yield self.take_small(u, EXPERTS)

            def geodesic_attention(self, u):
                yield from self.norm(u)
                yield self.unit_norms(u)
                yield self.take_transposed(u, bankC, 1.0)
                yield self.cosine_logs(u, 0)
                yield self.cosine_logs(u, 1)
                yield self.angles(u)
                yield self.kernel_values(u, 0)
                yield self.kernel_values(u, 1)
                yield self.take_values(u)
                yield self.take_attT(u)

            def single_attention(self, u):
                yield from self.norm(u)
                yield self.take_q(u, "L3_xattn")
                yield self.single_exp(u)
                yield self.take_attT(u)

            def mlp_mixture(self, u):
                yield from self.norm(u)
                yield self.gates(u)
                yield self.mlp_hidden(u, 0)
                for e in range(2, EXPERTS, 2):
                    self.seen.next(h_psum[u])
                    yield self.mlp_hidden(u, e)
                    if e == 2:
                        yield self.take_small(u, EXPERTS)
                self.seen.next(h_psum[u])

            def start(self, u):
                yield

            def finished(self, u):
                pass

        def load_tables(name):
            nc.scalar.preload_act_table_set(name)

        class PoolStages:
            def __init__(self, pool):
                self.pool, self.seen = pool, Seen()

            def wait(self, s):
                self.pool.wait_ge(s, self.seen.next(s))

            def load(self, turn, u, i):
                at = batch_columns(turn, u, i)
                nc.gpsimd.tensor_copy(ctx[u][:, :], ctx_all[:, at])
                nc.gpsimd.tensor_copy(x[u][:, :], x_all[:, at]).then_inc(x_in[u], 1)

            def expand(self, u, q):
                if q == 1:
                    self.wait(right_ready[u])
                nc.gpsimd.tensor_tensor(by_head(quarter(kX[u], q), 4), over_heads(right[u], 4),
                                        per_head(head_mask[:, 4 * q:4 * q + 4]), ALU.mult).then_inc(expanded[u], 1)

            def attention(self, u):
                for q in range(1, 4):
                    yield self.expand(u, q)

            def log_difference(self, u):
                self.wait(logs_ready[u])
                nc.gpsimd.tensor_tensor(pT[u][:, 0:HALF], pT[u][:, 0:HALF], sx[u][:, 0:HALF], ALU.subtract)\
                    .then_inc(logs_diff[u], 1)
                self.seen.next(logs_ready[u])
                self.seen.next(right_ready[u])

            def store(self, turn, u, i):
                self.wait(x_done[u])
                nc.gpsimd.tensor_copy(x_all[:, batch_columns(turn, u, i)], att[u][:, :]).then_inc(x_kept[u], 1)

        def first_layer(s, u):
            for _ in range(ROUNDS):
                yield from s.start(u)
                yield from s.rope_attention(u)
                yield from s.retention(u)
                yield from s.butterfly_mlp(u)
                yield s.finished(u)

        def other_layers(s, u):
            for _ in range(ROUNDS):
                yield from layers_1_to_3(s, u)

        def layers_1_to_3(s, u):
            yield from s.start(u)
            yield from s.filter_and_code(u)
            yield from s.masked_attention(u)
            yield from s.linear_mixture(u)
            yield from s.relative_attention(u)
            yield from s.relu_attention(u)
            yield from s.mixture_and_attention(u)
            yield from s.geodesic_attention(u)
            yield from s.single_attention(u)
            yield from s.mlp_mixture(u)
            yield s.finished(u)

        with nc.Fori(0, TURNS) as turn:
            with nc.Block() as block:
                @block.gpsimd
                def _(pool):
                    p = PoolStages(pool)

                    def lane(u):
                        for i in range(ROUNDS):
                            yield p.load(turn, u, i)
                            yield from p.attention(u)
                            yield p.store(turn, u, i)

                    interleave(ORDER_FIRST["gpsimd"], [lane(u) for u in LANE_RANGE])

                @block.tensor
                def _(pe):
                    t = TensorStages(pe)
                    interleave(ORDER_FIRST["tensor"], [first_layer(t, u) for u in LANE_RANGE])

                @block.vector
                def _(dve):
                    v = VectorStages(dve)
                    interleave(ORDER_FIRST["vector"], [first_layer(v, u) for u in LANE_RANGE])

                @block.scalar
                def _(act):
                    load_tables(EXP_LN)
                    a = ScalarStages(act)
                    interleave(ORDER_FIRST["scalar"], [first_layer(a, u) for u in LANE_RANGE])
            end_of_turn()

        with ExitStack() as scope:
            all_stats = sb("all_stats", [SEQ, BATCH * 6], F32, scope)
            all_mv = sb("all_mv", [SEQ, BATCH * 2], F32, scope)
            all_r = sb("all_r", [SEQ, 4 * BATCH], F32, scope)
            xh = sx[0]
            head_row = sx[1]
            sn, above = kX[0], kX[1]
            ext = sb("ext", [SEQ, 2], F32, scope)
            sc = sb("sc", [1, 32], F32, scope)
            fr = sb("fr", [DIM, 16], F32, scope)
            scaled = sb("scaled", [DIM, DIM], F32, scope)
            block = scope.enter_context(nc.Block())
            mvv = all_mv[:, :].rearrange("p (b t) -> p b t", t=2)
            var, r0, rt, rr = (all_r[:, i * BATCH:(i + 1) * BATCH] for i in range(4))
            n_first = SCALES[-1] ** 2

            @block.sync
            def _(sp):
                sp.wait_ge(xn_ready[0], 1)
                sp.dma_start(head_row[0:1, 0:n_first], xh[0:n_first // DIM, 0:DIM]).then_inc(loaded, 16)
                sp.wait_ge(loaded, 16)

            @block.vector
            def _(dve):
                seen = Seen()
                link = chained(dve, dve_step, seen)
                for b in range(BATCH):
                    last = nc.vector.bn_stats(all_stats[:, b * 6:b * 6 + 6], x_all[:, b * DIM:b * DIM + DIM])
                link(last)
                for b in range(BATCH):
                    last = nc.vector.bn_aggr(all_mv[:, b * 2:b * 2 + 2], all_stats[:, b * 6:b * 6 + 6])
                link(last)
                nc.vector.tensor_scalar(var[:, :, None], mvv[:, :, 1:2], EPS_LN, None, ALU.add).then_inc(var_ready[0], 1)
                dve.wait_ge(rstd_ready[0], 1)
                link(nc.vector.tensor_tensor(rt, var, r0, ALU.mult))
                link(nc.vector.tensor_tensor(rt, rt, r0, ALU.mult))
                link(nc.vector.tensor_scalar(rt, rt, -0.5, 1.5, ALU.mult, ALU.add))
                link(nc.vector.tensor_tensor(rr, r0, rt, ALU.mult))
                xv, xo = (t[:, :].rearrange("p (b d) -> p b d", b=BATCH) for t in (x_all, xh))
                link(nc.vector.tensor_tensor(xo, xv, mvv[:, :, 0:1].to_broadcast([SEQ, BATCH, DIM]), ALU.subtract))
                nc.vector.tensor_tensor(xo, xo, per_head(rr, DIM), ALU.mult).then_inc(xn_ready[0], 1)
                dve.wait_ge(xn_ready[0], 1)
                nc.vector.tensor_reduce(ext[:, 0:1], xh[:, :], AX, ALU.min)
                nc.vector.tensor_reduce(ext[:, 1:2], xh[:, :], AX, ALU.max).then_inc(small_ready[0], 1)
                dve.wait_ge(smallT_psum[0], 1)
                low, span, inv = sc[0:1, 0:1], sc[0:1, 1:2], sc[0:1, 2:3]
                nc.vector.tensor_reduce(low, bankB[0][0:1, 0:128], AX, ALU.min)
                link(nc.vector.tensor_reduce(span, bankB[0][0:1, 128:256], AX, ALU.max))
                link(nc.vector.tensor_tensor(span, span, low, ALU.subtract))
                link(nc.vector.tensor_scalar(span, span, 1e-10, None, ALU.add))
                link(nc.vector.reciprocal(inv, span))
                dve.wait_ge(loaded, 16)
                link(nc.vector.tensor_scalar(sn[0:1, 0:n_first], head_row[0:1, 0:n_first], low, inv, ALU.subtract, ALU.mult))
                for i, s in enumerate(SCALES):
                    n = s * s
                    m, c = sc[0:1, 3:4], sc[0:1, 8 + i:9 + i]
                    link(nc.vector.tensor_reduce(m, sn[0:1, 0:n], AX, ALU.add))
                    link(nc.vector.tensor_scalar(m, m, 1.0 / n, None, ALU.mult))
                    link(nc.vector.tensor_scalar(above[0:1, 0:n], sn[0:1, 0:n], m, None, ALU.is_gt))
                    link(nc.vector.tensor_reduce(c, above[0:1, 0:n], AX, ALU.add))
                nc.vector.tensor_scalar(sc[0:1, 8:13], sc[0:1, 8:13], 1.0, None, ALU.max).then_inc(small_ready[1], 1)
                dve.wait_ge(smallT_ready[1], 1)
                ly, prod = sc[0:1, 13:18], sc[0:1, 18:23]
                nc.vector.tensor_reduce(sc[0:1, 23:24], ly, AX, ALU.add)
                link(nc.vector.tensor_tensor(prod, ly, field("log_scales"), ALU.mult))
                link(nc.vector.tensor_reduce(sc[0:1, 24:25], prod, AX, ALU.add))
                lx = np.log(np.asarray(SCALES, np.float32))
                n = len(SCALES)
                den = float(n * (lx * lx).sum() - lx.sum() ** 2)
                link(nc.vector.tensor_scalar(sc[0:1, 23:24], sc[0:1, 23:24], float(lx.sum()), None, ALU.mult))
                link(nc.vector.tensor_scalar(sc[0:1, 24:25], sc[0:1, 24:25], float(n), None, ALU.mult))
                link(nc.vector.tensor_tensor(sc[0:1, 24:25], sc[0:1, 23:24], sc[0:1, 24:25], ALU.subtract))
                link(nc.vector.tensor_scalar(sc[0:1, 24:25], sc[0:1, 24:25], 1.0 / den, 1.0, ALU.mult, ALU.max))
                nc.vector.tensor_scalar(sc[0:1, 25:26], sc[0:1, 24:25], 2.0, None, ALU.min).then_inc(att_ready[0], 1)
                dve.wait_ge(y_psum[0], 1)
                D, wD, a, b, t, u = (fr[:, i:i + 1] for i in range(6))
                ka, ka2 = field("freq"), field("freq_sq")
                link(nc.vector.tensor_copy(D, bankC[0][:, 0:1]))
                link(nc.vector.tensor_scalar(wD, D, 0.2, 1.0, ALU.mult, ALU.add))
                link(nc.vector.tensor_tensor(wD, wD, D, ALU.mult))
                link(nc.vector.tensor_scalar(a, D, 0.5, 1.0, ALU.mult, ALU.add))
                link(nc.vector.tensor_scalar(b, D, 0.1, None, ALU.mult))
                link(nc.vector.tensor_tensor(t, a, ka, ALU.mult))
                link(nc.vector.tensor_tensor(t, t, wD, ALU.add))
                link(nc.vector.tensor_scalar(fr[:, 6:7], t, -1.0, float(np.pi), ALU.mult, ALU.add))
                link(nc.vector.tensor_tensor(u, b, ka2, ALU.mult))
                link(nc.vector.tensor_tensor(u, u, ka, ALU.subtract))
                link(nc.vector.tensor_tensor(u, u, wD, ALU.add))
                nc.vector.tensor_scalar(fr[:, 7:8], u, -1.0, float(np.pi / 2), ALU.mult, ALU.add)\
                    .then_inc(small_ready[0], 1)
                dve.wait_ge(smallT_ready[0], 1)
                link(nc.vector.tensor_tensor(fr[:, 10:11], fr[:, 8:9], fr[:, 9:10], ALU.mult))
                nc.vector.tensor_scalar(scaled[:, :], field("dft"), fr[:, 10:11], None, ALU.mult).then_inc(qk_ready[0], 1)
                dve.wait_ge(y_psum[0], 2)
                nc.vector.tensor_copy(circ[:, :], bankC[0][:, 128:256])

            @block.scalar
            def _(act):
                link = chained(act, act_step, Seen())
                load_tables(EXP_LN)
                act.wait_ge(var_ready[0], 1)
                link(nc.scalar.activation(rt, var, ACT.Ln))
                nc.scalar.activation(r0, rt, ACT.Exp, scale=-0.5).then_inc(rstd_ready[0], 1)
                act.wait_ge(small_ready[1], 1)
                nc.scalar.activation(sc[0:1, 13:18], sc[0:1, 8:13], ACT.Ln).then_inc(smallT_ready[1], 1)
                act.wait_ge(small_ready[0], 2)
                nc.scalar.activation(fr[:, 8:9], fr[:, 6:7], ACT.Sin)
                nc.scalar.activation(fr[:, 9:10], fr[:, 7:8], ACT.Sin).then_inc(smallT_ready[0], 1)

            @block.tensor
            def _(pe):
                pe.wait_ge(small_ready[0], 1)
                nc.tensor.transpose(bankB[0][0:1, 0:128], ext[:, 0:1], ident)
                nc.tensor.transpose(bankB[0][0:1, 128:256], ext[:, 1:2], ident).then_inc(smallT_psum[0], 1)
                pe.wait_ge(att_ready[0], 1)
                nc.tensor.matmul(bankC[0][:, 0:1], field("ones_row"), sc[0:1, 25:26], start=True, stop=True)\
                    .then_inc(y_psum[0], 1)
                pe.wait_ge(qk_ready[0], 1)
                nc.tensor.matmul(bankC[0][:, 128:256], scaled[:, :], field("dft"), start=True, stop=True)\
                    .then_inc(y_psum[0], 1)
        end_of_turn()

        with nc.Fori(0, TURNS) as turn:
            with nc.Block() as block:
                @block.gpsimd
                def _(pool):
                    p = PoolStages(pool)

                    def lane(u):
                        for i in range(ROUNDS):
                            yield p.load(turn, u, i)
                            for _ in range(5):
                                yield from p.attention(u)
                            yield p.log_difference(u)
                            yield p.store(turn, u, i)

                    interleave(ORDER_OTHERS["gpsimd"], [lane(u) for u in LANE_RANGE])

                @block.sync
                def _(sp):
                    seen = Seen()

                    def write(u, c):
                        sp.wait_ge(bd_ready[u], seen.next(bd_ready[u]))
                        sp.dma_start(dram["shift"][u][4 * c:4 * c + 4].rearrange("h (i c) -> i h c", c=SEQ + 1),
                                     by_head(zrel[u][:, :], HEADS)[:, 4 * c:4 * c + 4, :]).then_inc(bd_out[u][c], 16)

                    def read(u, c):
                        sp.wait_ge(bd_out[u][c], seen.next(bd_out[u][c], 16))
                        sp.dma_start(by_head(quarter(dshift[u], c), 4),
                                     dram["shift"][u][4 * c:4 * c + 4, SEQ:SEQ + SEQ * SEQ]
                                     .rearrange("h (i c) -> i h c", c=SEQ)).then_inc(bd_back[u][c], 16)

                    def lane(u):
                        for _ in range(ROUNDS):
                            yield write(u, 0)
                            for c in range(1, 4):
                                yield write(u, c)
                                yield read(u, c - 1)
                            yield read(u, 3)

                    interleave(ORDER_OTHERS["sync"], [lane(u) for u in LANE_RANGE])
                    for i in range(ROUNDS):
                        for u in LANE_RANGE:
                            sp.wait_ge(x_kept[u], i + 1)
                            batch = turn * (LANES * ROUNDS) + (i * LANES + u)
                            sp.dma_start(out[bass.ds(batch, 1), :, :].rearrange("b s d -> (b s) d"),
                                         x_all[:, batch_columns(turn, u, i)]).then_inc(stored, 16)

                @block.tensor
                def _(pe):
                    t = TensorStages(pe)
                    interleave(ORDER_OTHERS["tensor"], [other_layers(t, u) for u in LANE_RANGE])

                @block.vector
                def _(dve):
                    v = VectorStages(dve)
                    interleave(ORDER_OTHERS["vector"], [other_layers(v, u) for u in LANE_RANGE])

                @block.scalar
                def _(act):
                    load_tables(EXP_LN)
                    a = ScalarStages(act)
                    interleave(ORDER_OTHERS["scalar"], [other_layers(a, u) for u in LANE_RANGE])
            end_of_turn()
        with nc.Block() as block:
            @block.sync
            def _(sp):
                sp.wait_ge(stored, 16 * BATCH)


def rope_tables():
    freq = 1.0 / 10000.0 ** (np.arange(0, HDIM, 2, dtype=np.float32) / HDIM)
    angle = np.outer(np.arange(SEQ, dtype=np.float32), freq.astype(np.float32))
    emb = np.concatenate([angle, angle], -1).astype(np.float32)
    sign = np.where(np.arange(HDIM) < HDIM // 2, -1.0, 1.0)
    cos, sin = np.cos(emb), np.sin(emb) * sign
    return np.tile(cos, (1, 2 * HEADS)), np.tile(sin, (1, 2 * HEADS))


def position_table():
    freq = (1.0 / 10000.0 ** (np.arange(0, DIM, 2, dtype=np.float32) / DIM)).astype(np.float32)
    pos = np.arange(-(SEQ - 1), SEQ, dtype=np.float32)
    angle = (pos[:, None] * freq[None, :]).astype(np.float32)
    emb = np.zeros((2 * SEQ - 1, DIM), np.float32)
    emb[:, 0::2], emb[:, 1::2] = np.sin(angle), np.cos(angle)
    return emb


def fourier_basis():
    n, rows, freq = np.arange(DIM), [np.full(DIM, DIM ** -0.5)], [0]
    for k in range(1, DIM // 2):
        rows += [np.cos(2 * np.pi * k * n / DIM) * (2 / DIM) ** 0.5, np.sin(2 * np.pi * k * n / DIM) * (2 / DIM) ** 0.5]
        freq += [k, k]
    rows.append((1 - 2 * (n % 2)) * DIM ** -0.5)
    freq.append(DIM // 2)
    ka = (np.asarray(freq, np.float32) / np.float32(DIM)) + np.float32(1e-8)
    return np.asarray(rows), ka.astype(np.float32)


GOLAY_A = ["111011100011", "110111000110", "101110001101", "011100011011", "000011111111", "111100000000",
           "000011110000", "110011001100", "101010101010", "010101010101", "100110011001", "011001100110"]


def constants():
    cos, sin = rope_tables()
    basis, ka = fourier_basis()
    i, j = np.arange(SEQ)[:, None], np.arange(SEQ)[None, :]
    t = np.arange(SEQ)
    a = np.array([[int(c) for c in row] for row in GOLAY_A], np.float32)
    parity = np.concatenate([a.T, np.eye(DATA)], axis=1)
    return {
        "ident": np.eye(128),
        "head_mask": (np.arange(DIM)[:, None] // HDIM == np.arange(HEADS)[None, :]),
        "ones_row": np.ones((1, 128)),
        "ones": np.ones((128, 1)),
        "eps_ln": np.full((128, 1), EPS_LN),
        "one_half_pi": np.full((128, 1), 1 + np.pi / 2),
        "rope_cos": cos, "rope_sin": sin,
        "causal": np.where(j <= i, 0.0, MASKED),
        "decay": np.where(t[None, :] >= t[:, None], 0.9 ** np.maximum(t[None, :] - t[:, None], 0), 0.0),
        "sin_rpe": position_table().T,
        "rel_select": (j >= SEQ - 1 - i),
        "dft": basis,
        "freq": ka[:, None], "freq_sq": (ka * ka)[:, None],
        "log_scales": np.log(np.asarray(SCALES, np.float32))[None, :],
        "golay": np.broadcast_to(parity.reshape(1, -1), (SEQ, DATA * CODE)),
        "iota8": np.broadcast_to(np.arange(EXPERTS)[None, :], (SEQ, EXPERTS)),
    }


def lay_out(w):
    def rows(v):
        return np.broadcast_to(np.asarray(v).reshape(1, -1), (128, np.asarray(v).size))

    def column(v):
        return np.asarray(v).reshape(-1, 1)

    qkv0 = np.asarray(w["L0_attn_W_qkv"])
    swap = np.arange(DIM).reshape(HEADS, 2, HDIM // 2)[:, ::-1].reshape(-1)
    q0, k0, v0 = qkv0[0:128], qkv0[128:256], qkv0[256:384]
    first = {
        "L0_attn_WqksT": np.concatenate([q0, k0, q0[swap], k0[swap]], 0).T,
        "L0_attn_WvT": v0.T, "L0_attn_WoT": w["L0_attn_W_out"].T,
        "L0_ffn_W_exp": w["L0_ffn_W_exp"], "L0_ffn_W_conT": w["L0_ffn_W_con"].T,
        "L0_ffn_b_exp": w["L0_ffn_b_exp"].reshape(1, -1),
        "L0_ffn_up_bias": w["L0_ffn_up_bias"].reshape(4, 128).T,
        "L0_ffn_b_con": rows(w["L0_ffn_b_con"]), "L0_ffn_down_bias": rows(w["L0_ffn_down_bias"]),
    }
    qkv2, b2 = w["L2_ffn_W_qkv"], w["L2_ffn_b_qkv"]
    later = {
        "L1_attn_W_el": w["L1_attn_W_el"], "L1_attn_b_el": rows(w["L1_attn_b_el"]),
        "L1_attn_W_le": w["L1_attn_W_le"], "L1_attn_b_le": rows(w["L1_attn_b_le"]),
        "L1_xattn_WqT": w["L1_xattn_Wq"].T, "L1_xattn_WkT": w["L1_xattn_Wk"].T, "L1_xattn_WvT": w["L1_xattn_Wv"].T,
        "L1_xattn_WoT": w["L1_xattn_Wo"].T, "L1_xattn_bq": column(w["L1_xattn_bq"]),
        "L1_xattn_bk": column(w["L1_xattn_bk"]), "L1_xattn_bv": rows(w["L1_xattn_bv"]),
        "L1_xattn_bo": rows(w["L1_xattn_bo"]),
        "L1_ffn_Wg": w["L1_ffn_Wg"], "L1_ffn_bg": rows(w["L1_ffn_bg"]), "L1_ffn_be": w["L1_ffn_be"],
        "L1_ffn_WeT": w["L1_ffn_We"].transpose(2, 0, 1).reshape(DIM, -1),
        "L2_attn_WqT": w["L2_attn_Wq"].T, "L2_attn_WkT": w["L2_attn_Wk"].T, "L2_attn_WvT": w["L2_attn_Wv"].T,
        "L2_attn_WrT": w["L2_attn_Wr"].T,
        "L2_attn_u_bias": column(w["L2_attn_u_bias"]), "L2_attn_v_bias": column(w["L2_attn_v_bias"]),
        "L2_xattn_WqT": w["L2_xattn_Wq"].T, "L2_xattn_WkT": w["L2_xattn_Wk"].T, "L2_xattn_WvT": w["L2_xattn_Wv"].T,
        "L2_ffn_WqT": qkv2[:, 0:128], "L2_ffn_WkT": qkv2[:, 128:256], "L2_ffn_WvT": qkv2[:, 256:384],
        "L2_ffn_bq": column(b2[0:128]), "L2_ffn_bk": column(b2[128:256]), "L2_ffn_bv": rows(b2[256:384]),
        "L2_ffn_W_gate": w["L2_ffn_W_gate"], "L2_ffn_b_gate": rows(w["L2_ffn_b_gate"]),
        "L2_ffn_W_experts": w["L2_ffn_W_experts"].transpose(1, 0, 2).reshape(DIM, -1),
        "L2_ffn_b_experts": w["L2_ffn_b_experts"],
        "L3_attn_w_qkvT": w["L3_attn_w_qkv"].T, "L3_attn_b_qkv": rows(w["L3_attn_b_qkv"]),
        "L3_attn_w_outT": w["L3_attn_w_out"].T, "L3_attn_b_out": rows(w["L3_attn_b_out"]),
        "L3_xattn_WqT": w["L3_xattn_Wq"], "L3_xattn_WkT": w["L3_xattn_Wk"], "L3_xattn_WvT": w["L3_xattn_Wv"],
        "L3_xattn_bq": column(w["L3_xattn_bq"]), "L3_xattn_bk": column(w["L3_xattn_bk"]),
        "L3_xattn_bv": rows(w["L3_xattn_bv"]),
        "L3_ffn_W_router": w["L3_ffn_W_router"], "L3_ffn_b_router": rows(w["L3_ffn_b_router"]),
        "L3_ffn_W1": w["L3_ffn_W1"].transpose(1, 0, 2).reshape(DIM, -1),
        "L3_ffn_b1": w["L3_ffn_b1"].reshape(EXPERTS * 4, 128).T,
        "L3_ffn_W2": w["L3_ffn_W2"].reshape(EXPERTS, 4, 128, DIM).transpose(2, 0, 1, 3).reshape(128, -1),
        "L3_ffn_b2": w["L3_ffn_b2"],
    }
    return first, later


def side_by_side(fields):
    where, at = {}, 0
    for name, a in fields.items():
        where[name] = (at, a.shape[1], a.shape[0])
        at += a.shape[1]
    packed = np.zeros((128, at), np.float32)
    for name, a in fields.items():
        c, n, r = where[name]
        packed[0:r, c:c + n] = a
    return packed, where


def butterfly_rows(up, down):
    parts = []
    for weights, backwards in ((up, False), (down, True)):
        for s in (range(STAGES0 - 1, -1, -1) if backwards else range(STAGES0)):
            w = weights[s].reshape(HIDDEN0 // (2 * 2 ** s), 2 ** s, 2, 2)
            off = (w[..., 1, 0], w[..., 0, 1]) if backwards else (w[..., 0, 1], w[..., 1, 0])
            parts += [np.stack([w[..., 0, 0], w[..., 1, 1]], 1).reshape(-1), np.stack(off, 1).reshape(-1)]
    return np.concatenate(parts).reshape(1, -1)


def kernel(**inputs):
    import concourse.bacc as bacc
    from concourse.bass_utils import run_bass_kernel_spmd

    w = {k: np.asarray(v) for k, v in inputs.items()}
    first, later = lay_out(w)
    packs = {"first": side_by_side({**constants(), **first}), "later": side_by_side(later)}
    arrays = {
        "first": packs["first"][0], "later": packs["later"][0],
        "butterfly": np.ascontiguousarray(butterfly_rows(w["L0_ffn_up_weights"], w["L0_ffn_down_weights"])),
        "mask": np.ascontiguousarray(w["mask_1xSxS2_if1"][0]),
        "x": np.ascontiguousarray(w["x"]), "ctx": np.ascontiguousarray(w["ctx_1024"]),
    }
    nc = bacc.Bacc("TRN2", target_bir_lowering=False, num_devices=1)
    dram = {n: nc.dram_tensor(f"in_{n}", a.shape, mybir.dt.from_np(a.dtype), kind="ExternalInput").ap()
            for n, a in arrays.items()}
    dram["shift"] = [nc.dram_tensor(f"shift_{u}", (HEADS, SEQ * (SEQ + 1)), F32, kind="Internal").ap()
                     for u in LANE_RANGE]
    out = nc.dram_tensor("out_0", (BATCH, SEQ, DIM), F32, kind="ExternalOutput").ap()
    decoder_program(nc, dram, {n: p[1] for n, p in packs.items()}, out)
    r = run_bass_kernel_spmd(nc, [{f"in_{n}": a for n, a in arrays.items()}], core_ids=[0])
    return r.results[0]["out_0"]
```
